# Optimizing a Trainium2 kernel written in Bass

```python
import numpy as np
import jax
import jax.numpy as jnp

def _softmax(x, axis=-1):
    return jax.nn.softmax(x, axis=axis)

def _gelu(x):
    return jax.nn.gelu(x, approximate=True)

def _silu(x):
    return jax.nn.silu(x)

def _sigmoid(x):
    return jax.nn.sigmoid(x)

def _layernorm(x, axis=-1, eps=1e-05):
    m = jnp.mean(x, axis=axis, keepdims=True)
    v = jnp.var(x, axis=axis, keepdims=True)
    return (x - m) / jnp.sqrt(v + eps)

def _scatter_add(tgt, idx, src, axis=0):
    return tgt.at[idx].add(src)

def _segment_sum(src, seg, n):
    return jax.ops.segment_sum(src, seg, n)
kernel_name = 'mk_conv_attn_hybrid_d4_conv_nchw256_r4_144818'

def setup_inputs(seed: int=0):
    np.random.seed(seed)
    _w = jnp.asarray

    def _rec_inputs():
        import jax
        import jax.numpy as jnp
        _gk = jax.random.key(seed)
        x = 7.22e-05 + 1 * jax.random.normal(jax.random.fold_in(_gk, 1), (8, 64, 16, 16), jnp.float32)
        return x
    x = _rec_inputs()

    def _L0_conv_setup():
        import jax, jax.numpy as jnp
        import numpy as np
        EPS = 1e-05

        def _conv1x1(x, W, b):
            return jnp.einsum('bchw,oc->bohw', x, W) + b[None, :, None, None]

        def _maxpool2(x):
            B, C, H, W = x.shape
            return x.reshape(B, C, H // 2, 2, W // 2, 2).max(axis=(3, 5))
        key = jax.random.key(seed)
        ks = jax.random.split(key, 12)
        C, IC = (64, 32)
        B, H, W = (8, 16, 16)
        s_in = 1.0 / np.sqrt(C)
        s_ic = 1.0 / np.sqrt(IC)
        return {'x': jax.random.normal(ks[0], (B, C, H, W), jnp.float32), 'Wg': jax.random.normal(ks[1], (IC, C), jnp.float32) * s_in, 'bg': jax.random.normal(ks[2], (IC,), jnp.float32) * s_in, 'Wt': jax.random.normal(ks[3], (IC, C), jnp.float32) * s_in, 'bt': jax.random.normal(ks[4], (IC,), jnp.float32) * s_in, 'Wp': jax.random.normal(ks[5], (IC, C), jnp.float32) * s_in, 'bp': jax.random.normal(ks[6], (IC,), jnp.float32) * s_in, 'Ww': jax.random.normal(ks[7], (C, IC), jnp.float32) * s_ic, 'bw': jax.random.normal(ks[8], (C,), jnp.float32) * s_ic, 'gamma': jax.random.normal(ks[9], (C,), jnp.float32), 'beta': jax.random.normal(ks[10], (C,), jnp.float32)}
    _L0_conv_all = _L0_conv_setup()
    _L0_conv_in = {k: v for k, v in _L0_conv_all.items() if k in ('Wg', 'bg', 'Wt', 'bt', 'Wp', 'bp', 'Ww', 'bw', 'gamma', 'beta')}
    del _L0_conv_all

    def _L1_conv_setup():
        import jax, jax.numpy as jnp
        import numpy as np
        C = 64
        EPS = 1e-05

        def _cb(p):
            return p[None, :, None, None]

        def binary_act(x):
            poly = jnp.where(x < -1.0, -1.0, jnp.where(x < 0.0, x * x + 2.0 * x, jnp.where(x < 1.0, -x * x + 2.0 * x, 1.0)))
            return jax.lax.stop_gradient(jnp.sign(x) - poly) + poly

        def bin_weight(w):
            scale = jax.lax.stop_gradient(jnp.mean(jnp.abs(w), axis=(1, 2, 3), keepdims=True))
            cl = jnp.clip(w, -1.0, 1.0)
            return jax.lax.stop_gradient(scale * jnp.sign(w) - cl) + cl

        def conv(x, w, pad):
            return jax.lax.conv_general_dilated(x, w, window_strides=(1, 1), padding=((pad, pad), (pad, pad)), dimension_numbers=('NCHW', 'OIHW', 'NCHW'))

        def bn(x, g, b, m, v):
            inv = g * jax.lax.rsqrt(v + EPS)
            return x * _cb(inv) + _cb(b - m * inv)

        def prelu(x, a):
            return jnp.where(x > 0, x, _cb(a) * x)
        key = jax.random.key(seed)
        ks = jax.random.split(key, 3)
        z = jnp.zeros((C,), jnp.float32)
        o = jnp.ones((C,), jnp.float32)
        return {'x': jax.random.normal(ks[0], (32, C, 56, 56), jnp.float32), 'w3': jax.random.uniform(ks[1], (C, C, 3, 3), jnp.float32) * 0.001, 'w1': jax.random.uniform(ks[2], (C, C, 1, 1), jnp.float32) * 0.001, 'b11': z, 'b12': z, 'b13': z, 'b21': z, 'b22': z, 'b23': z, 'g1': o, 'be1': z, 'm1': z, 'v1': o, 'g2': o, 'be2': z, 'm2': z, 'v2': o, 'a1': jnp.full((C,), 0.25, jnp.float32), 'a2': jnp.full((C,), 0.25, jnp.float32)}
    _L1_conv_all = _L1_conv_setup()
    _L1_conv_in = {k: v for k, v in _L1_conv_all.items() if k in ('w3', 'w1', 'b11', 'b12', 'b13', 'b21', 'b22', 'b23', 'g1', 'be1', 'm1', 'v1', 'g2', 'be2', 'm2', 'v2', 'a1', 'a2')}
    del _L1_conv_all

    def _L2_attn_setup():
        import jax, jax.numpy as jnp
        import numpy as np
        key = jax.random.key(seed)
        ks = jax.random.split(key, 6)
        b, t, k, h = (2, 512, 64, 8)
        s = 1.0 / np.sqrt(k)
        return {'x': jax.random.normal(ks[0], (b, t, k), dtype=jnp.float32), 'Wq': jax.random.normal(ks[1], (k, k * h), dtype=jnp.float32) * s, 'Wk': jax.random.normal(ks[2], (k, k * h), dtype=jnp.float32) * s, 'Wv': jax.random.normal(ks[3], (k, k * h), dtype=jnp.float32) * s, 'Wu': jax.random.normal(ks[4], (k * h, k), dtype=jnp.float32) * (1.0 / np.sqrt(k * h)), 'bu': jnp.zeros((k,), dtype=jnp.float32)}
    _L2_attn_all = _L2_attn_setup()
    _L2_attn_in = {k: v for k, v in _L2_attn_all.items() if k in ('Wq', 'Wk', 'Wv', 'Wu', 'bu')}
    del _L2_attn_all

    def _L2_ffn_setup():
        import jax, jax.numpy as jnp
        import numpy as np
        B, T, D, H, E = (16, 1024, 64, 128, 8)
        key = jax.random.key(seed)
        ks = jax.random.split(key, 5)
        x = jax.random.normal(ks[0], (B, T, D), dtype=jnp.float32)
        gate_w = jax.random.normal(ks[1], (D, E), dtype=jnp.float32) * 0.02
        gate_b = jnp.zeros((E,), dtype=jnp.float32)
        W1 = jax.random.normal(ks[2], (E, D, H), dtype=jnp.float32) * 0.02
        b1 = jnp.zeros((E, H), dtype=jnp.float32)
        W2 = jax.random.normal(ks[3], (E, H, D), dtype=jnp.float32) * 0.02
        b2 = jnp.zeros((E, D), dtype=jnp.float32)
        return {'x': x, 'gate_w': gate_w, 'gate_b': gate_b, 'W1': W1, 'b1': b1, 'W2': W2, 'b2': b2}
    _L2_ffn_all = _L2_ffn_setup()
    _L2_ffn_in = {k: v for k, v in _L2_ffn_all.items() if k in ('gate_w', 'gate_b', 'W1', 'b1', 'W2', 'b2')}
    del _L2_ffn_all

    def _L3_attn_setup():
        import math
        import jax, jax.numpy as jnp
        import numpy as np
        B, T, C = (4, 512, 64)
        LEVELS = 3
        NEAR_WINDOW = 16
        THETA = 10000.0
        EPS_L2 = 1e-08
        EPS_VAR = 1e-06

        def haar_basis(T, levels):
            cols = []
            for j in range(levels):
                bc = 2 ** j
                bs = T // bc
                half = bs // 2
                for k in range(bc):
                    v = np.zeros(T, np.float32)
                    s = k * bs
                    v[s:s + half] = 1.0 / math.sqrt(half)
                    v[s + half:s + bs] = -1.0 / math.sqrt(half)
                    cols.append(v)
            return jnp.asarray(np.stack(cols, axis=1))

        def rope_tables(T, dim):
            half = dim // 2
            inv_freq = 1.0 / THETA ** (np.arange(half, dtype=np.float32) / half)
            ang = np.arange(T, dtype=np.float32)[:, None] * inv_freq[None, :]
            return (jnp.asarray(np.cos(ang)), jnp.asarray(np.sin(ang)))

        def apply_rope(x, cos, sin):
            half = x.shape[-1] // 2
            x1, x2 = (x[..., :half], x[..., half:])
            return jnp.concatenate([x1 * cos - x2 * sin, x1 * sin + x2 * cos], axis=-1)

        def l2_normalize(x, eps=EPS_L2):
            return x / (jnp.linalg.norm(x, axis=-1, keepdims=True) + eps)

        def variance_scaled_softmax(scores, eps=EPS_VAR):
            finite = jnp.isfinite(scores)
            m = finite.astype(scores.dtype)
            n = jnp.clip(jnp.sum(m, axis=-1, keepdims=True), 1.0, None)
            safe = jnp.where(finite, scores, 0.0)
            mean = jnp.sum(safe * m, axis=-1, keepdims=True) / n
            var = jnp.sum((safe - mean) ** 2 * m, axis=-1, keepdims=True) / n
            std = jnp.sqrt(jnp.clip(var, eps, None))
            scaled = jnp.where(finite, (safe - mean) / std, -jnp.inf)
            out = jax.nn.softmax(scaled, axis=-1)
            return jnp.where(n == 0, jnp.zeros_like(out), out)
        key = jax.random.key(seed)
        kx, kq, kv, ko = jax.random.split(key, 4)
        lim = math.sqrt(6.0 / (C + C))
        return {'x': jax.random.normal(kx, (B, T, C), dtype=jnp.float32), 'W_Q': jax.random.uniform(kq, (C, C), jnp.float32, -lim, lim), 'W_V': jax.random.normal(kv, (C, C), jnp.float32) * 0.02, 'W_O': jax.random.normal(ko, (C, C), jnp.float32) * 0.02}
    _L3_attn_all = _L3_attn_setup()
    _L3_attn_in = {k: v for k, v in _L3_attn_all.items() if k in ('W_Q', 'W_V', 'W_O')}
    del _L3_attn_all

    def _L3_ffn_setup():
        import jax, jax.numpy as jnp
        import numpy as np
        D_MODEL = 64
        N_EXPERTS = 16
        HIDDEN = 128
        SCALE = 0.02
        key = jax.random.key(seed)
        ks = jax.random.split(key, 5)
        x = jax.random.normal(ks[0], (4, 2048, D_MODEL), dtype=jnp.float32)
        gate_w = jax.random.normal(ks[1], (D_MODEL, N_EXPERTS), dtype=jnp.float32) * SCALE
        gate_b = jnp.zeros((N_EXPERTS,), dtype=jnp.float32)
        w1 = jax.random.normal(ks[2], (N_EXPERTS, D_MODEL, HIDDEN), dtype=jnp.float32) * SCALE
        w2 = jax.random.normal(ks[3], (N_EXPERTS, D_MODEL, HIDDEN), dtype=jnp.float32) * SCALE
        w3 = jax.random.normal(ks[4], (N_EXPERTS, HIDDEN, D_MODEL), dtype=jnp.float32) * SCALE
        return {'x': x, 'gate_w': gate_w, 'gate_b': gate_b, 'w1': w1, 'w2': w2, 'w3': w3}
    _L3_ffn_all = _L3_ffn_setup()
    _L3_ffn_in = {k: v for k, v in _L3_ffn_all.items() if k in ('gate_w', 'gate_b', 'w1', 'w2', 'w3')}
    del _L3_ffn_all
    return {'x': x, 'L0_conv_Wg': _L0_conv_in['Wg'], 'L0_conv_bg': _L0_conv_in['bg'], 'L0_conv_Wt': _L0_conv_in['Wt'], 'L0_conv_bt': _L0_conv_in['bt'], 'L0_conv_Wp': _L0_conv_in['Wp'], 'L0_conv_bp': _L0_conv_in['bp'], 'L0_conv_Ww': _L0_conv_in['Ww'], 'L0_conv_bw': _L0_conv_in['bw'], 'L0_conv_gamma': _L0_conv_in['gamma'], 'L0_conv_beta': _L0_conv_in['beta'], 'L1_conv_w3': _L1_conv_in['w3'], 'L1_conv_w1': _L1_conv_in['w1'], 'L1_conv_b11': _L1_conv_in['b11'], 'L1_conv_b12': _L1_conv_in['b12'], 'L1_conv_b13': _L1_conv_in['b13'], 'L1_conv_b21': _L1_conv_in['b21'], 'L1_conv_b22': _L1_conv_in['b22'], 'L1_conv_b23': _L1_conv_in['b23'], 'L1_conv_g1': _L1_conv_in['g1'], 'L1_conv_be1': _L1_conv_in['be1'], 'L1_conv_m1': _L1_conv_in['m1'], 'L1_conv_v1': _L1_conv_in['v1'], 'L1_conv_g2': _L1_conv_in['g2'], 'L1_conv_be2': _L1_conv_in['be2'], 'L1_conv_m2': _L1_conv_in['m2'], 'L1_conv_v2': _L1_conv_in['v2'], 'L1_conv_a1': _L1_conv_in['a1'], 'L1_conv_a2': _L1_conv_in['a2'], 'L2_attn_Wq': _L2_attn_in['Wq'], 'L2_attn_Wk': _L2_attn_in['Wk'], 'L2_attn_Wv': _L2_attn_in['Wv'], 'L2_attn_Wu': _L2_attn_in['Wu'], 'L2_attn_bu': _L2_attn_in['bu'], 'L2_ffn_gate_w': _L2_ffn_in['gate_w'], 'L2_ffn_gate_b': _L2_ffn_in['gate_b'], 'L2_ffn_W1': _L2_ffn_in['W1'], 'L2_ffn_b1': _L2_ffn_in['b1'], 'L2_ffn_W2': _L2_ffn_in['W2'], 'L2_ffn_b2': _L2_ffn_in['b2'], 'L3_attn_W_Q': _L3_attn_in['W_Q'], 'L3_attn_W_V': _L3_attn_in['W_V'], 'L3_attn_W_O': _L3_attn_in['W_O'], 'L3_ffn_gate_w': _L3_ffn_in['gate_w'], 'L3_ffn_gate_b': _L3_ffn_in['gate_b'], 'L3_ffn_w1': _L3_ffn_in['w1'], 'L3_ffn_w2': _L3_ffn_in['w2'], 'L3_ffn_w3': _L3_ffn_in['w3']}

def reference(x, L0_conv_Wg, L0_conv_bg, L0_conv_Wt, L0_conv_bt, L0_conv_Wp, L0_conv_bp, L0_conv_Ww, L0_conv_bw, L0_conv_gamma, L0_conv_beta, L1_conv_w3, L1_conv_w1, L1_conv_b11, L1_conv_b12, L1_conv_b13, L1_conv_b21, L1_conv_b22, L1_conv_b23, L1_conv_g1, L1_conv_be1, L1_conv_m1, L1_conv_v1, L1_conv_g2, L1_conv_be2, L1_conv_m2, L1_conv_v2, L1_conv_a1, L1_conv_a2, L2_attn_Wq, L2_attn_Wk, L2_attn_Wv, L2_attn_Wu, L2_attn_bu, L2_ffn_gate_w, L2_ffn_gate_b, L2_ffn_W1, L2_ffn_b1, L2_ffn_W2, L2_ffn_b2, L3_attn_W_Q, L3_attn_W_V, L3_attn_W_O, L3_ffn_gate_w, L3_ffn_gate_b, L3_ffn_w1, L3_ffn_w2, L3_ffn_w3):
    import jax
    import jax.numpy as jnp

    def _L0_conv_ref(x, Wg, bg, Wt, bt, Wp, bp, Ww, bw, gamma, beta):
        import jax, jax.numpy as jnp
        import numpy as np
        EPS = 1e-05

        def _conv1x1(x, W, b):
            return jnp.einsum('bchw,oc->bohw', x, W) + b[None, :, None, None]

        def _maxpool2(x):
            B, C, H, W = x.shape
            return x.reshape(B, C, H // 2, 2, W // 2, 2).max(axis=(3, 5))
        B, C, H, W = x.shape
        IC = Wg.shape[0]
        g_x = _maxpool2(_conv1x1(x, Wg, bg))
        g_x = g_x.reshape(B, IC, -1).transpose(0, 2, 1)
        theta_x = _conv1x1(x, Wt, bt).reshape(B, IC, -1).transpose(0, 2, 1)
        phi_x = _maxpool2(_conv1x1(x, Wp, bp)).reshape(B, IC, -1)
        f = jnp.einsum('bni,bim->bnm', theta_x, phi_x)
        f_div_C = jax.nn.softmax(f, axis=-1)
        y = jnp.einsum('bnm,bmi->bni', f_div_C, g_x)
        y = y.transpose(0, 2, 1).reshape(B, IC, H, W)
        w_y = _conv1x1(y, Ww, bw)
        mu = w_y.mean(axis=(0, 2, 3))
        var = w_y.var(axis=(0, 2, 3))
        w_y = (w_y - mu[None, :, None, None]) * jax.lax.rsqrt(var + EPS)[None, :, None, None]
        w_y = w_y * gamma[None, :, None, None] + beta[None, :, None, None]
        return w_y + x

    def _L1_conv_ref(x, w3, w1, b11, b12, b13, b21, b22, b23, g1, be1, m1, v1, g2, be2, m2, v2, a1, a2):
        import jax, jax.numpy as jnp
        import numpy as np
        C = 64
        EPS = 1e-05

        def _cb(p):
            return p[None, :, None, None]

        def binary_act(x):
            poly = jnp.where(x < -1.0, -1.0, jnp.where(x < 0.0, x * x + 2.0 * x, jnp.where(x < 1.0, -x * x + 2.0 * x, 1.0)))
            return jax.lax.stop_gradient(jnp.sign(x) - poly) + poly

        def bin_weight(w):
            scale = jax.lax.stop_gradient(jnp.mean(jnp.abs(w), axis=(1, 2, 3), keepdims=True))
            cl = jnp.clip(w, -1.0, 1.0)
            return jax.lax.stop_gradient(scale * jnp.sign(w) - cl) + cl

        def conv(x, w, pad):
            return jax.lax.conv_general_dilated(x, w, window_strides=(1, 1), padding=((pad, pad), (pad, pad)), dimension_numbers=('NCHW', 'OIHW', 'NCHW'))

        def bn(x, g, b, m, v):
            inv = g * jax.lax.rsqrt(v + EPS)
            return x * _cb(inv) + _cb(b - m * inv)

        def prelu(x, a):
            return jnp.where(x > 0, x, _cb(a) * x)
        out1 = binary_act(x + _cb(b11))
        out1 = conv(out1, bin_weight(w3), pad=1)
        out1 = bn(out1, g1, be1, m1, v1)
        out1 = x + out1
        out1 = prelu(out1 + _cb(b12), a1) + _cb(b13)
        out2 = binary_act(out1 + _cb(b21))
        out2 = conv(out2, bin_weight(w1), pad=0)
        out2 = bn(out2, g2, be2, m2, v2) + out1
        out2 = prelu(out2 + _cb(b22), a2) + _cb(b23)
        return out2

    def _L2_attn_ref(x, Wq, Wk, Wv, Wu, bu):
        import jax, jax.numpy as jnp
        import numpy as np
        b, t, k = x.shape
        h = Wq.shape[1] // k
        scale = k ** (-0.25)
        q = (x @ Wq).reshape(b, t, h, k).transpose(0, 2, 1, 3) * scale
        kk = (x @ Wk).reshape(b, t, h, k).transpose(0, 2, 1, 3) * scale
        v = (x @ Wv).reshape(b, t, h, k).transpose(0, 2, 1, 3)
        dot = jnp.einsum('bhqk,bhsk->bhqs', q, kk)
        attn = jax.nn.softmax(dot, axis=-1)
        out = jnp.einsum('bhqs,bhsk->bhqk', attn, v)
        out = out.transpose(0, 2, 1, 3).reshape(b, t, h * k)
        return out @ Wu + bu

    def _L2_ffn_ref(x, gate_w, gate_b, W1, b1, W2, b2):
        import jax, jax.numpy as jnp
        import numpy as np
        B, T, D, H, E = (16, 1024, 64, 128, 8)
        Bb, Tt, Dd = x.shape
        Ee = gate_w.shape[1]
        xf = x.reshape(-1, Dd)
        N = xf.shape[0]
        logits = xf @ gate_w + gate_b
        probs = jax.nn.softmax(logits, axis=-1)
        top2_vals, top2_idx = jax.lax.top_k(probs, 2)
        cw = jnp.zeros((N, Ee), dtype=xf.dtype).at[jnp.arange(N)[:, None], top2_idx].add(top2_vals)

        def step(acc, params):
            w1, bb1, w2, bb2, we = params
            h = jax.nn.gelu(xf @ w1 + bb1, approximate=False)
            y = h @ w2 + bb2
            return (acc + we[:, None] * y, None)
        out, _ = jax.lax.scan(step, jnp.zeros_like(xf), (W1, b1, W2, b2, cw.T))
        return out.reshape(Bb, Tt, Dd)

    def _L3_attn_ref(x, W_Q, W_V, W_O):
        import math
        import jax, jax.numpy as jnp
        import numpy as np
        B, T, C = (4, 512, 64)
        LEVELS = 3
        NEAR_WINDOW = 16
        THETA = 10000.0
        EPS_L2 = 1e-08
        EPS_VAR = 1e-06

        def haar_basis(T, levels):
            cols = []
            for j in range(levels):
                bc = 2 ** j
                bs = T // bc
                half = bs // 2
                for k in range(bc):
                    v = np.zeros(T, np.float32)
                    s = k * bs
                    v[s:s + half] = 1.0 / math.sqrt(half)
                    v[s + half:s + bs] = -1.0 / math.sqrt(half)
                    cols.append(v)
            return jnp.asarray(np.stack(cols, axis=1))

        def rope_tables(T, dim):
            half = dim // 2
            inv_freq = 1.0 / THETA ** (np.arange(half, dtype=np.float32) / half)
            ang = np.arange(T, dtype=np.float32)[:, None] * inv_freq[None, :]
            return (jnp.asarray(np.cos(ang)), jnp.asarray(np.sin(ang)))

        def apply_rope(x, cos, sin):
            half = x.shape[-1] // 2
            x1, x2 = (x[..., :half], x[..., half:])
            return jnp.concatenate([x1 * cos - x2 * sin, x1 * sin + x2 * cos], axis=-1)

        def l2_normalize(x, eps=EPS_L2):
            return x / (jnp.linalg.norm(x, axis=-1, keepdims=True) + eps)

        def variance_scaled_softmax(scores, eps=EPS_VAR):
            finite = jnp.isfinite(scores)
            m = finite.astype(scores.dtype)
            n = jnp.clip(jnp.sum(m, axis=-1, keepdims=True), 1.0, None)
            safe = jnp.where(finite, scores, 0.0)
            mean = jnp.sum(safe * m, axis=-1, keepdims=True) / n
            var = jnp.sum((safe - mean) ** 2 * m, axis=-1, keepdims=True) / n
            std = jnp.sqrt(jnp.clip(var, eps, None))
            scaled = jnp.where(finite, (safe - mean) / std, -jnp.inf)
            out = jax.nn.softmax(scaled, axis=-1)
            return jnp.where(n == 0, jnp.zeros_like(out), out)
        Bx, Tx, Cx = x.shape
        cos, sin = rope_tables(Tx, Cx)
        W_h = haar_basis(Tx, LEVELS)
        WK = jnp.linalg.pinv(W_Q)
        q = x @ W_Q
        k = x @ WK.T
        v = x @ W_V.T
        q = l2_normalize(apply_rope(q, cos, sin))
        k = l2_normalize(apply_rope(k, cos, sin))
        pos = jnp.arange(Tx)
        dist = pos[None, :] - pos[:, None]
        near_mask = (dist >= 0) & (dist <= NEAR_WINDOW)
        causal = dist <= 0
        scale = 1.0 / math.sqrt(Cx)
        attn_scores = jnp.einsum('btc,bsc->bts', q, k) * scale
        attn_near = jnp.where(near_mask, attn_scores, -jnp.inf)
        q_coef = jnp.einsum('tw,btc->bwc', W_h, q)
        k_coef = jnp.einsum('tw,btc->bwc', W_h, k)
        attn_coef = jnp.einsum('bwc,bvc->bwv', q_coef, k_coef) * scale
        attn_far = jnp.einsum('tw,bwv,sv->bts', W_h, attn_coef, W_h)
        attn = jnp.where(near_mask, attn_near, attn_far)
        attn = jnp.where(causal, attn, -jnp.inf)
        n_visible = jnp.clip(jnp.sum(jnp.isfinite(attn), axis=-1, keepdims=True).astype(attn.dtype), 1.0, None)
        attn = attn / jnp.sqrt(n_visible)
        attn = variance_scaled_softmax(attn)
        y = jnp.einsum('bts,bsc->btc', attn, v)
        return y @ W_O.T

    def _L3_ffn_ref(x, gate_w, gate_b, w1, w2, w3):
        import jax, jax.numpy as jnp
        import numpy as np
        D_MODEL = 64
        N_EXPERTS = 16
        HIDDEN = 128
        SCALE = 0.02
        n_experts = w1.shape[0]
        logits = jnp.einsum('bsd,de->bse', x, gate_w) + gate_b
        probs = jax.nn.softmax(logits, axis=-1)
        top_probs, top_idx = jax.lax.top_k(probs, 2)
        top_probs = top_probs / jnp.sum(top_probs, axis=-1, keepdims=True)
        dispatch = jnp.sum(jax.nn.one_hot(top_idx, n_experts, dtype=x.dtype) * top_probs[..., None], axis=-2)
        h1 = jnp.einsum('bsd,edh->bseh', x, w1)
        h2 = jnp.einsum('bsd,edh->bseh', x, w2)
        hidden = jax.nn.silu(h1) * h2
        expert_out = jnp.einsum('bseh,eho->bseo', hidden, w3)
        return jnp.einsum('bseo,bse->bso', expert_out, dispatch)

    def _gn(v, G=32, eps=1e-05):
        B_, C_, H_, W_ = v.shape
        g = v.reshape(B_, G, C_ // G, H_, W_)
        m = jnp.mean(g, axis=(2, 3, 4), keepdims=True)
        s = jnp.var(g, axis=(2, 3, 4), keepdims=True)
        return ((g - m) / jnp.sqrt(s + eps)).reshape(v.shape)

    def _ln_c(v, eps=1e-06):
        m = jnp.mean(v, axis=1, keepdims=True)
        s = jnp.var(v, axis=1, keepdims=True)
        return (v - m) / jnp.sqrt(s + eps)

    def _ln_t(v, eps=1e-05):
        m = jnp.mean(v, axis=-1, keepdims=True)
        s = jnp.var(v, axis=-1, keepdims=True)
        return (v - m) / jnp.sqrt(s + eps)

    def _to_tokens(v):
        B_, C_, H_, W_ = v.shape
        return v.reshape(B_, C_, H_ * W_).transpose(0, 2, 1)

    def _from_tokens(t, like):
        B_, C_, H_, W_ = like.shape
        return t.transpose(0, 2, 1).reshape(B_, C_, H_, W_)
    x = _L0_conv_ref(x, L0_conv_Wg, L0_conv_bg, L0_conv_Wt, L0_conv_bt, L0_conv_Wp, L0_conv_bp, L0_conv_Ww, L0_conv_bw, L0_conv_gamma, L0_conv_beta)
    x = _L1_conv_ref(x, L1_conv_w3, L1_conv_w1, L1_conv_b11, L1_conv_b12, L1_conv_b13, L1_conv_b21, L1_conv_b22, L1_conv_b23, L1_conv_g1, L1_conv_be1, L1_conv_m1, L1_conv_v1, L1_conv_g2, L1_conv_be2, L1_conv_m2, L1_conv_v2, L1_conv_a1, L1_conv_a2)
    t = _to_tokens(x)
    t = t + _L2_attn_ref(_ln_t(t), L2_attn_Wq, L2_attn_Wk, L2_attn_Wv, L2_attn_Wu, L2_attn_bu)
    t = t + _L2_ffn_ref(_ln_t(t), L2_ffn_gate_w, L2_ffn_gate_b, L2_ffn_W1, L2_ffn_b1, L2_ffn_W2, L2_ffn_b2)
    t = t + _L3_attn_ref(_ln_t(t), L3_attn_W_Q, L3_attn_W_V, L3_attn_W_O)
    t = t + _L3_ffn_ref(_ln_t(t), L3_ffn_gate_w, L3_ffn_gate_b, L3_ffn_w1, L3_ffn_w2, L3_ffn_w3)
    x = _from_tokens(t, x)
    return x

_drawn_inputs = setup_inputs


def setup_inputs(seed=0):
    import zlib

    import numpy as np

    out = dict(_drawn_inputs(seed))
    spreads = {'L1_conv_b11': (0.0, 0.8),
     'L1_conv_b12': (0.0, 0.1),
     'L1_conv_b13': (0.0, 0.1),
     'L1_conv_b21': (0.0, 0.8),
     'L1_conv_b22': (0.0, 0.1),
     'L1_conv_b23': (0.0, 0.1),
     'L1_conv_g1': (1.0, 0.6),
     'L1_conv_be1': (0.0, 0.1),
     'L1_conv_m1': (0.0, 0.1),
     'L1_conv_v1': (1.0, 0.6),
     'L1_conv_g2': (1.0, 0.6),
     'L1_conv_be2': (0.0, 0.1),
     'L1_conv_m2': (0.0, 0.1),
     'L1_conv_v2': (1.0, 0.6),
     'L1_conv_a1': (0.25, 0.6),
     'L1_conv_a2': (0.25, 0.6),
     'L2_attn_bu': (0.0, 0.1),
     'L2_ffn_gate_b': (0.0, 0.532),
     'L2_ffn_b1': (0.0, 0.8),
     'L2_ffn_b2': (0.0, 0.503),
     'L3_ffn_gate_b': (0.0, 0.8)}
    factors = {'L0_conv_bg': 8.0,
     'L0_conv_bp': 8.0,
     'L0_conv_bw': 8.0,
     'L1_conv_w3': 8.0,
     'L1_conv_w1': 8.0,
     'L2_ffn_gate_w': 5.066,
     'L2_ffn_W1': 8.0,
     'L2_ffn_W2': 8.0,
     'L3_attn_W_Q': 8.0,
     'L3_attn_W_V': 3.913,
     'L3_attn_W_O': 3.929,
     'L3_ffn_gate_w': 8.0,
     'L3_ffn_w1': 8.0,
     'L3_ffn_w2': 8.0,
     'L3_ffn_w3': 8.0}
    for name, (base, spread) in spreads.items():
        noise = np.random.default_rng([zlib.crc32(name.encode()), seed]).standard_normal(out[name].shape)
        drawn = base * np.exp(spread * noise) if base else spread * noise
        out[name] = jnp.asarray(drawn.astype(out[name].dtype))
    for name, factor in factors.items():
        out[name] = (out[name] * factor).astype(out[name].dtype)
    return out
```

```python
from contextlib import ExitStack
import math

import numpy as np

import concourse.bass as bass
from concourse import mybir

F32 = mybir.dt.float32
F32R = mybir.dt.float32r
BF16 = mybir.dt.bfloat16
ALU = mybir.AluOpType
ACT = mybir.ActivationFunctionType
AX = mybir.AxisListType

P = 128
B, C, IMG = 8, 64, 16
N = IMG * IMG
G, J, U = 2, B // 2, N // P
TILES = B * U
TOK = B * N
IC = 32
POOLED = N // 4
HEADS = 8
EXP2, EXP3, HID = 8, 16, 128
CHUNK = 512
CHUNKS = TOK // CHUNK
CT = CHUNK // P
BLK = 32
NB = N // BLK
LEVELS = 3
THETA = 10000.0
PAD = IMG + 2
EPS_BN, EPS_LN, EPS_VAR, EPS_L2 = 1e-5, 1e-5, 1e-6, 1e-8
NS_PER_BATCH = 10
HIDDEN_SCORE = -30000.0

VECS = ["bpg_bt", "bw", "gamma", "beta", "b11", "b12", "b13", "b21", "b22", "b23",
        "g1", "be1", "m1", "v1", "g2", "be2", "m2", "v2", "a1", "a2"]
VI = {n: i for i, n in enumerate(VECS)}

CONSTS = [("ident", P), ("halfavg", P), ("cos", 256), ("sin", 256), ("lower", P), ("expand", U * P),
          ("basis", U * NB), ("inblock", U * NB), ("own", U * NB), ("below", U * NB),
          ("count", U * 9), ("mask", U * 9), ("invn", U), ("scale", U)]
CO, _at = {}, 0
for _n, _w in CONSTS:
    CO[_n] = (_at, _w)
    _at += _w
NCONST = _at


def constants():
    out = np.zeros((P, NCONST), np.float32)

    def put(name, a):
        at, w = CO[name]
        a = np.asarray(a, np.float32)
        out[:a.shape[0], at:at + w] = a.reshape(a.shape[0], w)

    put("ident", np.eye(P))
    p = np.arange(P)
    put("halfavg", 0.5 * (p[:, None] % C == p[None, :] % C))
    half = C // 2
    inv_freq = 1.0 / THETA ** (np.arange(half, dtype=np.float32) / half)
    ang = np.arange(N, dtype=np.float32)[:, None] * inv_freq[None, :].astype(np.float32)

    def rope(t):
        t = t.astype(np.float32).reshape(U, P, 1, half).repeat(4, axis=2)
        return t.transpose(1, 0, 2, 3)
    put("cos", rope(np.cos(ang)))
    put("sin", rope(np.sin(ang)))
    put("lower", (p[:, None] // BLK == p[None, :] // BLK) & (p[:, None] < p[None, :]))
    tok = np.arange(N)
    blk = tok // BLK
    onehot = (blk[:, None] == np.arange(NB)[None, :]).astype(np.float32)
    put("expand", onehot.T)
    haar = []
    for level in range(LEVELS):
        size = N // 2 ** level
        for k in range(2 ** level):
            v = np.zeros(N)
            v[k * size:k * size + size // 2] = 1 / math.sqrt(size // 2)
            v[k * size + size // 2:(k + 1) * size] = -1 / math.sqrt(size // 2)
            haar.append(v)
    haar = np.stack(haar, 1)

    def by_tile(a):
        return np.asarray(a, np.float32).reshape(U, P, -1).transpose(1, 0, 2)
    put("basis", by_tile(haar @ haar[::BLK].T))
    put("inblock", by_tile(onehot))
    put("own", by_tile(onehot))
    put("below", by_tile(np.arange(NB)[None, :] < blk[:, None]))
    count = np.zeros((N, 9), np.float32)
    count[:, :NB] = np.clip(tok[:, None] - BLK * np.arange(NB)[None, :], 0, BLK)
    count[:, NB] = 1
    put("count", by_tile(count))
    put("mask", by_tile(np.where(count > 0, 0.0, HIDDEN_SCORE)))
    put("invn", by_tile(1.0 / (tok + 1.0)))
    put("scale", by_tile(1.0 / np.sqrt(float(C)) / np.sqrt(tok + 1.0)))
    return out


def hybrid_kernel(nc, io, out):
    ctx = ExitStack()
    with ctx:
        def sb(name, shape, dt=F32):
            return ctx.enter_context(nc.sbuf_tensor(name, shape, dt))

        sems = {}

        def S(name):
            if name not in sems:
                sems[name] = ctx.enter_context(nc.semaphore(name))
            return sems[name]

        consts = sb("consts", [P, NCONST])
        vec = sb("vec", [P, len(VECS)])

        def con(name):
            at, w = CO[name]
            return consts[:, at:at + w]

        def v_(name):
            return vec[:, VI[name]:VI[name] + 1]

        ident = con("ident")
        x0 = sb("x0", [P, J * N])
        w0 = sb("w0", [P, 96])
        wwT = sb("wwT", [P, C])
        theta_qk = sb("theta_qk", [P, TOK])
        theta = theta_qk[0:IC, :].rearrange("p (b n) -> p b n", b=B)
        QK = theta_qk[:, :].rearrange("p (a t h c) -> p a t h c", a=2, t=TILES, h=2)
        probT_rot = sb("probT_rot", [P, TOK])
        probT = probT_rot[0:C, :]
        R = probT_rot[:, :].rearrange("p (a t h c) -> p a t h c", a=2, t=TILES, h=2)
        pooled = sb("pooled", [2 * IC, B, POOLED])
        pg = sb("pg", [2 * IC, B, POOLED])
        gw = sb("gw", [C, B, C])
        f_both = sb("f_both", [P, 2, TILES, POOLED])
        f_sub, f_exp = f_both[:, 0], f_both[:, 1]
        RN = f_both[:, :].rearrange("p a t (h c) -> p (a t h c)", h=2).rearrange(
            "p (t h a c) -> p t h a c", t=TILES, h=2, a=2)
        f_prob = sb("f_prob", [P, TILES, POOLED])
        f_col = sb("f_col", [P, 3, TILES])
        wy = sb("wy", [P, J * N])
        bn6 = sb("bn6", [P, 2, 6])
        col = sb("col", [P, 64])
        x1 = sb("x1", [P, J * N])
        sgn = sb("sgn", [P, J, PAD, PAD], BF16)
        sgn2 = sb("sgn2", [P, J * N], BF16)
        w3T = sb("w3T", [P, 9, C])
        w1T = sb("w1T", [P, C])
        w3n = sb("w3n", [P, C * 9])
        w1n = sb("w1n", [P, C])
        w3s = sb("w3s", [P, 9, P], BF16)
        w1s = sb("w1s", [P, P], BF16)
        va = sb("va", [P, J * N])
        vb = sb("vb", [P, J * N])
        r1 = sb("r1", [P, J * N])
        x2 = sb("x2", [P, J * N])

        T = sb("T", [P, TILES, C])
        ln6 = sb("ln6", [P, TILES, 6])
        lnc = sb("lnc", [P, 8, TILES])
        xn2 = sb("xn2", [P, TILES, 2, C])
        XS = sb("XS", [P, TILES * P], F32R)

        wqT = sb("wqT", [C, HEADS, C])
        wkvT = sb("wkvT", [C, 2, HEADS, P])
        wkT, wvT = wkvT[:, 0], wkvT[:, 1]
        wu = sb("wu", [C, HEADS, C])
        bu = sb("bu", [P, C])
        AH = sb("AH", [P, HEADS, 2, C], F32R)
        AL = sb("AL", [P, HEADS, 2, C], F32R)
        GH = sb("GH", [P, HEADS * C], F32R)
        GL = sb("GL", [P, HEADS * C], F32R)
        xcur = sb("xcur", [P, 4, P], F32R)
        KH = sb("KH", [P, 2, 2, N], F32R)
        KL = sb("KL", [P, 2, 2, N], F32R)
        vproj = sb("vproj", [P, 4, HEADS, C + 1])
        negmax = sb("negmax", [P, 4, U])
        prob = sb("prob", [P, 2, U, N])
        pT = sb("pT", [P, 2, U, N])
        rsum = sb("rsum", [P, 2, 4])
        onorm = sb("onorm", [P, 2, U, 2, C])
        acc = sb("acc", [P, G, U, C])

        nsA = sb("nsA", [C, C])
        nsAT = sb("nsAT", [C, 2, C])
        nsX = sb("nsX", [C, 2, C])
        nsY = sb("nsY", [C, C])
        eye2 = sb("eye2", [C, C])
        nsc = sb("nsc", [C, 4])
        zeros = sb("zeros", [P, HID])
        ones64 = sb("ones64", [C, C])
        eyedup = sb("eyedup", [C, P])

        gw2 = sb("gw2", [P, EXP2])
        gw2p = sb("gw2p", [P, 2, EXP2], F32R)
        gb2 = sb("gb2", [P, EXP2])
        gw3 = sb("gw3", [P, EXP3])
        gw3p = sb("gw3p", [P, 2, EXP3], F32R)
        gb3 = sb("gb3", [P, EXP3])
        logit = sb("logit", [P, TILES, EXP3])
        top8 = sb("top8", [P, TILES, 8])
        gexp = w3n[:, TILES * EXP3:2 * TILES * EXP3].rearrange("p (t e) -> p t e", e=EXP3)
        gsel = w3n[:, 0:TILES * EXP3].rearrange("p (t e) -> p t e", e=EXP3)
        cw = sb("cw", [P, EXP3, TILES])
        cw2 = sb("cw2", [P, TILES, EXP2])
        gcol = sb("gcol", [P, 2, TILES])
        cwT = sb("cwT", [P, P])
        b2blk = sb("b2blk", [P, TILES, C])

        raw2 = sb("raw2", [P, 2, HID + C + 1])
        raw3 = sb("raw3", [P, 2, 2 * HID + C])
        wp1 = sb("wp1", [P, 2, 2, HID], F32R)
        wp2 = sb("wp2", [P, 2, 2, HID], F32R)
        silu = wy[:].rearrange("p (a n) -> p a n", a=2)
        hid = sb("hid", [P, 2, CHUNK])
        ytmp = x0[:].rearrange("p (a n) -> p a n", a=2)

        wv3 = sb("wv3", [C, P])
        wo3T = sb("wo3T", [C, C])
        wq3 = sb("wq3", [P, C])
        qkvw = sb("qkvw", [P, 2, 192], F32R)
        m_a, m_b, m_c, m_d = va, vb, r1, x1
        V3 = f_prob
        q8 = sb("q8", [C, B, NB])
        k8 = sb("k8", [C, B, NB])
        F8 = sb("F8", [NB, B * NB])
        a9 = sb("a9", [P, U, B, 9])
        z9 = sb("z9", [P, U, B, 9])
        e9 = sb("e9", [P, U, B, 9])
        t9 = sb("t9", [P, U, B, 9])
        s9 = sb("s9", [P, 8, U, B])
        dcol = sb("dcol", [P, TILES])
        n2 = sb("n2", [P, 3, TILES * 2])
        pown = sb("pown", [P, TILES])
        pdia = sb("pdia", [P, TILES])
        p8 = sb("p8", [P, U, B, NB])
        p8T = wkvT[0:NB].rearrange("p a h n -> p (a h n)")
        vsum = pg[0:NB]
        yfin = x2

        ps = ctx.enter_context(nc.psum_tensor("ps", [P, 8, 512], F32))

        def banks(a, b):
            return ps[:, a:b, :].rearrange("p a n -> p (a n)")

        def heads_added_after(k):
            return 7 * (k // 4) + 2 * (k % 4) + 1

        qs = [(j, u, g) for j in range(J) for u in range(U) for g in range(G)]

        def step_of(eng, name):
            done = [0]

            def step(ins):
                done[0] += 1
                ins.then_inc(S(name), 1)
                eng.wait_ge(S(name), done[0])
            return step

        block = ctx.enter_context(nc.Block())

        @block.sync
        def _(sp):
            def load(dst, src, name):
                sp.dma_start(dst, src).then_inc(S(name), 16)

            load(w0[:], io["w0"], "l0_loaded")
            load(x0[:], io["x"], "l0_loaded")
            load(vec[:], io["vec"], "vec_loaded")
            load(consts[:], io["consts"], "consts_loaded")
            load(w3n[:], io["w3n"], "l1_loaded")
            load(w1n[:], io["w1n"], "l1_loaded")
            load(w3T[:], io["w3T"], "l1_loaded")
            load(w1T[:], io["w1T"], "l1_loaded")
            load(wwT[IC:2 * IC, :], io["wwT"], "ww_loaded")
            load(wqT[:], io["wqT"], "attn_loaded")
            load(wkT[:], io["wkT"], "attn_loaded")
            load(wvT[:], io["wvT"], "attn_loaded")
            load(wu[:], io["wu"], "attn_loaded")
            load(bu[:], io["bu"], "bu_loaded")
            load(nsA[:], io["q3"][0:C, :], "ns_loaded")
            load(nsAT[:].rearrange("p a c -> p (a c)"), io["q3T"], "ns_loaded")
            load(wq3[:], io["q3"], "l3_loaded")
            load(wv3[:], io["wv3"], "l3_loaded")
            load(wo3T[:], io["wo3T"], "l3_loaded")
            load(gw2[:], io["gw2"], "gate_loaded")
            load(gb2[:], io["gb2"], "gate_loaded")
            load(gw3[:], io["gw3"], "gate_loaded")
            load(gb3[:], io["gb3"], "gate_loaded")
            sp.wait_ge(S("b2_zeroed"), 1)
            for q in range(TILES):
                load(b2blk[q * EXP2:(q + 1) * EXP2, q, :], io["b2"], "b2_loaded")
            for which, experts, raw in ((2, EXP2, raw2), (3, EXP3, raw3)):
                sp.sem_inc(S(f"f{which}_out_chunk"), 8)
                with sp.Fori(0, experts // 2) as i:
                    for e in range(2):
                        sp.wait_ge(S(f"f{which}_out_chunk"), i * 8 + 4 * (e + 1))
                        src = io[f"raw{which}"][bass.ds(i * (2 * P) + e * P, P), :]
                        sp.dma_start(raw[:, e, :], src).then_inc(S(f"f{which}_raw{e}"), 16)
            sp.wait_ge(S("out_ready"), 2)
            sp.dma_start(out, yfin[:]).then_inc(S("stored"), 16)
            sp.wait_ge(S("stored"), 16)

        def ffn(gp, which):
            experts, raw, parts = {2: (EXP2, raw2, [wp1]), 3: (EXP3, raw3, [wp1, wp2])}[which]
            nm = f"f{which}_"
            n = len(parts)

            def weights(i, e):
                gp.wait_ge(S(nm + "h_ready"), i * 8 + 4 * (e + 1))
                gp.wait_ge(S(nm + f"raw{e}"), i * 16 + 16)
                for k, part in enumerate(parts):
                    src = raw[:, e, k * HID:(k + 1) * HID]
                    gp.tensor_tensor(part[:, e, 0, :], src, zeros[:], ALU.add).then_inc(S(nm + "w_high"), 1)
                    gp.wait_ge(S(nm + "w_high"), i * (2 * n) + (n * e + k + 1))
                    gp.tensor_tensor(part[:, e, 1, :], src, part[:, e, 0, :].bitcast(F32),
                                     ALU.subtract).then_inc(S(nm + "w_split"), 1)

            def add_up(i, e):
                gp.wait_ge(S("ln_normalised"), TILES * (2 * which - 2))
                gp.wait_ge(S(nm + "base_ready"), 2)
                for half in range(2):
                    gp.wait_ge(S(nm + "y_weighted"), i * 4 + (4 + 2 * e + half + 1))
                    gp.wait_ge(S(nm + "added"), i * 4 + (2 * e + half + 3))
                    t = T[:, 8 * half:8 * half + 8, :]
                    gp.tensor_tensor(t, t, ytmp[:, half, :].rearrange("p (t c) -> p t c", c=C),
                                     ALU.add).then_inc(S(nm + "added"), 1)

            gp.sem_inc(S(nm + "added"), 1)
            with gp.Fori(0, experts // 2) as i:
                weights(i, 0)
                add_up(i, -1)
                weights(i, 1)
                add_up(i, 0)
            add_up(experts // 2, -1)

        def l3_pool(gp):
            gp.wait_ge(S("qk_evac"), 16)
            gp.wait_ge(S("consts_loaded"), 16)
            q1 = QK[:, 0].rearrange("p (j r) h c -> p j (r h c)", j=J)
            q2 = QK[:, 1].rearrange("p (j r) h c -> p j (r h c)", j=J)
            sin = con("sin").unsqueeze(1).broadcast_to([P, J, 256])
            gp.tensor_tensor(m_b[:].rearrange("p (j r) -> p j r", j=J), q2, sin,
                             ALU.mult).then_inc(S("rope_pool"), 1)
            gp.tensor_tensor(m_c[:].rearrange("p (j r) -> p j r", j=J), q1, sin,
                             ALU.mult).then_inc(S("rope_pool"), 1)
            gp.wait_ge(S("pdia_ready"), 1)
            gp.tensor_tensor(m_d[:].rearrange("p (t c) -> p t c", c=C), V3[:],
                             pdia[:].unsqueeze(2).broadcast_to([P, TILES, C]),
                             ALU.mult).then_inc(S("diag_done"), 1)

        @block.gpsimd
        def _(gp):
            step = step_of(gp, "gp_step")
            gp.memset(sgn[:], 0.0).then_inc(S("pads_zeroed"), 1)
            gp.memset(w3s[:], 0.0).then_inc(S("pads_zeroed"), 1)
            gp.memset(w1s[:], 0.0).then_inc(S("pads_zeroed"), 1)
            gp.memset(zeros[:], 0.0).then_inc(S("zeros_ready"), 1)
            gp.wait_ge(S("zeros_ready"), 1)
            gp.memset(ones64[:], 1.0).then_inc(S("ones_ready"), 1)
            gp.memset(b2blk[:], 0.0).then_inc(S("b2_zeroed"), 1)
            gp.memset(vproj[:], 1.0).then_inc(S("vproj_ones"), 1)
            gp.wait_ge(S("gate_loaded"), 64)
            for raw, parts in ((gw2, gw2p), (gw3, gw3p)):
                step(gp.tensor_copy(parts[:, 0, :], raw[:]))
                gp.tensor_tensor(parts[:, 1, :], raw[:], parts[:, 0, :].bitcast(F32),
                                 ALU.subtract).then_inc(S("gate_split"), 1)

            gp.wait_ge(S("bu_loaded"), 16)
            gp.wait_ge(S("ln_normalised"), TILES)
            for u in range(2):
                t8 = T[:, 8 * u:8 * u + 8, :]
                gp.tensor_tensor(t8, t8, bu[:].unsqueeze(1).broadcast_to([P, 8, C]),
                                 ALU.add).then_inc(S("t_biased"), 1)
            gp.sem_inc(S("heads_added"), 14)
            with gp.Fori(0, J) as j:
                for g in range(G):
                    for m in range(HEADS // 2):
                        k = g * (HEADS // 2) + m
                        gp.wait_ge(S("o_normalised"), j * 8 + (8 + k + 1))
                        if m == 0:
                            gp.wait_ge(S("stream_added"), j * 2 + (g + 1))
                            gp.tensor_tensor(acc[:, g], onorm[:, k % 2, :, 0, :], onorm[:, k % 2, :, 1, :],
                                             ALU.add).then_inc(S("heads_added"), 1)
                            continue
                        for h in range(2):
                            gp.wait_ge(S("heads_added"), j * 14 + (14 + 7 * g + 2 * m - 1 + h))
                            gp.tensor_tensor(acc[:, g], acc[:, g], onorm[:, k % 2, :, h, :],
                                             ALU.add).then_inc(S("heads_added"), 1)

            ffn(gp, 2)
            l3_pool(gp)
            ffn(gp, 3)

        def ln_act(act, n):
            act.wait_ge(S("ln_var"), n + 1)
            act.activation(lnc[:, 6, :], lnc[:, 5, :], ACT.Sqrt).then_inc(S("ln_std"), 1)
            for p in range(4):
                act.wait_ge(S("ln_transposed"), 4 * n + p + 1)
                act.activation(XS[:, p * 512:(p + 1) * 512], ps[:, p, :],
                               ACT.Copy).then_inc(S("ln_high"), 1)

        def gate_act(act, n):
            experts = (EXP2, EXP3)[n]
            act.wait_ge(S("gate_shifted"), n + 1)
            act.activation(gexp[:, :, 0:experts], logit[:, :, 0:experts],
                           ACT.Exp).then_inc(S("gate_exp"), 1)

        def attention_act(act):
            act.wait_ge(S("vproj_ones"), 1)
            act.sem_inc(S("probs_ready"), 16)
            act.sem_inc(S("kh_ready"), 8)
            act.sem_inc(S("pT_even"), 8)
            with act.Fori(0, J) as j:
                for t in range(4):
                    act.wait_ge(S("v_projected"), j * 4 + (t + 1))
                    act.wait_ge(S("pv_done"), j * 16 + 16)
                    act.activation(vproj[:, t, :, 0:C], ps[:, 3 + t, :].rearrange("p (h c) -> p h c", c=C),
                                   ACT.Copy).then_inc(S("v_ready"), 1)

                def key_high(k):
                    act.wait_ge(S("k_projected"), j * 8 + (k + 1))
                    act.wait_ge(S("scores_ready"), j * 16 + (16 + 2 * k - 2))
                    act.activation(KH[:, k % 2].rearrange("p h n -> p (h n)"), ps[:, 0, :],
                                   ACT.Copy).then_inc(S("kh_ready"), 1)

                key_high(0)
                for n in range(16):
                    if n % 2 == 0 and n // 2 + 1 < 8:
                        key_high(n // 2 + 1)
                    act.wait_ge(S("max_ready"), j * 16 + (n + 1))
                    act.wait_ge(S("p_transposed"), j * 16 + (16 + n - 1))
                    for u in range(U):
                        ins = act.activation(prob[:, n % 2, u, :],
                                             ps[:, 1 + n % 2, u * N:(u + 1) * N], ACT.Exp,
                                             bias=negmax[:, n % 4, u:u + 1])
                    ins.then_inc(S("probs_ready"), 1)
                    if n >= 2 and n % 2 == 0:
                        pT_copy(act, j, n - 2)
                pT_copy(act, j, 14)

        def pT_copy(eng, j, n):
            eng.wait_ge(S("p_transposed"), j * 16 + (16 + n + 1))
            eng.wait_ge(S("pv_done"), j * 16 + (16 + n - 1))
            dst = pT[:, n % 2].rearrange("p u n -> p (u n)")
            src = ps[:, 3 + n % 2, :]
            if n % 2 == 0:
                eng.activation(dst, src, ACT.Copy).then_inc(S("pT_even"), 1)
            else:
                eng.tensor_copy(dst, src).then_inc(S("pT_odd"), 1)

        @block.scalar
        def _(act):
            act.wait_ge(S("vec_loaded"), 16)
            for p in range(4):
                act.wait_ge(S("l0_projected"), p + 1)
                act.activation(theta[:, 2 * p:2 * p + 2, :].rearrange("p a n -> p (a n)"),
                               ps[2 * IC:3 * IC, p, :], ACT.Identity,
                               bias=vec[2 * IC:3 * IC, 0:1]).then_inc(S("theta_ready"), 1)
            act.wait_ge(S("l1_loaded"), 64)
            act.wait_ge(S("pads_zeroed"), 3)
            for g in range(G):
                h = slice(C * g, C * g + C)
                act.activation(w3s[h, :, h], w3T[h], ACT.Sign).then_inc(S("wsign_ready"), 1)
                act.activation(w1s[h, h], w1T[h], ACT.Sign).then_inc(S("wsign_ready"), 1)
            act.wait_ge(S("folded"), 1)
            for d in range(2):
                act.activation(AH[:, :, d, :], ps[:, 7, :].rearrange("p (h c) -> p h c", c=C), ACT.Copy,
                               scale=1.0 / math.sqrt(C)).then_inc(S("fold_high"), 1)
            act.wait_ge(S("folded"), 2)
            act.activation(GH[:], ps[:, 6, :], ACT.Copy).then_inc(S("fold_high"), 1)
            act.wait_ge(S("f_shifted"), 1)
            act.activation(f_exp[:], f_sub[:], ACT.Exp).then_inc(S("f_exp_ready"), 1)
            for p in range(2):
                act.wait_ge(S("f_transposed"), p + 1)
                act.activation(probT[:, p * 512:(p + 1) * 512], ps[0:C, p, :],
                               ACT.Copy).then_inc(S("probT_act"), 1)
            for p in range(2):
                act.wait_ge(S("wy_ready"), p + 1)
                act.activation(wy[:, p * 512:(p + 1) * 512], ps[:, 4 + p, :], ACT.Identity,
                               bias=v_("bw")).then_inc(S("wy_evac"), 1)
            act.wait_ge(S("bn_var_ready"), 1)
            act.activation(col[:, 11:14], col[:, 8:11], ACT.Sqrt).then_inc(S("bn_std_ready"), 1)
            for p in range(2):
                act.wait_ge(S("x1_ready"), p + 1)
                act.activation(sgn[:, 2 * p:2 * p + 2, 1:1 + IMG, 1:1 + IMG],
                               x1[:, p * 512:(p + 1) * 512].rearrange("p (j h w) -> p j h w", j=2, h=IMG),
                               ACT.Sign, bias=v_("b11")).then_inc(S("sgn_ready"), 1)
            for p in range(2):
                act.wait_ge(S("r1_ready"), p + 1)
                act.activation(sgn2[:, p * 512:(p + 1) * 512], r1[:, p * 512:(p + 1) * 512],
                               ACT.Sign, bias=v_("b21")).then_inc(S("sgn2_ready"), 1)
            act.wait_ge(S("x2_transposed"), 1)
            act.activation(T[:, 0:8, :].rearrange("p t c -> p (t c)"), ps[:, 4, :],
                           ACT.Copy).then_inc(S("T_act"), 1)
            ln_act(act, 0)
            attention_act(act)
            ln_act(act, 1)
            gate_act(act, 0)
            act.sem_inc(S("f2_hid_ready"), 8)
            with act.Fori(0, EXP2 // 2) as i:
                for e in range(2):
                    for c in range(CHUNKS):
                        k = CHUNKS * e + c
                        act.wait_ge(S("f2_h_ready"), i * 8 + (8 + k + 1))
                        act.wait_ge(S("f2_out_chunk"), i * 8 + (8 + k - 1))
                        act.wait_ge(S(f"f2_raw{e}"), i * 16 + 16)
                        act.activation(hid[:, c % 2, :], ps[:, c % 2, :], ACT.Gelu,
                                       bias=raw2[:, e, HID + C:HID + C + 1]).then_inc(S("f2_hid_ready"), 1)
            ln_act(act, 2)
            for q in range(0, TILES, 2):
                act.wait_ge(S("qkv_ready"), q // 2 + 1)
                z = ps[:, q // 2, 0:384].rearrange("p (g c) -> p g c", g=2)
                act.activation(QK[:, :, q:q + 2].rearrange("p a t h c -> p t a (h c)"),
                               z[:, :, 0:P].rearrange("p g (a c) -> p g a c", a=2),
                               ACT.Copy).then_inc(S("qk_evac"), 1)
                act.activation(V3[:, q:q + 2, :], z[:, :, P:192], ACT.Copy).then_inc(S("qk_evac"), 1)
            for half, (ready, dst) in enumerate((("r1h_ready", m_a), ("r2h_ready", m_c))):
                act.wait_ge(S(ready), 1)
                act.activation(dst[:], R[:, half].rearrange("p t h c -> p (t h c)"),
                               ACT.Square).then_inc(S("rsq_ready"), 1)
            act.wait_ge(S("n2_ready"), 1)
            act.activation(n2[:, 1, :], n2[:, 0, :], ACT.Sqrt).then_inc(S("norm_ready"), 1)
            act.wait_ge(S("qk8_ready"), 1)
            act.activation(q8[:], ps[0:C, 0, 0:64].rearrange("p (b n) -> p b n", n=NB),
                           ACT.Copy).then_inc(S("qk8_evac"), 1)
            act.activation(k8[:], ps[C:P, 0, 0:64].rearrange("p (b n) -> p b n", n=NB),
                           ACT.Copy).then_inc(S("qk8_evac"), 1)
            act.wait_ge(S("F8_ready"), 1)
            act.activation(F8[:], ps[0:NB, 1, 0:64], ACT.Copy).then_inc(S("F8_evac"), 1)
            act.wait_ge(S("vsum_ready"), 1)
            act.activation(vsum[:].rearrange("p b c -> p (b c)"), ps[0:NB, 3, :], ACT.Copy).then_inc(S("vsum_evac"), 1)
            act.wait_ge(S("a_var_ready"), 1)
            act.activation(s9[:, 3], s9[:, 2], ACT.Sqrt).then_inc(S("a_std_ready"), 1)
            act.wait_ge(S("z_ready"), 1)
            act.activation(e9[:], z9[:], ACT.Exp).then_inc(S("e9_ready"), 1)
            for p in range(2):
                act.wait_ge(S("p8T_ready"), p + 1)
                act.activation(p8T[:, p * 512:(p + 1) * 512], ps[0:NB, 4 + p, :],
                               ACT.Copy).then_inc(S("p8T_act"), 1)
            ln_act(act, 3)
            gate_act(act, 1)
            with act.Fori(0, EXP3 // 2) as i:
                for k in range(2 * CHUNKS):
                    act.wait_ge(S("f3_h_ready"), i * 8 + (8 + k + 1))
                    act.wait_ge(S("f3_hid_ready"), i * 8 + (8 + k - 1))
                    act.activation(silu[:, k % 2, :], ps[:, k % 2, :],
                                   ACT.Silu).then_inc(S("f3_silu_ready"), 1)
            act.wait_ge(S("out_transposed"), 1)
            act.activation(yfin[:, 0:512], ps[:, 0, :], ACT.Copy).then_inc(S("out_ready"), 1)

        def ln_pe(pe, n):
            for q in range(TILES):
                pe.wait_ge(S("ln_normalised"), TILES * n + q + 1)
                mm = pe.transpose(ps[:, q // 4, (q % 4) * P:(q % 4 + 1) * P],
                                  xn2[:, q].rearrange("p d c -> p (d c)"), ident)
                if q % 4 == 3:
                    mm.then_inc(S("ln_transposed"), 1)

        def gate_pe(pe, n):
            experts, parts = ((EXP2, gw2p), (EXP3, gw3p))[n]
            pe.wait_ge(S("gate_split"), 2)
            pe.wait_ge(S("ln_low"), 4 * (2 * n + 2))
            for q in range(TILES):
                for part in range(2):
                    mm = pe.matmul(ps[:, 4, q * experts:(q + 1) * experts], XS[:, q * P:(q + 1) * P],
                                   parts[:, part, :], start=(part == 0), stop=(part == 1))
            mm.then_inc(S("gate_logits"), 1)

        def attention_pe(pe):
            pe.wait_ge(S("fold_split"), 3)
            pe.wait_ge(S("nsx_ready"), 2)
            pe.sem_inc(S("scores_ready"), 16)
            pe.sem_inc(S("p_transposed"), 16)
            pe.sem_inc(S("pv_done"), 16)
            with pe.Fori(0, J) as j:
                def value(t):
                    if t < 2:
                        pe.wait_ge(S(("pT_even", "pT_odd")[t]), j * 8 + 8)
                    else:
                        pe.wait_ge(S("o_normalised"), j * 8 + (8 - 1 + t - 2))
                    pe.matmul(ps[:, 3 + t, :], xcur[:, t, :], GH[:], start=True, stop=False)
                    pe.matmul(ps[:, 3 + t, :], xcur[:, t, :], GL[:], start=False,
                              stop=True).then_inc(S("v_projected"), 1)

                def keys(k):
                    g, m = k // 4, k % 4
                    pe.wait_ge(S("kl_ready"), j * 8 + (8 + k))
                    pe.wait_ge(S("kh_ready"), j * 8 + (8 + k))
                    for h in range(2):
                        o = ps[:, 0, h * N:(h + 1) * N]
                        x = xcur[:, g::2, :]
                        pe.matmul(o, AH[:, 2 * m + h].rearrange("p d c -> p (d c)"), x, start=True, stop=False)
                        mm = pe.matmul(o, AL[:, 2 * m + h].rearrange("p d c -> p (d c)"), x, start=False, stop=True)
                    mm.then_inc(S("k_projected"), 1)

                def scores(n):
                    g, h, k = n // 8, n % 8, n // 2
                    if n % 2 == 0:
                        pe.wait_ge(S("kl_ready"), j * 8 + (8 + k + 1))
                    pe.wait_ge(S("probs_ready"), j * 16 + (16 + n - 1))
                    for u in range(U):
                        for part, K in enumerate((KH, KL)):
                            mm = pe.matmul(ps[:, 1 + n % 2, u * N:(u + 1) * N], xcur[:, 2 * u + g, :],
                                           K[:, k % 2, h % 2, :], start=(part == 0), stop=(part == 1))
                    mm.then_inc(S("scores_ready"), 1)

                def turn(n):
                    pe.wait_ge(S("probs_ready"), j * 16 + (16 + n + 1))
                    if n >= 2:
                        pe.wait_ge(S(("pT_even", "pT_odd")[n % 2]), j * 8 + (8 + n // 2))
                    else:
                        pe.wait_ge(S("v_ready"), j * 4 + (n + 1))
                    for su in range(U):
                        for u in range(U):
                            mm = pe.transpose(ps[:, 3 + n % 2, su * N + u * P:su * N + (u + 1) * P],
                                              prob[:, n % 2, u, su * P:(su + 1) * P], ident)
                    mm.then_inc(S("p_transposed"), 1)

                def product(n):
                    g, h, k = n // 8, n % 8, n // 2
                    pe.wait_ge(S(("pT_even", "pT_odd")[n % 2]), j * 8 + (8 + n // 2 + 1))
                    if n % 2 == 0:
                        if k >= 2:
                            pe.wait_ge(S("o_normalised"), j * 8 + (8 + k - 1))
                        else:
                            pe.wait_ge(S("v_ready"), j * 4 + 4)
                    for u in range(U):
                        o = ps[:, 5 + k % 2, (u * 2 + h % 2) * 65:(u * 2 + h % 2 + 1) * 65]
                        for su in range(U):
                            mm = pe.matmul(o, pT[:, n % 2, su, u * P:(u + 1) * P],
                                           vproj[:, 2 * su + g, h, :], start=(su == 0), stop=(su == 1))
                    mm.then_inc(S("pv_done"), 1)

                def newton(s):
                    pe.wait_ge(S("nsx_ready"), j * NS_PER_BATCH + (s + 2))
                    pe.matmul(ps[:, 7, 0:C], nsAT[:].rearrange("p a c -> p (a c)"), nsX[:, 1, :], start=True,
                              stop=True).then_inc(S("ns_ax"), 1)

                def newton_b(s):
                    pe.wait_ge(S("nsy_ready"), j * NS_PER_BATCH + (s + 1))
                    pe.matmul(ps[:, 7, 2 * C:3 * C], nsX[:].rearrange("p a c -> p (a c)"), nsY[:],
                              start=True, stop=True)
                    pe.matmul(ps[0:C, 7, C:2 * C], nsY[:], nsX[:, 0, :], start=True,
                              stop=True).then_inc(S("ns_xy"), 1)

                pe.wait_ge(S("xcur_ready"), j + 1)
                keys(0)
                for t in range(4):
                    value(t)
                for n in range(16 + 3):
                    if n < 16:
                        scores(n)
                    if n % 2 == 0 and n // 2 + 1 < 8:
                        keys(n // 2 + 1)
                    if n < NS_PER_BATCH:
                        newton(n)
                    if 2 <= n < 18:
                        turn(n - 2)
                    if n < NS_PER_BATCH:
                        newton_b(n)
                    if n >= 3:
                        product(n - 3)

        def ffn_pe(pe, which):
            experts, parts, raw, at = {2: (EXP2, [wp1], raw2, HID), 3: (EXP3, [wp1, wp2], raw3, 2 * HID)}[which]
            nm = f"f{which}_"
            nw = len(parts)
            if which == 2:
                pe.wait_ge(S("ln_low"), 8)
            pe.sem_inc(S(nm + "h_ready"), 8)
            with pe.Fori(0, experts // 2) as i:
                def hidden(k):
                    e, c = k // CHUNKS, k % CHUNKS
                    if c == 0:
                        pe.wait_ge(S(nm + "w_split"), i * (2 * nw) + (nw * (e + 1)))
                    pe.wait_ge(S(nm + "hid_ready"), i * 8 + (8 + k - 1))
                    for w, part in enumerate(parts):
                        for s in range(2):
                            mm = pe.matmul(ps[:, 2 * w + c % 2, :], part[:, e, s, :],
                                           XS[:, c * CHUNK:(c + 1) * CHUNK], start=(s == 0), stop=(s == 1))
                    mm.then_inc(S(nm + "h_ready"), 1)

                def output(k):
                    e, c = k // CHUNKS, k % CHUNKS
                    half = c // 2
                    pe.wait_ge(S(nm + "hid_ready"), i * 8 + (8 + k + 1))
                    if c % 2 == 0:
                        pe.wait_ge(S(nm + "y_weighted"), i * 4 + (2 * e + half + 1))
                    if c == 0:
                        pe.wait_ge(S(nm + f"raw{e}"), i * 16 + 16)
                    for t in range(CT):
                        q = (c % 2) * CT + t
                        w = raw[:, e, at:at + C]
                        mm = pe.matmul(ps[:, 4 + 2 * e + half, q * C:(q + 1) * C],
                                       hid[:, c % 2, t * P:(t + 1) * P], w, start=True, stop=True)
                    mm.then_inc(S(nm + "out_chunk"), 1)

                hidden(0)
                for k in range(8):
                    if k + 1 < 8:
                        hidden(k + 1)
                    output(k)

        def l3_pe(pe):
            pe.wait_ge(S("qkvw_ready"), 6)
            for q in range(TILES):
                if q % 2 == 0:
                    pe.wait_ge(S("ln_low"), 12)
                for part in range(2):
                    mm = pe.matmul(ps[:, q // 2, (q % 2) * 192:(q % 2 + 1) * 192], XS[:, q * P:(q + 1) * P],
                                   qkvw[:, part, :], start=(part == 0), stop=(part == 1))
                if q % 2 == 1:
                    mm.then_inc(S("qkv_ready"), 1)
            pe.wait_ge(S("qk_evac"), 16)
            for u in range(U):
                mm = pe.matmul(ps[0:NB, 3, :], con("inblock")[:, u * NB:(u + 1) * NB],
                               V3[:].rearrange("p (j u g) c -> p j u (g c)", j=J, u=U)[:, :, u, :],
                               start=(u == 0), stop=(u == 1))
            mm.then_inc(S("vsum_ready"), 1)
            for p in range(2):
                pe.matmul(ps[:, 6 + p, :], con("lower"), V3[:, 8 * p:8 * p + 8, :].rearrange("p t c -> p (t c)"),
                          start=True, stop=True).then_inc(S("prefix_ready"), 1)
            pe.wait_ge(S("rn_ready"), 2)
            for j in range(J):
                for g in range(G):
                    b = 2 * j + g
                    for u in range(U):
                        mm = pe.matmul(ps[:, 0, b * NB:(b + 1) * NB],
                                       RN[:, 4 * j + 2 * u + g].rearrange("p h a c -> p (h a c)"),
                                       con("basis")[:, u * NB:(u + 1) * NB], start=(u == 0), stop=(u == 1))
            mm.then_inc(S("qk8_ready"), 1)
            pe.wait_ge(S("qk8_evac"), 2)
            for b in range(B):
                mm = pe.matmul(ps[0:NB, 1, b * NB:(b + 1) * NB], q8[:, b, :], k8[:, b, :],
                               start=True, stop=True)
            mm.then_inc(S("F8_ready"), 1)
            pe.wait_ge(S("F8_evac"), 1)
            for u in range(U):
                mm = pe.matmul(ps[:, 2, u * 64:(u + 1) * 64], con("expand")[0:NB, u * P:(u + 1) * P],
                               F8[:], start=True, stop=True)
            mm.then_inc(S("far_ready"), 1)
            pe.wait_ge(S("p8_ready"), 1)
            for t in range(TILES):
                u, b = t // B, t % B
                bank = (4, 5, 0, 1)[t // 4]
                mm = pe.transpose(ps[0:NB, bank, (t % 4) * P:(t % 4 + 1) * P], p8[:, u, b, :], ident)
                if t % 4 == 3:
                    mm.then_inc(S("p8T_ready"), 1)
            pe.wait_ge(S("p8T_act"), 2)
            pe.wait_ge(S("p8T_vec"), 2)
            pe.wait_ge(S("vsum_evac"), 1)
            for q, (j, u, g) in enumerate(qs):
                t = u * B + 2 * j + g
                mm = pe.matmul(ps[:, 4 + q // 8, (q % 8) * C:(q % 8 + 1) * C], p8T[:, t * P:(t + 1) * P],
                               vsum[:, 2 * j + g, :], start=True, stop=True)
            mm.then_inc(S("yfar_ready"), 1)

        @block.tensor
        def _(pe):
            pe.wait_ge(S("l0_loaded"), 32)
            for p in range(4):
                g, jj = p // 2, p % 2
                h = slice(C * g, C * g + C)
                pe.matmul(ps[0:96, p, :], w0[h, :], x0[h, jj * 512:(jj + 1) * 512],
                          start=True, stop=True).then_inc(S("l0_projected"), 1)
            pe.wait_ge(S("attn_loaded"), 64)
            for h in range(HEADS):
                mm = pe.matmul(ps[:, 7, h * C:(h + 1) * C], wkT[:, h, :], wqT[:, h, :],
                               start=True, stop=True)
            mm.then_inc(S("folded"), 1)
            for h in range(HEADS):
                mm = pe.matmul(ps[:, 6, h * C:(h + 1) * C], wvT[:, h, :], wu[:, h, :],
                               start=True, stop=True)
            mm.then_inc(S("folded"), 1)
            pe.wait_ge(S("pg_ready"), 1)
            pe.wait_ge(S("ww_loaded"), 16)
            for b in range(B):
                mm = pe.matmul(ps[0:C, 4, b * C:(b + 1) * C], pg[IC:2 * IC, b, :], wwT[IC:2 * IC, :],
                               start=True, stop=True)
            mm.then_inc(S("gw_done"), 1)
            pe.wait_ge(S("theta_ready"), 4)
            pe.wait_ge(S("fold_split"), 3)
            for b in range(B):
                for u in range(U):
                    t = b * U + u
                    mm = pe.matmul(ps[:, 5 + t // 8, (t % 8) * C:(t % 8 + 1) * C],
                                   theta[:, b, u * P:(u + 1) * P], pg[0:IC, b, :], start=True, stop=True)
            mm.then_inc(S("f_ready"), 1)
            pe.wait_ge(S("l3_loaded"), 48)
            pe.matmul(ps[:, 7, 0:C], wv3[:], wo3T[:], start=True, stop=True).then_inc(S("vo_done"), 1)
            pe.wait_ge(S("ones_ready"), 1)
            pe.wait_ge(S("ns_sq_ready"), 1)
            pe.matmul(ps[0:C, 7, C:C + 1], ones64[:], nsc[:, 0:1], start=True,
                      stop=True).then_inc(S("ns_norm_done"), 1)
            pe.wait_ge(S("consts_loaded"), 16)
            pe.wait_ge(S("f_prob_ready"), 1)
            for t in range(TILES):
                mm = pe.transpose(ps[0:C, t // 4, (t % 4) * P:(t % 4 + 1) * P], f_prob[:, t, :], ident)
                if t % 4 == 3:
                    mm.then_inc(S("f_transposed"), 1)
            pe.wait_ge(S("gw_evac"), 1)
            pe.wait_ge(S("probT_act"), 2)
            pe.wait_ge(S("probT_vec"), 2)
            for p in range(2):
                for jj in range(2):
                    for g in range(G):
                        b = 4 * g + 2 * p + jj
                        mm = pe.matmul(ps[C * g:C * g + C, 4 + p, jj * N:(jj + 1) * N], gw[:, b, :],
                                       probT[:, b * N:(b + 1) * N], start=True, stop=True)
                mm.then_inc(S("wy_ready"), 1)
            pe.wait_ge(S("bn_mean_half"), 1)
            pe.matmul(ps[:, 6, 0:1], con("halfavg"), col[:, 0:1], start=True,
                      stop=True).then_inc(S("bn_mu_done"), 1)
            pe.wait_ge(S("bn_var_half"), 1)
            pe.matmul(ps[:, 6, 1:2], con("halfavg"), col[:, 4:5], start=True,
                      stop=True).then_inc(S("bn_var_done"), 1)
            pe.wait_ge(S("wsign_ready"), 4)
            for p in range(2):
                pe.wait_ge(S("sgn_ready"), p + 1)
                for k in range(9):
                    mm = pe.matmul(ps[:, p, :], w3s[:, k, :],
                                   sgn[:, 2 * p:2 * p + 2, k // 3:k // 3 + IMG, k % 3:k % 3 + IMG],
                                   start=(k == 0), stop=(k == 8))
                mm.then_inc(S("conv3_ready"), 1)
            for p in range(2):
                pe.wait_ge(S("sgn2_ready"), p + 1)
                pe.matmul(ps[:, 2 + p, :], w1s[:], sgn2[:, p * 512:(p + 1) * 512], start=True,
                          stop=True).then_inc(S("conv1_ready"), 1)
            for p in range(2):
                pe.wait_ge(S("x2_ready"), p + 1)
                for t in range(4 * p, 4 * p + 4):
                    mm = pe.transpose(ps[:, 4 + p, (t % 4) * P:(t % 4 + 1) * P],
                                      x2[:, t * P:(t + 1) * P], ident)
                mm.then_inc(S("x2_transposed"), 1)
            ln_pe(pe, 0)
            attention_pe(pe)
            pe.wait_ge(S("nsx_ready"), J * NS_PER_BATCH + 2)
            pe.matmul(ps[:, 7, 0:C], eyedup[:], nsX[:, 0, :], start=True, stop=True).then_inc(S("pinv_done"), 1)
            ln_pe(pe, 1)
            gate_pe(pe, 0)
            pe.wait_ge(S("cw2_ready"), 1)
            pe.transpose(ps[:, 1, 0:P], cw2[:].rearrange("p t e -> p (t e)"), ident).then_inc(S("cwT_done"), 1)
            pe.wait_ge(S("cwT_evac"), 1)
            pe.wait_ge(S("b2_loaded"), 16 * TILES)
            for p in range(2):
                pe.matmul(ps[:, 2 + p, :], cwT[:], b2blk[:, 8 * p:8 * p + 8, :].rearrange("p t c -> p (t c)"),
                          start=True, stop=True).then_inc(S("b2_done"), 1)
            pe.wait_ge(S("f2_base_ready"), 2)
            ffn_pe(pe, 2)
            ln_pe(pe, 2)
            l3_pe(pe)
            ln_pe(pe, 3)
            gate_pe(pe, 1)
            pe.wait_ge(S("f3_base_ready"), 2)
            ffn_pe(pe, 3)
            pe.wait_ge(S("f3_added"), 3 + 2 * EXP3)
            for p in range(2):
                for t in range(4):
                    q = 8 * p + 2 * t
                    mm = pe.transpose(ps[:, p, t * P:(t + 1) * P],
                                      T[:, q:q + 2, :].rearrange("p g c -> p (g c)"), ident)
                mm.then_inc(S("out_transposed"), 1)

        def l3_vector(dve, step, tt, ts, stt):
            dve.wait_ge(S("qk_evac"), 16)
            q1 = QK[:, 0].rearrange("p (j r) h c -> p j (r h c)", j=J)
            q2 = QK[:, 1].rearrange("p (j r) h c -> p j (r h c)", j=J)
            cos = con("cos").unsqueeze(1).broadcast_to([P, J, 256])

            def by_j(a):
                return a.rearrange("p (j r) -> p j r", j=J)
            r_1 = R[:, 0].rearrange("p t h c -> p (t h c)")
            r_2 = R[:, 1].rearrange("p t h c -> p (t h c)")
            step(tt(by_j(m_a[:]), q1, cos, ALU.mult))
            step(tt(by_j(m_d[:]), q2, cos, ALU.mult))
            dve.wait_ge(S("rope_pool"), 1)
            tt(r_1, m_a[:], m_b[:], ALU.subtract).then_inc(S("r1h_ready"), 1)
            dve.wait_ge(S("rope_pool"), 2)
            tt(r_2, m_c[:], m_d[:], ALU.add).then_inc(S("r2h_ready"), 1)
            dve.wait_ge(S("rsq_ready"), 2)
            step(tt(m_b[:], m_a[:], m_c[:], ALU.add))
            dve.tensor_reduce(n2[:, 0, :], m_b[:].rearrange("p (r c) -> p r c", c=32), AX.X,
                              ALU.add).then_inc(S("n2_ready"), 1)
            dve.wait_ge(S("norm_ready"), 1)
            step(ts(n2[:, 2, :], n2[:, 1, :], EPS_L2, None, ALU.add))
            step(dve.reciprocal(n2[:, 0, :], n2[:, 2, :]))
            for half in range(2):
                tt(RN[:, :, :, half, :].rearrange("p t h c -> p (t h) c"), R[:, half].rearrange("p t h c -> p (t h) c"),
                   n2[:, 0, :].unsqueeze(2).broadcast_to([P, 2 * TILES, 32]),
                   ALU.mult).then_inc(S("rn_ready"), 1)
            dve.wait_ge(S("rn_ready"), 2)
            step(tt(m_a[:].rearrange("p (t c) -> p t c", c=C), RN[:, :, 0].rearrange("p t a c -> p t (a c)"),
                    RN[:, :, 1].rearrange("p t a c -> p t (a c)"), ALU.mult))
            step(dve.tensor_reduce(dcol[:], m_a[:].rearrange("p (t c) -> p t c", c=C), AX.X, ALU.add))

            def table(name):
                return con(name).rearrange("p (u n) -> p u n", u=U).unsqueeze(2).broadcast_to([P, U, B, 9])
            def of_u(a, u):
                return a.rearrange("p (j u g) -> p j u g", j=J, u=U)[:, :, u, :]
            for u in range(U):
                step(ts(a9[:, u, :, NB].rearrange("p (j g) -> p j g", g=G), of_u(dcol[:], u),
                        con("scale")[:, u:u + 1], None, ALU.mult))
            dve.wait_ge(S("far_ready"), 1)
            for u in range(U):
                step(ts(a9[:, u, :, 0:NB], ps[:, 2, u * 64:(u + 1) * 64].rearrange("p (b n) -> p b n", n=NB),
                        con("scale")[:, u:u + 1], None, ALU.mult))

            def over(c):
                return c.unsqueeze(3).broadcast_to([P, U, B, 9])
            step(tt(t9[:], a9[:], table("count"), ALU.mult))
            step(dve.tensor_reduce(s9[:, 0], t9[:], AX.X, ALU.add))
            for u in range(U):
                step(ts(s9[:, 1, u], s9[:, 0, u], con("invn")[:, u:u + 1], None, ALU.mult))
            step(tt(z9[:], a9[:], over(s9[:, 1]), ALU.subtract))
            step(tt(t9[:], z9[:], z9[:], ALU.mult))
            step(tt(t9[:], t9[:], table("count"), ALU.mult))
            step(dve.tensor_reduce(s9[:, 0], t9[:], AX.X, ALU.add))
            for u in range(U):
                ins = ts(s9[:, 2, u], s9[:, 0, u], con("invn")[:, u:u + 1], EPS_VAR, ALU.mult, ALU.max)
                ins.then_inc(S("a_var_half"), 1)
            dve.wait_ge(S("a_var_half"), 2)
            dve.nop().then_inc(S("a_var_ready"), 1)
            dve.wait_ge(S("a_std_ready"), 1)
            step(dve.reciprocal(s9[:, 4], s9[:, 3]))
            step(tt(z9[:], z9[:], over(s9[:, 4]), ALU.mult))
            step(tt(z9[:], z9[:], table("mask"), ALU.add))
            step(dve.tensor_reduce(s9[:, 5], z9[:], AX.X, ALU.max))
            tt(z9[:], z9[:], over(s9[:, 5]), ALU.subtract).then_inc(S("z_ready"), 1)
            dve.wait_ge(S("e9_ready"), 1)
            step(tt(t9[:], e9[:], table("count"), ALU.mult))
            step(dve.tensor_reduce(s9[:, 6], t9[:], AX.X, ALU.add))
            step(dve.reciprocal(s9[:, 7], s9[:, 6]))
            step(tt(e9[:], e9[:], over(s9[:, 7]), ALU.mult))

            def blocks(name):
                return con(name).rearrange("p (u n) -> p u n", u=U).unsqueeze(2).broadcast_to([P, U, B, NB])
            tt(p8[:], e9[:, :, :, 0:NB], blocks("below"), ALU.mult).then_inc(S("p8_ready"), 1)
            for u in range(U):
                ins = dve.tensor_copy(of_u(pdia[:], u), e9[:, u, :, NB].rearrange("p (j g) -> p j g", g=G))
                step(ins)
            dve.nop().then_inc(S("pdia_ready"), 1)
            step(tt(t9[:, :, :, 0:NB], e9[:, :, :, 0:NB], blocks("own"), ALU.mult))
            for u in range(U):
                step(dve.tensor_reduce(of_u(pown[:], u), t9[:, u, :, 0:NB].rearrange("p (j g) n -> p j g n", g=G),
                                       AX.X, ALU.add))
            for p in range(2, 4):
                dve.wait_ge(S("p8T_ready"), p + 1)
                dve.tensor_copy(p8T[:, p * 512:(p + 1) * 512], ps[0:NB, p - 2, :]).then_inc(S("p8T_vec"), 1)
            dve.wait_ge(S("prefix_ready"), 2)
            t = T[:].rearrange("p t c -> p (t c)")
            ma = m_a[:].rearrange("p (t c) -> p t c", c=C)
            step(tt(ma, ps[:, 6:8, :].rearrange("p a (t c) -> p (a t) c", c=C),
                    pown[:].unsqueeze(2).broadcast_to([P, TILES, C]), ALU.mult))
            step(tt(t, t, m_a[:], ALU.add))
            dve.wait_ge(S("yfar_ready"), 1)
            step(tt(t, t, ps[:, 4:6, :].rearrange("p a n -> p (a n)"), ALU.add))
            dve.wait_ge(S("diag_done"), 1)
            step(tt(t, t, m_d[:], ALU.add))

        @block.vector
        def _(dve):
            step = step_of(dve, "dve_step")
            tt, ts, stt = dve.tensor_tensor, dve.tensor_scalar, dve.scalar_tensor_tensor

            for p in range(4):
                dve.wait_ge(S("l0_projected"), p + 1)
                ins = dve.tensor_reduce(pooled[:, 2 * p:2 * p + 2, :].rearrange("p b n -> p (b n)")
                                        .rearrange("p (r w) -> p r w", w=IMG // 2),
                                        ps[0:2 * IC, p, :].rearrange("p (r a w b) -> p r w a b", a=2, b=2, w=IMG // 2),
                                        AX.XY, ALU.max)
            step(ins)
            dve.wait_ge(S("vec_loaded"), 16)
            ts(pg[:], pooled[:], vec[0:2 * IC, 0:1], None, ALU.add).then_inc(S("pg_ready"), 1)
            dve.wait_ge(S("fold_high"), 3)
            for d in range(2):
                stt(AL[:, :, d, :], ps[:, 7, :].rearrange("p (h c) -> p h c", c=C), 1.0 / math.sqrt(C),
                    AH[:, :, d, :].bitcast(F32), ALU.mult, ALU.subtract).then_inc(S("fold_split"), 1)
            tt(GL[:], ps[:, 6, :], GH[:].bitcast(F32), ALU.subtract).then_inc(S("fold_split"), 1)
            dve.wait_ge(S("gw_done"), 1)
            dve.tensor_copy(gw[:], ps[0:C, 4, :].rearrange("p (b c) -> p b c", c=C)).then_inc(S("gw_evac"), 1)
            dve.wait_ge(S("f_ready"), 1)
            f = ps[:, 5:7, :].rearrange("p a (t c) -> p (a t) c", c=POOLED)

            def wide(c, n=POOLED, t=TILES):
                return c.unsqueeze(2).broadcast_to([P, t, n])
            step(dve.tensor_reduce(f_col[:, 0, :], f, AX.X, ALU.max))
            tt(f_sub[:], f, wide(f_col[:, 0, :]), ALU.subtract).then_inc(S("f_shifted"), 1)
            dve.wait_ge(S("ns_loaded"), 32)
            step(dve.tensor_tensor_reduce(nsY[:], nsA[:], nsA[:], 1.0, 0.0, ALU.mult, ALU.add, nsc[:, 0:1]))
            dve.nop().then_inc(S("ns_sq_ready"), 1)
            dve.wait_ge(S("consts_loaded"), 16)
            step(ts(eye2[:], ident[0:C, 0:C], 2.0, None, ALU.mult))
            for d in range(2):
                step(dve.tensor_copy(eyedup[:, d * C:(d + 1) * C], ident[0:C, 0:C]))
            dve.wait_ge(S("f_exp_ready"), 1)
            step(dve.tensor_reduce(f_col[:, 1, :], f_exp[:], AX.X, ALU.add))
            step(dve.reciprocal(f_col[:, 2, :], f_col[:, 1, :]))
            tt(f_prob[:], f_exp[:], wide(f_col[:, 2, :]), ALU.mult).then_inc(S("f_prob_ready"), 1)
            dve.wait_ge(S("ns_norm_done"), 1)
            step(dve.reciprocal(nsc[:, 1:2], ps[0:C, 7, C:C + 1]))
            ts(nsX[:, 1, :], nsAT[:, 0, :], nsc[:, 1:2], None, ALU.mult).then_inc(S("nsx_ready"), 1)
            ts(nsX[:, 0, :], nsA[:], nsc[:, 1:2], None, ALU.mult).then_inc(S("nsx_ready"), 1)
            dve.wait_ge(S("vo_done"), 1)
            dve.wait_ge(S("l3_loaded"), 48)

            def query_or_key(part, h):
                return qkvw[:, part, 0:P].rearrange("p (a h c) -> p a h c", a=2, h=2)[:, :, h, :]
            split = [(query_or_key(0, 0), query_or_key(1, 0), wq3[:].rearrange("p (a c) -> p a c", a=2)),
                     (qkvw[:, 0, P:192], qkvw[:, 1, P:192], ps[:, 7, 0:C])]
            for high, low, raw in split:
                step(dve.tensor_copy(high, raw))
                tt(low, raw, high.bitcast(F32), ALU.subtract).then_inc(S("qkvw_ready"), 2)
            dve.wait_ge(S("l1_loaded"), 64)
            ones = [("w3n", w3n, 9 * C, 20), ("w1n", w1n, C, 21)]
            for _, w, n, c in ones:
                step(dve.tensor_reduce(col[:, c:c + 1], w[:], AX.X, ALU.add, apply_absolute_value=True))
            step(ts(col[:, 22:23], col[:, 20:21], 1.0 / (9 * C), None, ALU.mult))
            step(ts(col[:, 23:24], col[:, 21:22], 1.0 / C, None, ALU.mult))
            step(ts(col[:, 9:10], v_("v1"), EPS_BN, None, ALU.add))
            step(ts(col[:, 10:11], v_("v2"), EPS_BN, None, ALU.add))
            for p in range(2, 4):
                dve.wait_ge(S("f_transposed"), p + 1)
                dve.tensor_copy(probT[:, p * 512:(p + 1) * 512], ps[0:C, p, :]).then_inc(S("probT_vec"), 1)
            dve.wait_ge(S("wy_evac"), 2)
            for p in range(2):
                step(dve.bn_stats(bn6[:, p, :], wy[:, p * 512:(p + 1) * 512]))
            dve.bn_aggr(col[:, 0:2], bn6[:].rearrange("p a s -> p (a s)")).then_inc(S("bn_mean_half"), 1)
            dve.wait_ge(S("bn_mean_half"), 1)
            dve.wait_ge(S("bn_mu_done"), 1)
            step(dve.tensor_copy(col[:, 2:3], ps[:, 6, 0:1]))
            step(tt(col[:, 3:4], col[:, 0:1], col[:, 2:3], ALU.subtract))
            stt(col[:, 4:5], col[:, 3:4], col[:, 3:4], col[:, 1:2], ALU.mult, ALU.add).then_inc(S("bn_var_half"), 1)
            dve.wait_ge(S("bn_var_done"), 1)
            ts(col[:, 8:9], ps[:, 6, 1:2], EPS_BN, None, ALU.add).then_inc(S("bn_var_ready"), 1)
            dve.wait_ge(S("bn_std_ready"), 1)
            step(dve.reciprocal(col[:, 24:27], col[:, 11:14]))
            step(tt(col[:, 28:29], col[:, 24:25], v_("gamma"), ALU.mult))
            step(tt(col[:, 30:31], col[:, 28:29], col[:, 2:3], ALU.mult))
            step(tt(col[:, 29:30], v_("beta"), col[:, 30:31], ALU.subtract))
            dve.wait_ge(S("l0_loaded"), 32)
            for p in range(2):
                s = slice(p * 512, (p + 1) * 512)
                step(ts(va[:, s], wy[:, s], col[:, 28:29], col[:, 29:30], ALU.mult, ALU.add))
                tt(x1[:, s], va[:, s], x0[:, s], ALU.add).then_inc(S("x1_ready"), 1)
            for k, (g_, be, m_, b_) in enumerate((("g1", "be1", "m1", "b12"), ("g2", "be2", "m2", "b22"))):
                inv = col[:, 32 + k:33 + k]
                step(tt(inv, v_(g_), col[:, 25 + k:26 + k], ALU.mult))
                step(tt(col[:, 34 + k:35 + k], inv, col[:, 22 + k:23 + k], ALU.mult))
                step(tt(col[:, 38:39], inv, v_(m_), ALU.mult))
                step(tt(col[:, 39:40], v_(be), col[:, 38:39], ALU.subtract))
                step(tt(col[:, 36 + k:37 + k], col[:, 39:40], v_(b_), ALU.add))

            def prelu(dst, src, a, after, tmp):
                step(ts(tmp, src, 0.0, v_(a), ALU.min, ALU.mult))
                step(stt(dst, src, 0.0, tmp, ALU.max, ALU.add))
                return ts(dst, dst, v_(after), None, ALU.add)

            for bank, ready, k, src, dst, a, after, done in (
                    (0, "conv3_ready", 0, x1, r1, "a1", "b13", "r1_ready"),
                    (2, "conv1_ready", 1, r1, x2, "a2", "b23", "x2_ready")):
                for p in range(2):
                    s = slice(p * 512, (p + 1) * 512)
                    dve.wait_ge(S(ready), p + 1)
                    step(ts(va[:, s], ps[:, bank + p, :], col[:, 34 + k:35 + k], col[:, 36 + k:37 + k],
                            ALU.mult, ALU.add))
                    step(tt(vb[:, s], va[:, s], src[:, s], ALU.add))
                    prelu(dst[:, s], vb[:, s], a, after, va[:, s]).then_inc(S(done), 1)
                    dve.wait_ge(S(done), p + 1)
            dve.wait_ge(S("x2_transposed"), 2)
            dve.tensor_copy(T[:, 8:16, :].rearrange("p t c -> p (t c)"), ps[:, 5, :]).then_inc(S("T_vec"), 1)
            dve.wait_ge(S("T_act"), 1)
            dve.wait_ge(S("T_vec"), 1)

            def layer_norm(n):
                for q in range(TILES):
                    ins = dve.bn_stats(ln6[:, q, :], T[:, q, :])
                step(ins)
                me, mo = ln6[:, :, 1], ln6[:, :, 4]
                step(tt(lnc[:, 0, :], me, mo, ALU.add))
                step(tt(lnc[:, 1, :], me, mo, ALU.subtract))
                step(tt(lnc[:, 2, :], ln6[:, :, 2], ln6[:, :, 5], ALU.add))
                step(tt(lnc[:, 3, :], lnc[:, 1, :], lnc[:, 1, :], ALU.mult))
                step(stt(lnc[:, 4, :], lnc[:, 3, :], C / 4.0, lnc[:, 2, :], ALU.mult, ALU.add))
                step(ts(lnc[:, 1, :], lnc[:, 0, :], 0.5, None, ALU.mult))
                ts(lnc[:, 5, :], lnc[:, 4, :], 1.0 / C, EPS_LN, ALU.mult, ALU.add).then_inc(S("ln_var"), 1)
                dve.wait_ge(S("ln_std"), n + 1)
                step(dve.reciprocal(lnc[:, 7, :], lnc[:, 6, :]))
                for q in range(TILES):
                    ts(xn2[:, q], T[:, q, :].unsqueeze(1).broadcast_to([P, 2, C]), lnc[:, 1, q:q + 1],
                       lnc[:, 7, q:q + 1], ALU.subtract, ALU.mult).then_inc(S("ln_normalised"), 1)
                for p in range(4):
                    dve.wait_ge(S("ln_high"), 4 * n + p + 1)
                    low = XS[C:P, p * 512:(p + 1) * 512]
                    tt(low, ps[C:P, p, :], low.bitcast(F32), ALU.subtract).then_inc(S("ln_low"), 1)

            def gate(n):
                experts, gb = ((EXP2, gb2), (EXP3, gb3))[n]
                dve.wait_ge(S("gate_loaded"), 64)
                dve.wait_ge(S("gate_logits"), n + 1)
                lg, ge, gs = logit[:, :, 0:experts], gexp[:, :, 0:experts], gsel[:, :, 0:experts]
                step(tt(lg, ps[:, 4, 0:TILES * experts].rearrange("p (t e) -> p t e", e=experts),
                        gb[:].unsqueeze(1).broadcast_to([P, TILES, experts]), ALU.add))
                for q in range(TILES):
                    ins = dve.max(top8[:, q, :], lg[:, q, :])
                step(ins)
                step(tt(gs, lg, wide(top8[:, :, 1], experts), ALU.is_ge))
                tt(lg, lg, wide(top8[:, :, 0], experts), ALU.subtract).then_inc(S("gate_shifted"), 1)
                dve.wait_ge(S("gate_exp"), n + 1)
                step(tt(gs, ge, gs, ALU.mult))
                step(dve.tensor_reduce(gcol[:, 0, :], (ge, gs)[n], AX.X, ALU.add))
                step(dve.reciprocal(gcol[:, 1, :], gcol[:, 0, :]))
                step(tt(cw[:, 0:experts, :].rearrange("p e t -> p t e"), gs, wide(gcol[:, 1, :], experts), ALU.mult))

            layer_norm(0)
            dve.sem_inc(S("kl_ready"), 8)
            dve.sem_inc(S("pT_odd"), 8)
            dve.sem_inc(S("o_normalised"), 8)
            dve.sem_inc(S("stream_added"), 2)
            with dve.Fori(0, J) as j:
                dve.wait_ge(S("scores_ready"), j * 16 + 16)
                dve.wait_ge(S("ln_low"), 4)
                dve.tensor_copy(xcur[:].rearrange("p t n -> p (t n)").unsqueeze(1),
                                XS[:].bitcast(F32).rearrange("p (j n) -> p j n", j=J)[:, bass.ds(j, 1), :]
                                ).then_inc(S("xcur_ready"), 1)

                def key_low(k):
                    dve.wait_ge(S("kh_ready"), j * 8 + (8 + k + 1))
                    dve.wait_ge(S("scores_ready"), j * 16 + (16 + 2 * k - 2))
                    tt(KL[:, k % 2].rearrange("p h n -> p (h n)"), ps[:, 0, :],
                       KH[:, k % 2].rearrange("p h n -> p (h n)").bitcast(F32),
                       ALU.subtract).then_inc(S("kl_ready"), 1)

                def normalise(k):
                    dve.wait_ge(S("pv_done"), j * 16 + (16 + 2 * k + 2))
                    o = ps[:, 5 + k % 2, 0:260].rearrange("p (r c) -> p r c", c=C + 1)
                    dve.reciprocal(rsum[:, k % 2, :], o[:, :, C]).then_inc(S("rsum_ready"), 1)
                    dve.wait_ge(S("rsum_ready"), j * 8 + (k + 1))
                    dve.wait_ge(S("heads_added"), j * 14 + (14 + heads_added_after(k - 2)))
                    tt(onorm[:, k % 2].rearrange("p u h c -> p (u h) c"), o[:, :, 0:C],
                       rsum[:, k % 2, :].unsqueeze(2).broadcast_to([P, 4, C]),
                       ALU.mult).then_inc(S("o_normalised"), 1)

                key_low(0)
                for n in range(16 + 4):
                    if n % 2 == 0 and n // 2 + 1 < 8:
                        key_low(n // 2 + 1)
                    if n < 16:
                        dve.wait_ge(S("scores_ready"), j * 16 + (16 + n + 1))
                        dve.wait_ge(S("probs_ready"), j * 16 + (16 + n - 3))
                        dve.tensor_reduce(negmax[:, n % 4, :],
                                          ps[:, 1 + n % 2, :].rearrange("p (u n) -> p u n", u=U), AX.X, ALU.max,
                                          negate=True).then_inc(S("max_ready"), 1)
                    if n < NS_PER_BATCH:
                        dve.wait_ge(S("ns_ax"), j * NS_PER_BATCH + (n + 1))
                        tt(nsY[:], eye2[:], ps[0:C, 7, 0:C], ALU.subtract).then_inc(S("nsy_ready"), 1)
                    if n >= 2 and n % 2 == 1 and n - 2 < 16:
                        pT_copy(dve, j, n - 2)
                    if n < NS_PER_BATCH:
                        dve.wait_ge(S("ns_xy"), j * NS_PER_BATCH + (n + 1))
                        dve.tensor_copy(nsX[:].rearrange("p a c -> p (a c)"),
                                        ps[0:C, 7, C:3 * C]).then_inc(S("nsx_ready"), 1)
                    if n >= 4 and n % 2 == 0:
                        normalise((n - 4) // 2)
                    if n == 14 or n == 19:
                        g = n // 19
                        dve.wait_ge(S("t_biased"), 2)
                        dve.wait_ge(S("heads_added"), j * 14 + (14 + 7 * (g + 1)))
                        t = T[:].rearrange("p (j u g) c -> p j u g c", j=J, u=U)[:, bass.ds(j, 1), :, g, :]
                        tt(t, t, acc[:, g].unsqueeze(1), ALU.add).then_inc(S("stream_added"), 1)
            dve.wait_ge(S("pinv_done"), 1)
            raw = ps[:, 7, 0:C].rearrange("p (a c) -> p a c", a=2)
            step(dve.tensor_copy(query_or_key(0, 1), raw))
            tt(query_or_key(1, 1), raw, query_or_key(0, 1).bitcast(F32), ALU.subtract).then_inc(S("qkvw_ready"), 2)

            dve.wait_ge(S("stream_added"), 2 + 2 * J)
            layer_norm(1)
            gate(0)
            dve.tensor_copy(cw2[:], cw[:, 0:EXP2, :].rearrange("p e t -> p t e")).then_inc(S("cw2_ready"), 1)
            dve.wait_ge(S("cwT_done"), 1)
            dve.tensor_copy(cwT[:], ps[:, 1, 0:P]).then_inc(S("cwT_evac"), 1)
            for p in range(2):
                dve.wait_ge(S("b2_done"), p + 1)
                t = T[:, 8 * p:8 * p + 8, :].rearrange("p t c -> p (t c)")
                tt(t, ps[:, 2 + p, :], t, ALU.add).then_inc(S("f2_base_ready"), 1)

            def weigh(which, i, e, half):
                nm = f"f{which}_"
                dve.wait_ge(S(nm + "out_chunk"), i * 8 + (8 + 4 * e + 2 * half + 2))
                dve.wait_ge(S(nm + "added"), i * 4 + (2 * e + half + 2))
                weight = cw[:].rearrange("p (i e) t -> p i e t", e=2)[:, bass.ds(i, 1), e, 8 * half:8 * half + 8]
                tt(ytmp[:, half, :].rearrange("p (t c) -> p t c", c=C),
                   ps[:, 4 + 2 * e + half, :].rearrange("p (t c) -> p t c", c=C),
                   weight.rearrange("p i t -> p (i t)").unsqueeze(2).broadcast_to([P, 8, C]),
                   ALU.mult).then_inc(S(nm + "y_weighted"), 1)

            dve.memset(ytmp[:], 0.0).then_inc(S("ytmp_zeroed"), 1)
            dve.wait_ge(S("ytmp_zeroed"), 1)
            dve.sem_inc(S("f2_y_weighted"), 4)
            with dve.Fori(0, EXP2 // 2) as i:
                for e in range(2):
                    for half in range(2):
                        weigh(2, i, e, half)
            dve.wait_ge(S("f2_added"), 3 + 2 * EXP2)
            layer_norm(2)
            l3_vector(dve, step, tt, ts, stt)
            layer_norm(3)
            gate(1)
            dve.memset(ytmp[:], 0.0).then_inc(S("ytmp_zeroed"), 1)
            dve.wait_ge(S("ytmp_zeroed"), 2)
            dve.sem_inc(S("f3_base_ready"), 2)
            dve.sem_inc(S("f3_y_weighted"), 4)
            dve.sem_inc(S("f3_hid_ready"), 8)
            with dve.Fori(0, EXP3 // 2) as i:
                for e in range(2):
                    for c in range(CHUNKS):
                        k = CHUNKS * e + c
                        dve.wait_ge(S("f3_silu_ready"), i * 8 + (k + 1))
                        dve.wait_ge(S("f3_out_chunk"), i * 8 + (8 + k - 1))
                        tt(hid[:, c % 2, :], ps[:, 2 + c % 2, :], silu[:, c % 2, :],
                           ALU.mult).then_inc(S("f3_hid_ready"), 1)
                        if c % 2 == 1 and k > 1:
                            kk = k - 2
                            weigh(3, i, kk // CHUNKS, (kk % CHUNKS) // 2)
                weigh(3, i, 1, 1)
            dve.wait_ge(S("out_transposed"), 2)
            dve.tensor_copy(yfin[:, 512:1024], ps[:, 1, :]).then_inc(S("out_ready"), 1)

def kernel(**inputs):
    import concourse.bacc as bacc
    from concourse.bass_utils import run_bass_kernel_spmd

    a = {k: np.asarray(v) for k, v in inputs.items()}

    def twice(m):
        return np.concatenate([m, m], axis=0)

    def rows(v):
        return np.broadcast_to(v[None, :], (P, v.shape[0]))

    vec = {"bw": a["L0_conv_bw"], "gamma": a["L0_conv_gamma"], "beta": a["L0_conv_beta"]}
    vec.update({n: a["L1_conv_" + n] for n in VECS if n not in vec and n != "bpg_bt"})
    cols = [np.concatenate([a["L0_conv_bp"], a["L0_conv_bg"], a["L0_conv_bt"], np.zeros(IC, np.float32)])]
    cols += [np.concatenate([vec[n], vec[n]]) for n in VECS[1:]]

    def by_head(w, dup):
        t = w.reshape(C, HEADS, C).transpose(2, 1, 0)
        return np.concatenate([t, t], axis=2) if dup else t

    w3, w1 = a["L1_conv_w3"], a["L1_conv_w1"]
    arrays = {
        "x": a["x"].reshape(G, J, C, N).transpose(0, 2, 1, 3).reshape(P, J * N),
        "w0": twice(np.concatenate([a["L0_conv_Wp"].T, a["L0_conv_Wg"].T, a["L0_conv_Wt"].T], axis=1)),
        "wwT": a["L0_conv_Ww"].T,
        "vec": np.stack(cols, axis=1),
        "w3T": twice(w3.transpose(1, 2, 3, 0).reshape(C, 9, C)),
        "w1T": twice(w1[:, :, 0, 0].T),
        "w3n": twice(w3.reshape(C, C * 9)),
        "w1n": twice(w1.reshape(C, C)),
        "wqT": by_head(a["L2_attn_Wq"], False),
        "wkT": by_head(a["L2_attn_Wk"], True),
        "wvT": by_head(a["L2_attn_Wv"], True),
        "wu": a["L2_attn_Wu"].reshape(HEADS, C, C).transpose(1, 0, 2),
        "bu": rows(a["L2_attn_bu"]),
        "q3": twice(a["L3_attn_W_Q"]),
        "q3T": np.concatenate([a["L3_attn_W_Q"].T] * 2, axis=1),
        "wv3": np.concatenate([a["L3_attn_W_V"]] * 2, axis=1),
        "wo3T": a["L3_attn_W_O"].T,
        "gw2": twice(a["L2_ffn_gate_w"]),
        "gb2": rows(a["L2_ffn_gate_b"]),
        "gw3": twice(a["L3_ffn_gate_w"]),
        "gb3": rows(a["L3_ffn_gate_b"]),
        "raw2": np.concatenate([np.concatenate([a["L2_ffn_W1"]] * 2, axis=1), a["L2_ffn_W2"],
                                a["L2_ffn_b1"][:, :, None]], axis=2).reshape(EXP2 * P, -1),
        "b2": a["L2_ffn_b2"],
        "raw3": np.concatenate([np.concatenate([a["L3_ffn_w1"]] * 2, axis=1),
                                np.concatenate([a["L3_ffn_w2"]] * 2, axis=1), a["L3_ffn_w3"]], axis=2).reshape(EXP3 * P, -1),
        "consts": constants(),
    }
    arrays = {k: np.ascontiguousarray(v) for k, v in arrays.items()}
    nc = bacc.Bacc("TRN2", target_bir_lowering=False, num_devices=1)
    io = {k: nc.dram_tensor(f"in_{k}", v.shape, mybir.dt.from_np(v.dtype), kind="ExternalInput").ap()
          for k, v in arrays.items()}
    out = nc.dram_tensor("out_y", (P, J * N), F32, kind="ExternalOutput").ap()
    hybrid_kernel(nc, io, out)
    r = run_bass_kernel_spmd(nc, [{f"in_{k}": v for k, v in arrays.items()}], core_ids=[0])
    y = r.results[0]["out_y"]
    return y.reshape(G, C, J, N).transpose(0, 2, 1, 3).reshape(B, C, IMG, IMG)
```

```python
from contextlib import ExitStack
import math

import numpy as np

import concourse.bass as bass
from concourse import mybir

F32 = mybir.dt.float32
F32R = mybir.dt.float32r
BF16 = mybir.dt.bfloat16
ALU = mybir.AluOpType
ACT = mybir.ActivationFunctionType
AX = mybir.AxisListType

P = 128
B, C, IMG = 8, 64, 16
N = IMG * IMG
G, J, U = 2, B // 2, N // P
TILES = B * U
TOK = B * N
IC = 32
POOLED = N // 4
HEADS = 8
EXP2, EXP3, HID = 8, 16, 128
CHUNK = 512
CHUNKS = TOK // CHUNK
CT = CHUNK // P
BLK = 32
NB = N // BLK
LEVELS = 3
THETA = 10000.0
PAD = IMG + 2
EPS_BN, EPS_LN, EPS_VAR, EPS_L2 = 1e-5, 1e-5, 1e-6, 1e-8
PAIRS = G * HEADS // 2
NEWTON = (J - 1) * PAIRS
HIDDEN_SCORE = -30000.0

VECS = ["bpg_bt", "bw", "gamma", "beta", "b11", "b12", "b13", "b21", "b22", "b23",
        "g1", "be1", "m1", "v1", "g2", "be2", "m2", "v2", "a1", "a2"]
VI = {n: i for i, n in enumerate(VECS)}

CONSTS = [("ident", P), ("halfavg", P), ("cos", 256), ("sin", 256), ("lower", P), ("expand", U * P),
          ("basis", U * NB), ("inblock", U * P), ("own", U * NB), ("below", U * NB),
          ("count", U * 9), ("mask", U * 9), ("invn", U), ("scale", U), ("sameb", B), ("fold", C), ("newton", 2 * NEWTON)]
CO, _at = {}, 0
for _n, _w in CONSTS:
    CO[_n] = (_at, _w)
    _at += _w
NCONST = _at


def newton_scales():
    low = (10 * C * np.finfo(np.float32).eps) ** 2 / C
    scales = []
    for _ in range(NEWTON):
        scale = 2.0 / (1.0 + max(low, 1e-2)) if low < 0.9 else 1.0
        scales.append(scale)
        low = min(scale * v * (2.0 - scale * v) for v in (low, 1.0))
    assert low > 1 - 1e-7
    return np.array(scales)


def constants():
    out = np.zeros((P, NCONST), np.float32)

    def put(name, a):
        at, w = CO[name]
        a = np.asarray(a, np.float32)
        out[:a.shape[0], at:at + w] = a.reshape(a.shape[0], w)

    put("ident", np.eye(P))
    p = np.arange(P)
    put("halfavg", 0.5 * (p[:, None] % C == p[None, :] % C))
    half = C // 2
    inv_freq = 1.0 / THETA ** (np.arange(half, dtype=np.float32) / half)
    ang = np.arange(N, dtype=np.float32)[:, None] * inv_freq[None, :].astype(np.float32)

    def rope(t):
        t = t.astype(np.float32).reshape(U, P, 1, half).repeat(4, axis=2)
        return t.transpose(1, 0, 2, 3)
    put("cos", rope(np.cos(ang)))
    put("sin", rope(np.sin(ang)))
    put("lower", (p[:, None] // BLK == p[None, :] // BLK) & (p[:, None] < p[None, :]))
    tok = np.arange(N)
    blk = tok // BLK
    onehot = (blk[:, None] == np.arange(NB)[None, :]).astype(np.float32)
    put("expand", onehot.T)
    haar = []
    for level in range(LEVELS):
        size = N // 2 ** level
        for k in range(2 ** level):
            v = np.zeros(N)
            v[k * size:k * size + size // 2] = 1 / math.sqrt(size // 2)
            v[k * size + size // 2:(k + 1) * size] = -1 / math.sqrt(size // 2)
            haar.append(v)
    haar = np.stack(haar, 1)

    def by_tile(a):
        return np.asarray(a, np.float32).reshape(U, P, -1).transpose(1, 0, 2)
    put("basis", by_tile(haar @ haar[::BLK].T))
    put("inblock", by_tile(np.tile(onehot, (1, U * B))))
    put("own", by_tile(onehot))
    put("below", by_tile(np.arange(NB)[None, :] < blk[:, None]))
    count = np.zeros((N, 9), np.float32)
    count[:, :NB] = np.clip(tok[:, None] - BLK * np.arange(NB)[None, :], 0, BLK)
    count[:, NB] = 1
    put("count", by_tile(count))
    put("mask", by_tile(np.where(count > 0, 0.0, HIDDEN_SCORE)))
    put("invn", by_tile(1.0 / (tok + 1.0)))
    put("sameb", p[:, None] // NB % B == np.arange(B)[None, :])
    put("fold", p[:, None] % C == np.arange(C)[None, :])
    f = newton_scales()
    put("newton", np.tile(np.stack([-f * f, 2 * f], axis=1).reshape(1, -1), (P, 1)))
    put("scale", by_tile(1.0 / np.sqrt(float(C)) / np.sqrt(tok + 1.0)))
    return out


def hybrid_kernel(nc, io, out):
    ctx = ExitStack()
    with ctx:
        def sb(name, shape, dt=F32):
            return ctx.enter_context(nc.sbuf_tensor(name, shape, dt))

        sems = {}

        def S(name):
            if name not in sems:
                sems[name] = ctx.enter_context(nc.semaphore(name))
            return sems[name]

        consts = sb("consts", [P, NCONST])
        vec = sb("vec", [P, len(VECS)])

        def con(name):
            at, w = CO[name]
            return consts[:, at:at + w]

        def v_(name):
            return vec[:, VI[name]:VI[name] + 1]

        ident = con("ident")
        x0 = sb("x0", [P, J * N])
        w0 = sb("w0", [P, 96])
        wwT = sb("wwT", [P, C])
        theta_qk = sb("theta_qk", [P, TOK])
        theta = theta_qk[0:IC, :].rearrange("p (b n) -> p b n", b=B)
        QK = theta_qk[:, :].rearrange("p (a t h c) -> p a t h c", a=2, t=TILES, h=2)
        probT_rot = sb("probT_rot", [P, TOK])
        probT = probT_rot[0:C, :]
        R = probT_rot[:, :].rearrange("p (a t h c) -> p a t h c", a=2, t=TILES, h=2)
        pooled = sb("pooled", [2 * IC, B, POOLED])
        pg_vsum = sb("pg_vsum", [P, B, C])
        pg = pg_vsum[0:2 * IC]
        gw = sb("gw", [C, B, C])
        f_both = sb("f_both", [P, 2, TILES, POOLED])
        f_sub, f_exp = f_both[:, 0], f_both[:, 1]
        RN = f_both[:, :].rearrange("p a t (h c) -> p (a t h c)", h=2).rearrange(
            "p (t h a c) -> p t h a c", t=TILES, h=2, a=2)
        f_prob = sb("f_prob", [P, TILES, POOLED])
        f_col = sb("f_col", [P, 3, TILES])
        wy = sb("wy", [P, J * N])
        bn6 = sb("bn6", [P, 2, 6])
        col = sb("col", [P, 64])
        x1 = sb("x1", [P, J * N])
        sgn = sb("sgn", [P, J, PAD, PAD], BF16)
        sgn2 = sb("sgn2", [P, J * N], BF16)
        w3T = sb("w3T", [P, 9, C])
        w1T = sb("w1T", [P, C])
        w3n = sb("w3n", [P, C * 9])
        w1n = sb("w1n", [P, C])
        w3s = sb("w3s", [P, 9, P], BF16)
        w1s = sb("w1s", [P, P], BF16)
        va_vb = sb("va_vb", [P, 2 * J * N])
        va, vb = va_vb[:, 0:J * N], va_vb[:, J * N:2 * J * N]
        prob = va_vb[:].rearrange("p (k u n) -> p k u n", k=4, u=U)
        r1 = sb("r1", [P, J * N])
        x2 = sb("x2", [P, J * N])

        T = sb("T", [P, TILES, C])
        ln6 = sb("ln6", [P, TILES, 6])
        lnc = sb("lnc", [P, 8, TILES])
        xn = sb("xn", [P, TILES, C])
        XS = sb("XS", [P, TILES * P], F32R)

        wqT = sb("wqT", [C, HEADS, C])
        wkvT = sb("wkvT", [C, 2, HEADS, P])
        wkT, wvT = wkvT[:, 0], wkvT[:, 1]
        wu = sb("wu", [C, HEADS, C])
        bu = sb("bu", [P, C])
        AH = sb("AH", [P, HEADS, 2, C], F32R)
        AL = sb("AL", [P, HEADS, 2, C], F32R)
        GH = sb("GH", [P, HEADS * C], F32R)
        GL = sb("GL", [P, HEADS * C], F32R)
        xcur = sb("xcur", [P, G, U * P], F32R)
        keys_gates = sb("keys_gates", [P, TOK], F32R)
        KH, KL = (keys_gates[:, s * 4 * N:(s + 1) * 4 * N].rearrange("p (k h n) -> p k h n", k=2, h=2)
                  for s in range(2))
        vproj = sb("vproj", [P, G, U, HEADS * C])
        negmax = sb("negmax", [P, 4, U])
        rowsum = sb("rowsum", [P, 4, U])
        rowinv = sb("rowinv", [P, 4, U])
        scaled_eye = sb("scaled_eye", [P, 2, U, P])
        pT = sb("pT", [P, 4, U, N])
        outT = sb("outT", [P, N])

        nsA = sb("nsA", [C, C])
        nsAT = sb("nsAT", [C, 2, C])
        nsX = sb("nsX", [C, 2, C])
        nsY = sb("nsY", [C, C])
        nsZ = sb("nsZ", [C, C])
        nscoef = sb("nscoef", [C, PAIRS, 2])
        nsc = sb("nsc", [C, 4])
        zeros = sb("zeros", [P, HID])
        ones64 = sb("ones64", [C, C])
        eyedup = sb("eyedup", [C, P])

        gw2 = sb("gw2", [P, EXP2])
        gw2p = sb("gw2p", [P, 2, EXP2], F32R)
        gb2 = sb("gb2", [P, EXP2])
        gw3 = sb("gw3", [P, EXP3])
        gw3p = sb("gw3p", [P, 2, EXP3], F32R)
        gb3 = sb("gb3", [P, EXP3])
        logit = sb("logit", [P, TILES, EXP3])
        top8 = sb("top8", [P, TILES, 8])
        gexp = w3n[:, TILES * EXP3:2 * TILES * EXP3].rearrange("p (t e) -> p t e", e=EXP3)
        gsel = w3n[:, 0:TILES * EXP3].rearrange("p (t e) -> p t e", e=EXP3)
        gates = sb("gates", [P, TILES, C])
        gcol = sb("gcol", [P, 2, TILES])
        b2two = sb("b2two", [P, C])

        in2, in3 = sb("in2", [P, 2, HID + 1]), sb("in3", [P, 2, 2 * HID + 1])
        out2, out3 = sb("out2", [P, 2, C + 1]), sb("out3", [P, 2, C])
        wp1 = sb("wp1", [P, 2, 2, HID], F32R)
        wp2 = sb("wp2", [P, 2, 2, HID], F32R)
        pick = sb("pick", [P, 2, HID], F32R)
        gatesT = keys_gates
        act_out = wy[:].rearrange("p (a n) -> p a n", a=2)
        glu = x0[:].rearrange("p (a n) -> p a n", a=2)
        hid = probT_rot[:].rearrange("p (a n) -> p a n", a=4)
        sums = x0[:].rearrange("p (a n) -> p a n", a=2)

        wv3 = sb("wv3", [C, P])
        wo3T = sb("wo3T", [C, C])
        wq3 = sb("wq3", [P, C])
        qkvw = sb("qkvw", [P, 2, 192], F32R)
        m_a, m_b, m_c, m_d = va, vb, r1, x1
        V3 = f_prob
        q8 = sb("q8", [C, B, NB])
        k8 = sb("k8", [C, B, NB])
        F8 = sb("F8", [NB, B * NB])
        a9 = sb("a9", [P, U, B, 9])
        z9 = sb("z9", [P, U, B, 9])
        e9 = sb("e9", [P, U, B, 9])
        t9 = sb("t9", [P, U, B, 9])
        s9 = sb("s9", [P, 8, U, B])
        dcol = sb("dcol", [P, TILES])
        n2 = sb("n2", [P, 3, TILES * 2])
        pown = sb("pown", [P, TILES])
        pdia = sb("pdia", [P, TILES])
        p8 = sb("p8", [P, U, B, NB])
        p8T = sb("p8T", [P, P])
        vsum = pg_vsum
        yfin = x2

        ps = ctx.enter_context(nc.psum_tensor("ps", [P, 8, 512], F32))

        def banks(a, b):
            return ps[:, a:b, :].rearrange("p a n -> p (a n)")

        def upto(eng, name, j, a_round, more):
            if isinstance(j, int) and j * a_round + more <= 0:
                return
            eng.wait_ge(S(name), j * a_round + more)

        def attention_steps(eng, step, in_loop=None):
            for k in range(-2, 2):
                step(0, k, lambda pair: pair >= 0)
            with eng.Fori(0, J - 1) as j:
                if in_loop:
                    in_loop(j)
                for k in range(2, 2 + PAIRS):
                    step(j, k, lambda pair: True)
            for k in range(2, 2 + PAIRS):
                step(J - 1, k, lambda pair: pair < PAIRS)

        qs = [(j, u, g) for j in range(J) for u in range(U) for g in range(G)]

        def step_of(eng, name):
            done = [0]

            def step(ins):
                done[0] += 1
                ins.then_inc(S(name), 1)
                eng.wait_ge(S(name), done[0])
            return step

        block = ctx.enter_context(nc.Block())

        @block.sync
        def _(sp):
            def load(dst, src, name):
                sp.dma_start(dst, src).then_inc(S(name), 16)

            load(w0[:], io["w0"], "l0_loaded")
            load(x0[:], io["x"], "l0_loaded")
            load(vec[:], io["vec"], "vec_loaded")
            load(consts[:], io["consts"], "consts_loaded")
            load(w3n[:], io["w3n"], "l1_loaded")
            load(w1n[:], io["w1n"], "l1_loaded")
            load(w3T[:], io["w3T"], "l1_loaded")
            load(w1T[:], io["w1T"], "l1_loaded")
            load(wwT[IC:2 * IC, :], io["wwT"], "ww_loaded")
            load(wqT[:], io["wqT"], "attn_loaded")
            load(wkT[:], io["wkT"], "attn_loaded")
            load(wvT[:], io["wvT"], "attn_loaded")
            load(wu[:], io["wu"], "attn_loaded")
            load(bu[:], io["bu"], "bu_loaded")
            load(nsA[:], io["q3"][0:C, :], "ns_loaded")
            load(nsAT[:].rearrange("p a c -> p (a c)"), io["q3T"], "ns_loaded")
            load(wq3[:], io["q3"], "l3_loaded")
            load(wv3[:], io["wv3"], "l3_loaded")
            load(wo3T[:], io["wo3T"], "l3_loaded")
            load(gw2[:], io["gw2"], "gate_loaded")
            load(gb2[:], io["gb2"], "gate_loaded")
            load(gw3[:], io["gw3"], "gate_loaded")
            load(gb3[:], io["gb3"], "gate_loaded")
            sp.wait_ge(S("b2_zeroed"), 1)
            for half in range(2):
                load(b2two[C * half:C * half + EXP2, :], io["b2"], "b2_loaded")
            for which, experts, w_in, w_out, n in ((2, EXP2, in2, out2, 2), (3, EXP3, in3, out3, 3)):
                nm = f"f{which}_"
                sp.sem_inc(S(nm + "w_split"), 2 * n)
                sp.sem_inc(S(nm + "out_chunk"), 8)
                with sp.Fori(0, experts // 2) as i:
                    for e in range(2):
                        rows = bass.ds(i * (2 * P) + e * P, P)
                        sp.wait_ge(S(nm + "w_split"), i * (2 * n) + n * (e + 1))
                        sp.dma_start(w_in[:, e, :], io[nm + "in"][rows, :]).then_inc(S(nm + f"in{e}"), 16)
                        sp.wait_ge(S(nm + "out_chunk"), i * 8 + 4 * (e + 1))
                        sp.dma_start(w_out[:, e, :], io[nm + "out"][rows, :]).then_inc(S(nm + f"out{e}"), 16)
            sp.wait_ge(S("out_ready"), 2)
            sp.dma_start(out, yfin[:]).then_inc(S("stored"), 16)
            sp.wait_ge(S("stored"), 16)

        def ffn(gp, which):
            experts, w_in, parts = {2: (EXP2, in2, [wp1]), 3: (EXP3, in3, [wp1, wp2])}[which]
            nm = f"f{which}_"
            n = len(parts)
            with gp.Fori(0, experts // 2) as i:
                for e in range(2):
                    gp.wait_ge(S(nm + "spread"), i * 8 + 4 * (e + 1))
                    gp.wait_ge(S(nm + f"in{e}"), i * 16 + 16)
                    gp.tensor_tensor(pick[:, e, :], zeros[:],
                                     w_in[:, e, n * HID:n * HID + 1].broadcast_to([P, HID]),
                                     ALU.add).then_inc(S(nm + "w_split"), 1)
                    for k, part in enumerate(parts):
                        src = w_in[:, e, k * HID:(k + 1) * HID]
                        gp.tensor_tensor(part[:, e, 0, :], src, zeros[:], ALU.add).then_inc(S(nm + "w_high"), 1)
                        gp.wait_ge(S(nm + "w_high"), i * (2 * n) + (n * e + k + 1))
                        gp.tensor_tensor(part[:, e, 1, :], src, part[:, e, 0, :].bitcast(F32),
                                         ALU.subtract).then_inc(S(nm + "w_split"), 1)

        def l3_pool(gp):
            gp.wait_ge(S("qk_evac"), 16)
            gp.wait_ge(S("consts_loaded"), 16)
            q1 = QK[:, 0].rearrange("p (j r) h c -> p j (r h c)", j=J)
            q2 = QK[:, 1].rearrange("p (j r) h c -> p j (r h c)", j=J)
            sin = con("sin").unsqueeze(1).broadcast_to([P, J, 256])
            gp.tensor_tensor(m_b[:].rearrange("p (j r) -> p j r", j=J), q2, sin,
                             ALU.mult).then_inc(S("rope_pool"), 1)
            gp.tensor_tensor(m_c[:].rearrange("p (j r) -> p j r", j=J), q1, sin,
                             ALU.mult).then_inc(S("rope_pool"), 1)
            gp.wait_ge(S("pdia_ready"), 1)
            gp.tensor_tensor(m_d[:].rearrange("p (t c) -> p t c", c=C), V3[:],
                             pdia[:].unsqueeze(2).broadcast_to([P, TILES, C]),
                             ALU.mult).then_inc(S("diag_done"), 1)

        @block.gpsimd
        def _(gp):
            step = step_of(gp, "gp_step")
            gp.memset(sgn[:], 0.0).then_inc(S("pads_zeroed"), 1)
            gp.memset(w3s[:], 0.0).then_inc(S("pads_zeroed"), 1)
            gp.memset(w1s[:], 0.0).then_inc(S("pads_zeroed"), 1)
            gp.memset(zeros[:], 0.0).then_inc(S("zeros_ready"), 1)
            gp.wait_ge(S("zeros_ready"), 1)
            gp.memset(ones64[:], 1.0).then_inc(S("ones_ready"), 1)
            gp.memset(b2two[:], 0.0).then_inc(S("b2_zeroed"), 1)
            gp.memset(gates[:], 0.0).then_inc(S("gates_zeroed"), 1)
            gp.wait_ge(S("gate_loaded"), 64)
            for raw, parts in ((gw2, gw2p), (gw3, gw3p)):
                step(gp.tensor_copy(parts[:, 0, :], raw[:]))
                gp.tensor_tensor(parts[:, 1, :], raw[:], parts[:, 0, :].bitcast(F32),
                                 ALU.subtract).then_inc(S("gate_split"), 1)

            gp.wait_ge(S("bu_loaded"), 16)
            gp.wait_ge(S("ln_normalised"), TILES)
            for u in range(2):
                t8 = T[:, 8 * u:8 * u + 8, :]
                gp.tensor_tensor(t8, t8, bu[:].unsqueeze(1).broadcast_to([P, 8, C]),
                                 ALU.add).then_inc(S("t_biased"), 1)
            ffn(gp, 2)
            l3_pool(gp)
            ffn(gp, 3)

        def ln_act(act, n):
            act.wait_ge(S("ln_var"), n + 1)
            act.activation(lnc[:, 6, :], lnc[:, 5, :], ACT.Sqrt).then_inc(S("ln_std"), 1)
            for p in range(4):
                act.wait_ge(S("ln_transposed"), 4 * n + p + 1)
                act.activation(XS[0:C, p * 512:(p + 1) * 512], ps[0:C, p, :],
                               ACT.Copy).then_inc(S("ln_high"), 1)

        def gate_act(act, n):
            experts = (EXP2, EXP3)[n]
            act.wait_ge(S("gate_shifted"), n + 1)
            act.activation(gexp[:, :, 0:experts], logit[:, :, 0:experts],
                           ACT.Exp).then_inc(S("gate_exp"), 1)
            for p in range(4):
                act.wait_ge(S("gates_transposed"), 4 * n + p + 1)
                act.activation(gatesT[0:C, p * 512:(p + 1) * 512], ps[0:C, 4 + p, :],
                               ACT.Copy).then_inc(S("gates_high"), 1)

        def transposed_copy(eng, j, n):
            upto(eng, "p_turned", j, 2 * PAIRS, n + 1)
            upto(eng, "pv_done", j, PAIRS, PAIRS + n // 2 - 1)
            dst = pT[:, n % 4].rearrange("p u n -> p (u n)")
            src = ps[:, 3 + n % 2, :]
            if n % 2 == 0:
                eng.activation(dst, src, ACT.Copy).then_inc(S("pT_even"), 1)
            else:
                eng.tensor_copy(dst, src).then_inc(S("pT_odd"), 1)

        def attention_act(act):
            def key_high(j, k):
                upto(act, "k_projected", j, PAIRS, k + 1)
                upto(act, "scores_ready", j, 2 * PAIRS, 2 * k - 2)
                act.activation(KH[:, k % 2].rearrange("p h n -> p (h n)"), ps[:, 0, :],
                               ACT.Copy).then_inc(S("kh_ready"), 1)

            def exponentials(j, n):
                upto(act, "max_ready", j, 2 * PAIRS, n + 1)
                upto(act, "p_turned", j, 2 * PAIRS, n - 3)
                for u in range(U):
                    ins = act.activation(prob[:, n % 4, u, :], ps[:, 1 + n % 2, u * N:(u + 1) * N], ACT.Exp,
                                         bias=negmax[:, n % 4, u:u + 1], accum_out=rowsum[:, n % 4, u:u + 1])
                ins.then_inc(S("probs_ready"), 1)

            def value_copy(j, m, u):
                upto(act, "v_projected", j, G * U, U * m + u + 1)
                upto(act, "pv_done", j, PAIRS, PAIRS + 4 * m - 4)
                act.activation(vproj[:, m % 2, u, :], ps[:, 7, :], ACT.Copy).then_inc(S("v_ready"), 1)

            def out_copy(j, m):
                upto(act, "pv_done", j, PAIRS, PAIRS + 4 * m + 4)
                upto(act, "out_turned", j, G, G + m)
                act.activation(outT[:], ps[:, 5, 0:N], ACT.Copy).then_inc(S("outT_ready"), 1)

            def step(j, k, there):
                if there(k + 2):
                    key_high(j, k + 2)
                if there(k + 1):
                    exponentials(j, 2 * k + 2)
                if there(k):
                    transposed_copy(act, j, 2 * k)
                if k % 4 == 3 and there(k + 1):
                    value_copy(j, (k + 1) // 4, 0)
                if k % 4 == 0 and there(k):
                    value_copy(j, k // 4, 1)
                if there(k + 1):
                    exponentials(j, 2 * k + 3)
                if k % 4 == 0 and there(k - 1):
                    out_copy(j, k // 4 - 1)

            act.preload_act_table(ACT.Exp)
            attention_steps(act, step)

        @block.scalar
        def _(act):
            act.sem_inc(S("f2_act"), 8)
            act.wait_ge(S("vec_loaded"), 16)
            for p in range(4):
                act.wait_ge(S("l0_projected"), p + 1)
                act.activation(theta[:, 2 * p:2 * p + 2, :].rearrange("p a n -> p (a n)"),
                               ps[2 * IC:3 * IC, p, :], ACT.Identity,
                               bias=vec[2 * IC:3 * IC, 0:1]).then_inc(S("theta_ready"), 1)
            act.wait_ge(S("l1_loaded"), 64)
            act.wait_ge(S("pads_zeroed"), 3)
            for g in range(G):
                h = slice(C * g, C * g + C)
                act.activation(w3s[h, :, h], w3T[h], ACT.Sign).then_inc(S("wsign_ready"), 1)
                act.activation(w1s[h, h], w1T[h], ACT.Sign).then_inc(S("wsign_ready"), 1)
            act.wait_ge(S("folded"), 1)
            for d in range(2):
                act.activation(AH[:, :, d, :], ps[:, 7, :].rearrange("p (h c) -> p h c", c=C), ACT.Copy,
                               scale=1.0 / math.sqrt(C)).then_inc(S("fold_high"), 1)
            act.wait_ge(S("folded"), 2)
            act.activation(GH[:], ps[:, 6, :], ACT.Copy).then_inc(S("fold_high"), 1)
            act.wait_ge(S("f_shifted"), 1)
            act.activation(f_exp[:], f_sub[:], ACT.Exp).then_inc(S("f_exp_ready"), 1)
            for p in range(2):
                act.wait_ge(S("f_transposed"), p + 1)
                act.activation(probT[:, p * 512:(p + 1) * 512], ps[0:C, p, :],
                               ACT.Copy).then_inc(S("probT_act"), 1)
            for p in range(2):
                act.wait_ge(S("wy_ready"), p + 1)
                act.activation(wy[:, p * 512:(p + 1) * 512], ps[:, 4 + p, :], ACT.Identity,
                               bias=v_("bw")).then_inc(S("wy_evac"), 1)
            act.wait_ge(S("bn_var_ready"), 1)
            act.activation(col[:, 11:14], col[:, 8:11], ACT.Sqrt).then_inc(S("bn_std_ready"), 1)
            for p in range(2):
                act.wait_ge(S("x1_ready"), p + 1)
                act.activation(sgn[:, 2 * p:2 * p + 2, 1:1 + IMG, 1:1 + IMG],
                               x1[:, p * 512:(p + 1) * 512].rearrange("p (j h w) -> p j h w", j=2, h=IMG),
                               ACT.Sign, bias=v_("b11")).then_inc(S("sgn_ready"), 1)
            for p in range(2):
                act.wait_ge(S("r1_ready"), p + 1)
                act.activation(sgn2[:, p * 512:(p + 1) * 512], r1[:, p * 512:(p + 1) * 512],
                               ACT.Sign, bias=v_("b21")).then_inc(S("sgn2_ready"), 1)
            act.wait_ge(S("x2_transposed"), 1)
            act.activation(T[:, 0:8, :].rearrange("p t c -> p (t c)"), ps[:, 4, :],
                           ACT.Copy).then_inc(S("T_act"), 1)
            ln_act(act, 0)
            attention_act(act)
            ln_act(act, 1)
            gate_act(act, 0)
            act.preload_act_table(ACT.Gelu)
            with act.Fori(0, EXP2 // 2) as i:
                for k in range(2 * CHUNKS):
                    e = k // CHUNKS
                    act.wait_ge(S("f2_h_ready"), i * 8 + (k + 1))
                    act.wait_ge(S("f2_hid_ready"), i * 8 + (8 + k - 1))
                    act.wait_ge(S(f"f2_out{e}"), i * 16 + 16)
                    act.activation(act_out[:, k % 2, :], ps[:, k % 2, :], ACT.Gelu,
                                   bias=out2[:, e, C:C + 1]).then_inc(S("f2_act"), 1)
            act.wait_ge(S("f2_out_chunk"), 8 + CHUNKS * EXP2)
            act.activation(sums[:, 0, :], ps[:, 6, :], ACT.Copy).then_inc(S("f2_sum_act"), 1)
            ln_act(act, 2)
            for q in range(0, TILES, 2):
                act.wait_ge(S("qkv_ready"), q // 2 + 1)
                z = ps[:, q // 2, 0:384].rearrange("p (g c) -> p g c", g=2)
                act.activation(QK[:, :, q:q + 2].rearrange("p a t h c -> p t a (h c)"),
                               z[:, :, 0:P].rearrange("p g (a c) -> p g a c", a=2),
                               ACT.Copy).then_inc(S("qk_evac"), 1)
                act.activation(V3[:, q:q + 2, :], z[:, :, P:192], ACT.Copy).then_inc(S("qk_evac"), 1)
            for half, (ready, dst) in enumerate((("r1h_ready", m_a), ("r2h_ready", m_c))):
                act.wait_ge(S(ready), 1)
                act.activation(dst[:], R[:, half].rearrange("p t h c -> p (t h c)"),
                               ACT.Square).then_inc(S("rsq_ready"), 1)
            act.wait_ge(S("n2_ready"), 1)
            act.activation(n2[:, 1, :], n2[:, 0, :], ACT.Sqrt).then_inc(S("norm_ready"), 1)
            act.wait_ge(S("qk8_ready"), 1)
            act.activation(q8[:], ps[0:C, 0, 0:64].rearrange("p (b n) -> p b n", n=NB),
                           ACT.Copy).then_inc(S("qk8_evac"), 1)
            act.activation(k8[:], ps[C:P, 0, 0:64].rearrange("p (b n) -> p b n", n=NB),
                           ACT.Copy).then_inc(S("qk8_evac"), 1)
            act.wait_ge(S("F8_ready"), 1)
            act.activation(F8[:], ps[0:NB, 1, 0:64], ACT.Copy).then_inc(S("F8_evac"), 1)
            act.wait_ge(S("a_var_ready"), 1)
            act.activation(s9[:, 3], s9[:, 2], ACT.Sqrt).then_inc(S("a_std_ready"), 1)
            act.wait_ge(S("z_ready"), 1)
            act.activation(e9[:], z9[:], ACT.Exp).then_inc(S("e9_ready"), 1)
            act.wait_ge(S("p8T_ready"), 1)
            act.activation(p8T[:], ps[:, 4, 0:P], ACT.Copy).then_inc(S("p8T_evac"), 1)
            ln_act(act, 3)
            gate_act(act, 1)
            act.preload_act_table(ACT.Silu)
            with act.Fori(0, EXP3 // 2) as i:
                for k in range(2 * CHUNKS):
                    act.wait_ge(S("f3_h_ready"), i * 8 + (k + 1))
                    act.wait_ge(S("f3_glu"), i * 8 + (8 + k - 1))
                    act.activation(act_out[:, k % 2, :], ps[:, k % 2, :],
                                   ACT.Silu).then_inc(S("f3_act"), 1)
            act.wait_ge(S("f3_out_chunk"), 8 + CHUNKS * EXP3)
            act.activation(yfin[:, 0:512], ps[:, 6, :], ACT.Copy).then_inc(S("out_ready"), 1)

        def ln_pe(pe, n):
            for q in range(TILES):
                pe.wait_ge(S("ln_normalised"), TILES * n + q + 1)
                mm = pe.transpose(ps[0:C, q // 4, (q % 4) * P:(q % 4 + 1) * P],
                                  xn[:, q], ident)
                if q % 4 == 3:
                    mm.then_inc(S("ln_transposed"), 1)

        def gate_pe(pe, n):
            experts, parts = ((EXP2, gw2p), (EXP3, gw3p))[n]
            pe.wait_ge(S("gate_split"), 2)
            for q in range(TILES):
                if q % 4 == 0:
                    pe.wait_ge(S("ln_low"), 4 * (2 * n + 1) + q // 4 + 1)
                mm = pe.matmul(ps[:, 4 + q // 8, (q % 8) * 2 * experts:(q % 8 + 1) * 2 * experts],
                               XS[:, q * P:(q + 1) * P], parts[:].rearrange("p a e -> p (a e)"),
                               start=True, stop=True)
                if q % 8 == 7:
                    mm.then_inc(S("gate_logits"), 1)

        def gates_pe(pe, n):
            pe.wait_ge(S("gates_ready"), n + 1)
            for q in range(TILES):
                mm = pe.transpose(ps[0:C, 4 + q // 4, (q % 4) * P:(q % 4 + 1) * P],
                                  gates[:, q], ident)
                if q % 4 == 3:
                    mm.then_inc(S("gates_transposed"), 1)

        def attention_pe(pe):
            def keys(j, k):
                upto(pe, "xcur_ready", j, G, k // 4 + 1)
                upto(pe, "kl_ready", j, PAIRS, k)
                g = (k // 4) % 2
                for h in range(2):
                    o = ps[:, 0, h * N:(h + 1) * N]
                    head = 2 * (k % 4) + h
                    pe.matmul(o, AH[:, head].rearrange("p d c -> p (d c)"), xcur[:, g, :], start=True, stop=False)
                    mm = pe.matmul(o, AL[:, head].rearrange("p d c -> p (d c)"), xcur[:, g, :],
                                   start=False, stop=True)
                mm.then_inc(S("k_projected"), 1)

            def value(j, m, u):
                g = m % 2
                if u == 0:
                    upto(pe, "stream_added", j, G, G + m - 1)
                upto(pe, "v_ready", j, G * U, U * m + u)
                x = xcur[:, g, u * P:(u + 1) * P]
                pe.matmul(ps[:, 7, :], x, GH[:], start=True, stop=False)
                pe.matmul(ps[:, 7, :], x, GL[:], start=False, stop=True).then_inc(S("v_projected"), 1)

            def scores(j, n):
                g, k = (n // 8) % 2, n // 2
                upto(pe, "kl_ready", j, PAIRS, k + 1)
                upto(pe, "probs_ready", j, 2 * PAIRS, n - 1)
                for u in range(U):
                    for part, K in enumerate((KH, KL)):
                        mm = pe.matmul(ps[:, 1 + n % 2, u * N:(u + 1) * N], xcur[:, g, u * P:(u + 1) * P],
                                       K[:, k % 2, n % 2, :], start=(part == 0), stop=(part == 1))
                mm.then_inc(S("scores_ready"), 1)

            def turn(j, n):
                upto(pe, "eye_scaled", j, 2 * PAIRS, n + 1)
                upto(pe, ("pT_even", "pT_odd")[n % 2], j, PAIRS, n // 2)
                for su in range(U):
                    for u in range(U):
                        mm = pe.matmul(ps[:, 3 + n % 2, su * N + u * P:su * N + (u + 1) * P],
                                       prob[:, n % 4, u, su * P:(su + 1) * P], scaled_eye[:, n % 2, u, :],
                                       start=True, stop=True)
                mm.then_inc(S("p_turned"), 1)

            def products(j, k):
                g = (k // 4) % 2
                upto(pe, "pT_even", j, PAIRS, k + 1)
                upto(pe, "pT_odd", j, PAIRS, k + 1)
                upto(pe, "v_ready", j, G * U, U * (k // 4 + 1))
                if k % 4 == 0:
                    upto(pe, "outT_ready", j, G, k // 4)
                for su in range(U):
                    for h in range(2):
                        head = 2 * (k % 4) + h
                        mm = pe.matmul(ps[h * C:(h + 1) * C, 5, 0:N], vproj[:, g, su, head * C:(head + 1) * C],
                                       pT[:, (2 * k + h) % 4, su, :], start=(k % 4 == 0 and su == 0),
                                       stop=(k % 4 == 3 and su == 1), skip_group_check=True)
                mm.then_inc(S("pv_done"), 1)

            def turn_out(j, m, there):
                upto(pe, "outT_ready", j, G, m + 1)
                upto(pe, "v_ready", j, G * U, U * (m + 2 if there(4 * m + 4) else m + 1))
                for u in range(U):
                    mm = pe.matmul(ps[:, 7, u * C:(u + 1) * C], outT[:, u * P:(u + 1) * P], con("fold"),
                                   start=True, stop=True)
                mm.then_inc(S("out_turned"), 1)

            def newton_a(j, s):
                upto(pe, "nsx_ready", j, PAIRS, s + 2)
                pe.matmul(ps[:, 6, 0:C], nsAT[:].rearrange("p a c -> p (a c)"), nsX[:, 1, :], start=True,
                          stop=True).then_inc(S("ns_ax"), 1)

            def newton_b(j, s):
                upto(pe, "nsy_ready", j, PAIRS, s + 1)
                pe.matmul(ps[:, 6, 2 * C:3 * C], nsX[:].rearrange("p a c -> p (a c)"), nsY[:],
                          start=True, stop=True)
                pe.matmul(ps[0:C, 6, C:2 * C], nsY[:], nsX[:, 0, :], start=True,
                          stop=True).then_inc(S("ns_xy"), 1)

            def step(j, k, there):
                in_loop = not isinstance(j, int)
                if there(k + 1):
                    scores(j, 2 * k + 2)
                if there(k + 2):
                    keys(j, k + 2)
                if in_loop:
                    newton_a(j, k - 2)
                if there(k):
                    turn(j, 2 * k)
                if there(k + 1):
                    scores(j, 2 * k + 3)
                if k % 4 == 3 and there(k + 1):
                    value(j, (k + 1) // 4, 0)
                if k % 4 == 0 and there(k):
                    value(j, k // 4, 1)
                if k % 4 == 1 and there(k - 2):
                    turn_out(j, k // 4 - 1, there)
                if in_loop:
                    newton_b(j, k - 2)
                if there(k):
                    turn(j, 2 * k + 1)
                if there(k - 1):
                    products(j, k - 1)

            pe.wait_ge(S("fold_split"), 3)
            pe.wait_ge(S("nsx_ready"), 2)
            pe.sem_inc(S("pv_done"), PAIRS)
            pe.sem_inc(S("out_turned"), G)
            attention_steps(pe, step)

        def ffn_pe(pe, which, start_sums):
            experts, parts, w_out = {2: (EXP2, [wp1], out2), 3: (EXP3, [wp1, wp2], out3)}[which]
            nm = f"f{which}_"
            n = len(parts) + 1
            left = {2: "f2_act", 3: "f3_glu"}[which]

            def hidden(i, k):
                e, c = (k // CHUNKS) % 2, k % CHUNKS
                if c == 0:
                    pe.wait_ge(S(nm + "w_split"), i * (2 * n) + (2 * n + n * (k // CHUNKS + 1)))
                pe.wait_ge(S(left), i * 8 + (8 + k - 1))
                chunk = slice(c * CHUNK, (c + 1) * CHUNK)
                for w, part in enumerate(parts):
                    for s in range(2):
                        mm = pe.matmul(ps[:, 2 * w + c % 2, :], part[:, e, s, :], XS[:, chunk],
                                       start=(s == 0), stop=(s == 1))
                mm.then_inc(S(nm + "h_ready"), 1)

            def spread(i, k):
                e, c = (k // CHUNKS) % 2, k % CHUNKS
                chunk = slice(c * CHUNK, (c + 1) * CHUNK)
                pe.wait_ge(S(nm + "hid_ready"), i * 8 + (8 + k - 1))
                pe.matmul(ps[:, 4 + c % 2, :], pick[:, e, :], gatesT[:, chunk],
                          start=True, stop=True).then_inc(S(nm + "spread"), 1)

            def output(i, k):
                e, c = k // CHUNKS, k % CHUNKS
                if c == 0:
                    pe.wait_ge(S(nm + f"out{e}"), i * 16 + 16)
                pe.wait_ge(S(nm + "hid_ready"), i * 8 + (8 + k + 1))
                half = slice(C * (c % 2), C * (c % 2) + C)
                pe.matmul(ps[half, 6 + c // 2, :], w_out[:, e, 0:C], hid[:, c, :], start=False,
                          stop=False, skip_group_check=True).then_inc(S(nm + "out_chunk"), 1)

            def pairs(i, last):
                for k in range(0, 8, 2):
                    ahead = () if last and k == 6 else (k + 2, k + 3)
                    for kk in ahead:
                        hidden(i, kk)
                    output(i, k)
                    output(i, k + 1)
                    for kk in ahead:
                        spread(i, kk)

            for k in range(2):
                hidden(0, k)
            gates_pe(pe, which - 2)
            for k in range(2):
                pe.wait_ge(S("gates_low"), 4 * (which - 2) + k + 1)
                spread(0, k)
            pe.wait_ge(S("gates_low"), 4 * (which - 1))
            start_sums()
            with pe.Fori(0, experts // 2 - 1) as i:
                pairs(i, False)
            pairs(experts // 2 - 1, True)
        def l3_pe(pe):
            pe.wait_ge(S("qkvw_ready"), 6)
            for q in range(TILES):
                if q % 2 == 0:
                    pe.wait_ge(S("ln_low"), 12)
                for part in range(2):
                    mm = pe.matmul(ps[:, q // 2, (q % 2) * 192:(q % 2 + 1) * 192], XS[:, q * P:(q + 1) * P],
                                   qkvw[:, part, :], start=(part == 0), stop=(part == 1))
                if q % 2 == 1:
                    mm.then_inc(S("qkv_ready"), 1)
            pe.wait_ge(S("qk_evac"), 16)
            for u in range(U):
                mm = pe.matmul(ps[:, 3, :], con("inblock")[:, u * P:(u + 1) * P],
                               V3[:].rearrange("p (j u g) c -> p j u (g c)", j=J, u=U)[:, :, u, :],
                               start=(u == 0), stop=(u == 1))
            mm.then_inc(S("vsum_ready"), 1)
            for p in range(2):
                pe.matmul(ps[:, 6 + p, :], con("lower"), V3[:, 8 * p:8 * p + 8, :].rearrange("p t c -> p (t c)"),
                          start=True, stop=True).then_inc(S("prefix_ready"), 1)
            pe.wait_ge(S("rn_ready"), 2)
            for j in range(J):
                for g in range(G):
                    b = 2 * j + g
                    for u in range(U):
                        mm = pe.matmul(ps[:, 0, b * NB:(b + 1) * NB],
                                       RN[:, 4 * j + 2 * u + g].rearrange("p h a c -> p (h a c)"),
                                       con("basis")[:, u * NB:(u + 1) * NB], start=(u == 0), stop=(u == 1))
            mm.then_inc(S("qk8_ready"), 1)
            pe.wait_ge(S("qk8_evac"), 2)
            for b in range(B):
                mm = pe.matmul(ps[0:NB, 1, b * NB:(b + 1) * NB], q8[:, b, :], k8[:, b, :],
                               start=True, stop=True)
            mm.then_inc(S("F8_ready"), 1)
            pe.wait_ge(S("F8_evac"), 1)
            for u in range(U):
                mm = pe.matmul(ps[:, 2, u * 64:(u + 1) * 64], con("expand")[0:NB, u * P:(u + 1) * P],
                               F8[:], start=True, stop=True)
            mm.then_inc(S("far_ready"), 1)
            pe.wait_ge(S("p8_ready"), 1)
            pe.transpose(ps[:, 4, 0:P], p8[:].rearrange("p u b n -> p (u b n)"), ident).then_inc(S("p8T_ready"), 1)
            pe.wait_ge(S("p8T_evac"), 1)
            pe.wait_ge(S("vsum_evac"), 1)
            for u in range(U):
                h = slice(C * u, C * u + C)
                mm = pe.matmul(ps[:, u, :], p8T[h, :], vsum[h].rearrange("p b c -> p (b c)"), start=True, stop=True)
            mm.then_inc(S("yfar_ready"), 1)

        @block.tensor
        def _(pe):
            pe.wait_ge(S("l0_loaded"), 32)
            pe.sem_inc(S("f2_spread"), 8)
            pe.sem_inc(S("f3_spread"), 8)
            for p in range(4):
                g, jj = p // 2, p % 2
                h = slice(C * g, C * g + C)
                pe.matmul(ps[0:96, p, :], w0[h, :], x0[h, jj * 512:(jj + 1) * 512],
                          start=True, stop=True).then_inc(S("l0_projected"), 1)
            pe.wait_ge(S("attn_loaded"), 64)
            for h in range(HEADS):
                mm = pe.matmul(ps[:, 7, h * C:(h + 1) * C], wkT[:, h, :], wqT[:, h, :],
                               start=True, stop=True)
            mm.then_inc(S("folded"), 1)
            for h in range(HEADS):
                mm = pe.matmul(ps[:, 6, h * C:(h + 1) * C], wvT[:, h, :], wu[:, h, :],
                               start=True, stop=True)
            mm.then_inc(S("folded"), 1)
            pe.wait_ge(S("pg_ready"), 1)
            pe.wait_ge(S("ww_loaded"), 16)
            for b in range(B):
                mm = pe.matmul(ps[0:C, 4, b * C:(b + 1) * C], pg[IC:2 * IC, b, :], wwT[IC:2 * IC, :],
                               start=True, stop=True)
            mm.then_inc(S("gw_done"), 1)
            pe.wait_ge(S("theta_ready"), 4)
            pe.wait_ge(S("fold_split"), 3)
            for b in range(B):
                for u in range(U):
                    t = b * U + u
                    mm = pe.matmul(ps[:, 5 + t // 8, (t % 8) * C:(t % 8 + 1) * C],
                                   theta[:, b, u * P:(u + 1) * P], pg[0:IC, b, :], start=True, stop=True)
            mm.then_inc(S("f_ready"), 1)
            pe.wait_ge(S("l3_loaded"), 48)
            pe.matmul(ps[:, 7, 0:C], wv3[:], wo3T[:], start=True, stop=True).then_inc(S("vo_done"), 1)
            pe.wait_ge(S("ones_ready"), 1)
            pe.wait_ge(S("ns_sq_ready"), 1)
            pe.matmul(ps[0:C, 7, C:C + 1], ones64[:], nsc[:, 0:1], start=True,
                      stop=True).then_inc(S("ns_norm_done"), 1)
            pe.wait_ge(S("consts_loaded"), 16)
            pe.wait_ge(S("f_prob_ready"), 1)
            for t in range(TILES):
                mm = pe.transpose(ps[0:C, t // 4, (t % 4) * P:(t % 4 + 1) * P], f_prob[:, t, :], ident)
                if t % 4 == 3:
                    mm.then_inc(S("f_transposed"), 1)
            pe.wait_ge(S("gw_evac"), 1)
            pe.wait_ge(S("probT_act"), 2)
            pe.wait_ge(S("probT_vec"), 2)
            for p in range(2):
                for jj in range(2):
                    for g in range(G):
                        b = 4 * g + 2 * p + jj
                        mm = pe.matmul(ps[C * g:C * g + C, 4 + p, jj * N:(jj + 1) * N], gw[:, b, :],
                                       probT[:, b * N:(b + 1) * N], start=True, stop=True)
                mm.then_inc(S("wy_ready"), 1)
            pe.wait_ge(S("bn_mean_half"), 1)
            pe.matmul(ps[:, 6, 0:1], con("halfavg"), col[:, 0:1], start=True,
                      stop=True).then_inc(S("bn_mu_done"), 1)
            pe.wait_ge(S("bn_var_half"), 1)
            pe.matmul(ps[:, 6, 1:2], con("halfavg"), col[:, 4:5], start=True,
                      stop=True).then_inc(S("bn_var_done"), 1)
            pe.wait_ge(S("wsign_ready"), 4)
            for p in range(2):
                pe.wait_ge(S("sgn_ready"), p + 1)
                for k in range(9):
                    mm = pe.matmul(ps[:, p, :], w3s[:, k, :],
                                   sgn[:, 2 * p:2 * p + 2, k // 3:k // 3 + IMG, k % 3:k % 3 + IMG],
                                   start=(k == 0), stop=(k == 8))
                mm.then_inc(S("conv3_ready"), 1)
            for p in range(2):
                pe.wait_ge(S("sgn2_ready"), p + 1)
                pe.matmul(ps[:, 2 + p, :], w1s[:], sgn2[:, p * 512:(p + 1) * 512], start=True,
                          stop=True).then_inc(S("conv1_ready"), 1)
            for p in range(2):
                pe.wait_ge(S("x2_ready"), p + 1)
                for t in range(4 * p, 4 * p + 4):
                    mm = pe.transpose(ps[:, 4 + p, (t % 4) * P:(t % 4 + 1) * P],
                                      x2[:, t * P:(t + 1) * P], ident)
                mm.then_inc(S("x2_transposed"), 1)
            ln_pe(pe, 0)
            attention_pe(pe)
            pe.wait_ge(S("nsx_ready"), NEWTON + 2)
            pe.matmul(ps[:, 6, 0:C], eyedup[:], nsX[:, 0, :], start=True, stop=True).then_inc(S("pinv_done"), 1)
            ln_pe(pe, 1)
            gate_pe(pe, 0)

            def start_with_biases():
                pe.wait_ge(S("b2_loaded"), 32)
                for c in range(CHUNKS):
                    pe.matmul(ps[C * (c % 2):C * (c % 2) + C, 6 + c // 2, :], b2two[:],
                              gatesT[:, c * CHUNK:(c + 1) * CHUNK].bitcast(F32), start=True, stop=False,
                              skip_group_check=True)

            ffn_pe(pe, 2, start_with_biases)
            for b, done in enumerate(("f2_sum_act", "f2_sum_vec")):
                pe.wait_ge(S(done), 1)
                for t in range(CT):
                    mm = pe.transpose(ps[:, b, t * P:(t + 1) * P], sums[:, b, t * P:(t + 1) * P], ident)
                mm.then_inc(S("f2_turned"), 1)
            ln_pe(pe, 2)
            l3_pe(pe)
            ln_pe(pe, 3)
            gate_pe(pe, 1)

            def start_with_stream():
                for q in range(TILES):
                    c, t = q // CT, q % CT
                    pe.matmul(ps[C * (c % 2):C * (c % 2) + C, 6 + c // 2, t * P:(t + 1) * P], T[:, q, :], ident,
                              start=(t == 0), stop=False, skip_group_check=True)

            ffn_pe(pe, 3, start_with_stream)

        def l3_vector(dve, step, tt, ts, stt):
            dve.wait_ge(S("qk_evac"), 16)
            q1 = QK[:, 0].rearrange("p (j r) h c -> p j (r h c)", j=J)
            q2 = QK[:, 1].rearrange("p (j r) h c -> p j (r h c)", j=J)
            cos = con("cos").unsqueeze(1).broadcast_to([P, J, 256])

            def by_j(a):
                return a.rearrange("p (j r) -> p j r", j=J)
            r_1 = R[:, 0].rearrange("p t h c -> p (t h c)")
            r_2 = R[:, 1].rearrange("p t h c -> p (t h c)")
            step(tt(by_j(m_a[:]), q1, cos, ALU.mult))
            step(tt(by_j(m_d[:]), q2, cos, ALU.mult))
            dve.wait_ge(S("rope_pool"), 1)
            tt(r_1, m_a[:], m_b[:], ALU.subtract).then_inc(S("r1h_ready"), 1)
            dve.wait_ge(S("rope_pool"), 2)
            tt(r_2, m_c[:], m_d[:], ALU.add).then_inc(S("r2h_ready"), 1)
            dve.wait_ge(S("rsq_ready"), 2)
            step(tt(m_b[:], m_a[:], m_c[:], ALU.add))
            dve.tensor_reduce(n2[:, 0, :], m_b[:].rearrange("p (r c) -> p r c", c=32), AX.X,
                              ALU.add).then_inc(S("n2_ready"), 1)
            dve.wait_ge(S("norm_ready"), 1)
            step(ts(n2[:, 2, :], n2[:, 1, :], EPS_L2, None, ALU.add))
            step(dve.reciprocal(n2[:, 0, :], n2[:, 2, :]))
            for half in range(2):
                tt(RN[:, :, :, half, :].rearrange("p t h c -> p (t h) c"), R[:, half].rearrange("p t h c -> p (t h) c"),
                   n2[:, 0, :].unsqueeze(2).broadcast_to([P, 2 * TILES, 32]),
                   ALU.mult).then_inc(S("rn_ready"), 1)
            dve.wait_ge(S("vsum_ready"), 1)
            tt(vsum[:], ps[:, 3, :].rearrange("p (b c) -> p b c", c=C),
               con("sameb").unsqueeze(2).broadcast_to([P, B, C]), ALU.mult).then_inc(S("vsum_evac"), 1)
            dve.wait_ge(S("rn_ready"), 2)
            step(tt(m_a[:].rearrange("p (t c) -> p t c", c=C), RN[:, :, 0].rearrange("p t a c -> p t (a c)"),
                    RN[:, :, 1].rearrange("p t a c -> p t (a c)"), ALU.mult))
            step(dve.tensor_reduce(dcol[:], m_a[:].rearrange("p (t c) -> p t c", c=C), AX.X, ALU.add))

            def table(name):
                return con(name).rearrange("p (u n) -> p u n", u=U).unsqueeze(2).broadcast_to([P, U, B, 9])
            def of_u(a, u):
                return a.rearrange("p (j u g) -> p j u g", j=J, u=U)[:, :, u, :]
            for u in range(U):
                step(ts(a9[:, u, :, NB].rearrange("p (j g) -> p j g", g=G), of_u(dcol[:], u),
                        con("scale")[:, u:u + 1], None, ALU.mult))
            dve.wait_ge(S("far_ready"), 1)
            for u in range(U):
                step(ts(a9[:, u, :, 0:NB], ps[:, 2, u * 64:(u + 1) * 64].rearrange("p (b n) -> p b n", n=NB),
                        con("scale")[:, u:u + 1], None, ALU.mult))

            def over(c):
                return c.unsqueeze(3).broadcast_to([P, U, B, 9])
            step(tt(t9[:], a9[:], table("count"), ALU.mult))
            step(dve.tensor_reduce(s9[:, 0], t9[:], AX.X, ALU.add))
            for u in range(U):
                step(ts(s9[:, 1, u], s9[:, 0, u], con("invn")[:, u:u + 1], None, ALU.mult))
            step(tt(z9[:], a9[:], over(s9[:, 1]), ALU.subtract))
            step(tt(t9[:], z9[:], z9[:], ALU.mult))
            step(tt(t9[:], t9[:], table("count"), ALU.mult))
            step(dve.tensor_reduce(s9[:, 0], t9[:], AX.X, ALU.add))
            for u in range(U):
                ins = ts(s9[:, 2, u], s9[:, 0, u], con("invn")[:, u:u + 1], EPS_VAR, ALU.mult, ALU.max)
                ins.then_inc(S("a_var_half"), 1)
            dve.wait_ge(S("a_var_half"), 2)
            dve.nop().then_inc(S("a_var_ready"), 1)
            dve.wait_ge(S("a_std_ready"), 1)
            step(dve.reciprocal(s9[:, 4], s9[:, 3]))
            step(tt(z9[:], z9[:], over(s9[:, 4]), ALU.mult))
            step(tt(z9[:], z9[:], table("mask"), ALU.add))
            step(dve.tensor_reduce(s9[:, 5], z9[:], AX.X, ALU.max))
            tt(z9[:], z9[:], over(s9[:, 5]), ALU.subtract).then_inc(S("z_ready"), 1)
            dve.wait_ge(S("e9_ready"), 1)
            step(tt(t9[:], e9[:], table("count"), ALU.mult))
            step(dve.tensor_reduce(s9[:, 6], t9[:], AX.X, ALU.add))
            step(dve.reciprocal(s9[:, 7], s9[:, 6]))
            step(tt(e9[:], e9[:], over(s9[:, 7]), ALU.mult))

            def blocks(name):
                return con(name).rearrange("p (u n) -> p u n", u=U).unsqueeze(2).broadcast_to([P, U, B, NB])
            tt(p8[:], e9[:, :, :, 0:NB], blocks("below"), ALU.mult).then_inc(S("p8_ready"), 1)
            for u in range(U):
                ins = dve.tensor_copy(of_u(pdia[:], u), e9[:, u, :, NB].rearrange("p (j g) -> p j g", g=G))
                step(ins)
            dve.nop().then_inc(S("pdia_ready"), 1)
            step(tt(t9[:, :, :, 0:NB], e9[:, :, :, 0:NB], blocks("own"), ALU.mult))
            for u in range(U):
                step(dve.tensor_reduce(of_u(pown[:], u), t9[:, u, :, 0:NB].rearrange("p (j g) n -> p j g n", g=G),
                                       AX.X, ALU.add))
            dve.wait_ge(S("prefix_ready"), 2)
            t = T[:].rearrange("p t c -> p (t c)")
            ma = m_a[:].rearrange("p (t c) -> p t c", c=C)
            step(tt(ma, ps[:, 6:8, :].rearrange("p a (t c) -> p (a t) c", c=C),
                    pown[:].unsqueeze(2).broadcast_to([P, TILES, C]), ALU.mult))
            step(tt(t, t, m_a[:], ALU.add))
            dve.wait_ge(S("yfar_ready"), 1)
            tu = T[:].rearrange("p (j u g) c -> p j u g c", j=J, u=U)
            for u in range(U):
                ins = tt(tu[:, :, u], tu[:, :, u], ps[:, u, :].rearrange("p (j g c) -> p j g c", j=J, g=G), ALU.add)
            step(ins)
            dve.wait_ge(S("diag_done"), 1)
            step(tt(t, t, m_d[:], ALU.add))

        @block.vector
        def _(dve):
            step = step_of(dve, "dve_step")
            tt, ts, stt = dve.tensor_tensor, dve.tensor_scalar, dve.scalar_tensor_tensor
            for name in ("f2_hid_ready", "f3_glu", "f3_hid_ready"):
                dve.sem_inc(S(name), 8)

            for p in range(4):
                dve.wait_ge(S("l0_projected"), p + 1)
                ins = dve.tensor_reduce(pooled[:, 2 * p:2 * p + 2, :].rearrange("p b n -> p (b n)")
                                        .rearrange("p (r w) -> p r w", w=IMG // 2),
                                        ps[0:2 * IC, p, :].rearrange("p (r a w b) -> p r w a b", a=2, b=2, w=IMG // 2),
                                        AX.XY, ALU.max)
            step(ins)
            dve.wait_ge(S("vec_loaded"), 16)
            ts(pg[:], pooled[:], vec[0:2 * IC, 0:1], None, ALU.add).then_inc(S("pg_ready"), 1)
            dve.wait_ge(S("fold_high"), 3)
            for d in range(2):
                stt(AL[:, :, d, :], ps[:, 7, :].rearrange("p (h c) -> p h c", c=C), 1.0 / math.sqrt(C),
                    AH[:, :, d, :].bitcast(F32), ALU.mult, ALU.subtract).then_inc(S("fold_split"), 1)
            tt(GL[:], ps[:, 6, :], GH[:].bitcast(F32), ALU.subtract).then_inc(S("fold_split"), 1)
            dve.wait_ge(S("gw_done"), 1)
            dve.tensor_copy(gw[:], ps[0:C, 4, :].rearrange("p (b c) -> p b c", c=C)).then_inc(S("gw_evac"), 1)
            dve.wait_ge(S("f_ready"), 1)
            f = ps[:, 5:7, :].rearrange("p a (t c) -> p (a t) c", c=POOLED)

            def wide(c, n=POOLED, t=TILES):
                return c.unsqueeze(2).broadcast_to([P, t, n])
            step(dve.tensor_reduce(f_col[:, 0, :], f, AX.X, ALU.max))
            tt(f_sub[:], f, wide(f_col[:, 0, :]), ALU.subtract).then_inc(S("f_shifted"), 1)
            dve.wait_ge(S("ns_loaded"), 32)
            step(dve.tensor_tensor_reduce(nsY[:], nsA[:], nsA[:], 1.0, 0.0, ALU.mult, ALU.add, nsc[:, 0:1]))
            dve.nop().then_inc(S("ns_sq_ready"), 1)
            dve.wait_ge(S("consts_loaded"), 16)
            for d in range(2):
                step(dve.tensor_copy(eyedup[:, d * C:(d + 1) * C], ident[0:C, 0:C]))
            dve.wait_ge(S("f_exp_ready"), 1)
            step(dve.tensor_reduce(f_col[:, 1, :], f_exp[:], AX.X, ALU.add))
            step(dve.reciprocal(f_col[:, 2, :], f_col[:, 1, :]))
            tt(f_prob[:], f_exp[:], wide(f_col[:, 2, :]), ALU.mult).then_inc(S("f_prob_ready"), 1)
            dve.wait_ge(S("ns_norm_done"), 1)
            step(dve.reciprocal(nsc[:, 1:2], ps[0:C, 7, C:C + 1]))
            ts(nsX[:, 1, :], nsAT[:, 0, :], nsc[:, 1:2], None, ALU.mult).then_inc(S("nsx_ready"), 1)
            ts(nsX[:, 0, :], nsA[:], nsc[:, 1:2], None, ALU.mult).then_inc(S("nsx_ready"), 1)
            dve.wait_ge(S("vo_done"), 1)
            dve.wait_ge(S("l3_loaded"), 48)

            def query_or_key(part, h):
                return qkvw[:, part, 0:P].rearrange("p (a h c) -> p a h c", a=2, h=2)[:, :, h, :]
            split = [(query_or_key(0, 0), query_or_key(1, 0), wq3[:].rearrange("p (a c) -> p a c", a=2)),
                     (qkvw[:, 0, P:192], qkvw[:, 1, P:192], ps[:, 7, 0:C])]
            for high, low, raw in split:
                step(dve.tensor_copy(high, raw))
                tt(low, raw, high.bitcast(F32), ALU.subtract).then_inc(S("qkvw_ready"), 2)
            dve.wait_ge(S("l1_loaded"), 64)
            ones = [("w3n", w3n, 9 * C, 20), ("w1n", w1n, C, 21)]
            for _, w, n, c in ones:
                step(dve.tensor_reduce(col[:, c:c + 1], w[:], AX.X, ALU.add, apply_absolute_value=True))
            step(ts(col[:, 22:23], col[:, 20:21], 1.0 / (9 * C), None, ALU.mult))
            step(ts(col[:, 23:24], col[:, 21:22], 1.0 / C, None, ALU.mult))
            step(ts(col[:, 9:10], v_("v1"), EPS_BN, None, ALU.add))
            step(ts(col[:, 10:11], v_("v2"), EPS_BN, None, ALU.add))
            for p in range(2, 4):
                dve.wait_ge(S("f_transposed"), p + 1)
                dve.tensor_copy(probT[:, p * 512:(p + 1) * 512], ps[0:C, p, :]).then_inc(S("probT_vec"), 1)
            dve.wait_ge(S("wy_evac"), 2)
            for p in range(2):
                step(dve.bn_stats(bn6[:, p, :], wy[:, p * 512:(p + 1) * 512]))
            dve.bn_aggr(col[:, 0:2], bn6[:].rearrange("p a s -> p (a s)")).then_inc(S("bn_mean_half"), 1)
            dve.wait_ge(S("bn_mean_half"), 1)
            dve.wait_ge(S("bn_mu_done"), 1)
            step(dve.tensor_copy(col[:, 2:3], ps[:, 6, 0:1]))
            step(tt(col[:, 3:4], col[:, 0:1], col[:, 2:3], ALU.subtract))
            stt(col[:, 4:5], col[:, 3:4], col[:, 3:4], col[:, 1:2], ALU.mult, ALU.add).then_inc(S("bn_var_half"), 1)
            dve.wait_ge(S("bn_var_done"), 1)
            ts(col[:, 8:9], ps[:, 6, 1:2], EPS_BN, None, ALU.add).then_inc(S("bn_var_ready"), 1)
            dve.wait_ge(S("bn_std_ready"), 1)
            step(dve.reciprocal(col[:, 24:27], col[:, 11:14]))
            step(tt(col[:, 28:29], col[:, 24:25], v_("gamma"), ALU.mult))
            step(tt(col[:, 30:31], col[:, 28:29], col[:, 2:3], ALU.mult))
            step(tt(col[:, 29:30], v_("beta"), col[:, 30:31], ALU.subtract))
            dve.wait_ge(S("l0_loaded"), 32)
            for p in range(2):
                s = slice(p * 512, (p + 1) * 512)
                step(ts(va[:, s], wy[:, s], col[:, 28:29], col[:, 29:30], ALU.mult, ALU.add))
                tt(x1[:, s], va[:, s], x0[:, s], ALU.add).then_inc(S("x1_ready"), 1)
            for k, (g_, be, m_, b_) in enumerate((("g1", "be1", "m1", "b12"), ("g2", "be2", "m2", "b22"))):
                inv = col[:, 32 + k:33 + k]
                step(tt(inv, v_(g_), col[:, 25 + k:26 + k], ALU.mult))
                step(tt(col[:, 34 + k:35 + k], inv, col[:, 22 + k:23 + k], ALU.mult))
                step(tt(col[:, 38:39], inv, v_(m_), ALU.mult))
                step(tt(col[:, 39:40], v_(be), col[:, 38:39], ALU.subtract))
                step(tt(col[:, 36 + k:37 + k], col[:, 39:40], v_(b_), ALU.add))

            def prelu(dst, src, a, after, tmp):
                step(ts(tmp, src, 0.0, v_(a), ALU.min, ALU.mult))
                step(stt(dst, src, 0.0, tmp, ALU.max, ALU.add))
                return ts(dst, dst, v_(after), None, ALU.add)

            for bank, ready, k, src, dst, a, after, done in (
                    (0, "conv3_ready", 0, x1, r1, "a1", "b13", "r1_ready"),
                    (2, "conv1_ready", 1, r1, x2, "a2", "b23", "x2_ready")):
                for p in range(2):
                    s = slice(p * 512, (p + 1) * 512)
                    dve.wait_ge(S(ready), p + 1)
                    step(ts(va[:, s], ps[:, bank + p, :], col[:, 34 + k:35 + k], col[:, 36 + k:37 + k],
                            ALU.mult, ALU.add))
                    step(tt(vb[:, s], va[:, s], src[:, s], ALU.add))
                    prelu(dst[:, s], vb[:, s], a, after, va[:, s]).then_inc(S(done), 1)
                    dve.wait_ge(S(done), p + 1)
            dve.wait_ge(S("x2_transposed"), 2)
            dve.tensor_copy(T[:, 8:16, :].rearrange("p t c -> p (t c)"), ps[:, 5, :]).then_inc(S("T_vec"), 1)
            dve.wait_ge(S("T_act"), 1)
            dve.wait_ge(S("T_vec"), 1)

            def layer_norm(n):
                for q in range(TILES):
                    ins = dve.bn_stats(ln6[:, q, :], T[:, q, :])
                step(ins)
                me, mo = ln6[:, :, 1], ln6[:, :, 4]
                tt(lnc[:, 0, :], me, mo, ALU.add)
                tt(lnc[:, 2, :], ln6[:, :, 2], ln6[:, :, 5], ALU.add)
                step(tt(lnc[:, 1, :], me, mo, ALU.subtract))
                step(tt(lnc[:, 3, :], lnc[:, 1, :], lnc[:, 1, :], ALU.mult))
                step(stt(lnc[:, 4, :], lnc[:, 3, :], C / 4.0, lnc[:, 2, :], ALU.mult, ALU.add))
                ts(lnc[:, 1, :], lnc[:, 0, :], 0.5, None, ALU.mult)
                ts(lnc[:, 5, :], lnc[:, 4, :], 1.0 / C, EPS_LN, ALU.mult, ALU.add).then_inc(S("ln_var"), 1)
                dve.wait_ge(S("ln_std"), n + 1)
                step(dve.reciprocal(lnc[:, 7, :], lnc[:, 6, :]))
                for q in range(TILES):
                    ts(xn[:, q], T[:, q, :], lnc[:, 1, q:q + 1],
                       lnc[:, 7, q:q + 1], ALU.subtract, ALU.mult).then_inc(S("ln_normalised"), 1)
                for p in range(4):
                    dve.wait_ge(S("ln_high"), 4 * n + p + 1)
                    low = XS[C:P, p * 512:(p + 1) * 512]
                    high = XS[0:C, p * 512:(p + 1) * 512].bitcast(F32)
                    tt(low, ps[0:C, p, :], high, ALU.subtract).then_inc(S("ln_low"), 1)

            def gate(n):
                experts, gb = ((EXP2, gb2), (EXP3, gb3))[n]
                dve.wait_ge(S("gate_loaded"), 64)
                lg, ge, gs = logit[:, :, 0:experts], gexp[:, :, 0:experts], gsel[:, :, 0:experts]
                for half in range(2):
                    dve.wait_ge(S("gate_logits"), 2 * n + half + 1)
                    both = ps[:, 4 + half, 0:16 * experts].rearrange("p (t a e) -> p t a e", a=2, e=experts)
                    lh = lg[:, 8 * half:8 * half + 8, :]
                    step(tt(lh, both[:, :, 0, :], gb[:].unsqueeze(1).broadcast_to([P, 8, experts]), ALU.add))
                    step(tt(lh, lh, both[:, :, 1, :], ALU.add))
                    for q in range(8 * half, 8 * half + 8):
                        ins = dve.max(top8[:, q, :], lg[:, q, :])
                step(ins)
                step(tt(gs, lg, wide(top8[:, :, 1], experts), ALU.is_ge))
                tt(lg, lg, wide(top8[:, :, 0], experts), ALU.subtract).then_inc(S("gate_shifted"), 1)
                dve.wait_ge(S("gate_exp"), n + 1)
                step(tt(gs, ge, gs, ALU.mult))
                step(dve.tensor_reduce(gcol[:, 0, :], (ge, gs)[n], AX.X, ALU.add))
                step(dve.reciprocal(gcol[:, 1, :], gcol[:, 0, :]))
                dve.wait_ge(S("gates_zeroed"), 1)
                tt(gates[:, :, 0:experts], gs, wide(gcol[:, 1, :], experts),
                   ALU.mult).then_inc(S("gates_ready"), 1)
                for p in range(4):
                    dve.wait_ge(S("gates_high"), 4 * n + p + 1)
                    low = gatesT[C:P, p * 512:(p + 1) * 512]
                    high = gatesT[0:C, p * 512:(p + 1) * 512].bitcast(F32)
                    tt(low, ps[0:C, 4 + p, :], high, ALU.subtract).then_inc(S("gates_low"), 1)

            layer_norm(0)
            def tokens(j, m):
                upto(dve, "scores_ready", j, 2 * PAIRS, 8 * m - 8)
                dve.wait_ge(S("ln_low"), 4)
                src = XS[:].bitcast(F32).rearrange("p (j u g n) -> p j u g n", j=J, u=U, g=G)
                at = j + m // 2
                at = slice(at, at + 1) if isinstance(at, int) else bass.ds(at, 1)
                dve.tensor_copy(xcur[:, m % 2, :].rearrange("p (u n) -> p u n", u=U).unsqueeze(1),
                                src[:, at, :, m % 2, :]).then_inc(S("xcur_ready"), 1)

            def key_low(j, k):
                upto(dve, "kh_ready", j, PAIRS, k + 1)
                tt(KL[:, k % 2].rearrange("p h n -> p (h n)"), ps[:, 0, :],
                   KH[:, k % 2].rearrange("p h n -> p (h n)").bitcast(F32),
                   ALU.subtract).then_inc(S("kl_ready"), 1)

            def maxima(j, n):
                upto(dve, "scores_ready", j, 2 * PAIRS, n + 1)
                upto(dve, "probs_ready", j, 2 * PAIRS, n - 3)
                dve.tensor_reduce(negmax[:, n % 4, :],
                                  ps[:, 1 + n % 2, :].rearrange("p (u n) -> p u n", u=U), AX.X, ALU.max,
                                  negate=True).then_inc(S("max_ready"), 1)

            def scale_eye(j, n):
                upto(dve, "probs_ready", j, 2 * PAIRS, n + 1)
                dve.reciprocal(rowinv[:, n % 4, :], rowsum[:, n % 4, :]).then_inc(S("rowinv_ready"), 1)
                upto(dve, "rowinv_ready", j, 2 * PAIRS, n + 1)
                upto(dve, "p_turned", j, 2 * PAIRS, n - 1)
                tt(scaled_eye[:, n % 2], ident.unsqueeze(1).broadcast_to([P, U, P]),
                   rowinv[:, n % 4, :].unsqueeze(2).broadcast_to([P, U, P]), ALU.mult).then_inc(S("eye_scaled"), 1)

            def add_out(j, m):
                dve.wait_ge(S("t_biased"), 2)
                upto(dve, "out_turned", j, G, G + m + 1)
                at = slice(j, j + 1) if isinstance(j, int) else bass.ds(j, 1)
                t = T[:].rearrange("p (j u g) c -> p j u g c", j=J, u=U)[:, at, :, m % 2, :]
                tt(t, t, ps[:, 7, 0:U * C].rearrange("p (u c) -> p u c", u=U).unsqueeze(1),
                   ALU.add).then_inc(S("stream_added"), 1)

            def newton_factors(j):
                dve.tensor_copy(nscoef[:].rearrange("p s a -> p (s a)").unsqueeze(1),
                                con("newton")[0:C].rearrange("p (j n) -> p j n", j=J - 1)[:, bass.ds(j, 1), :]
                                ).then_inc(S("ns_factors"), 1)
                dve.wait_ge(S("ns_factors"), j + 1)

            def newton_y(j, s):
                ts(nsZ[:], ident[0:C, 0:C], nscoef[:, s, 1:2], None, ALU.mult).then_inc(S("nsz_ready"), 1)
                upto(dve, "nsz_ready", j, PAIRS, s + 1)
                upto(dve, "ns_ax", j, PAIRS, s + 1)
                stt(nsY[:], ps[0:C, 6, 0:C], nscoef[:, s, 0:1], nsZ[:], ALU.mult, ALU.add).then_inc(S("nsy_ready"), 1)

            def newton_x(j, s):
                upto(dve, "ns_xy", j, PAIRS, s + 1)
                dve.tensor_copy(nsX[:].rearrange("p a c -> p (a c)"),
                                ps[0:C, 6, C:3 * C]).then_inc(S("nsx_ready"), 1)

            def attention_step(j, k, there):
                in_loop = not isinstance(j, int)
                if k % 4 == 1 and there(k + 3):
                    tokens(j, (k + 3) // 4)
                if there(k + 1):
                    maxima(j, 2 * k + 2)
                if there(k + 2):
                    key_low(j, k + 2)
                if in_loop:
                    newton_y(j, k - 2)
                if there(k + 1):
                    scale_eye(j, 2 * k + 2)
                    maxima(j, 2 * k + 3)
                if k % 4 == 1 and there(k - 2):
                    add_out(j, k // 4 - 1)
                if in_loop:
                    newton_x(j, k - 2)
                if there(k):
                    transposed_copy(dve, j, 2 * k + 1)
                if there(k + 1):
                    scale_eye(j, 2 * k + 3)

            dve.sem_inc(S("stream_added"), G)
            tokens(0, 0)
            attention_steps(dve, attention_step, in_loop=newton_factors)
            dve.wait_ge(S("pinv_done"), 1)
            raw = ps[:, 6, 0:C].rearrange("p (a c) -> p a c", a=2)
            step(dve.tensor_copy(query_or_key(0, 1), raw))
            tt(query_or_key(1, 1), raw, query_or_key(0, 1).bitcast(F32), ALU.subtract).then_inc(S("qkvw_ready"), 2)

            dve.wait_ge(S("stream_added"), G + G * J)
            layer_norm(1)
            gate(0)

            def weigh(which, src, i, k):
                nm = f"f{which}_"
                dve.wait_ge(S(nm + "spread"), i * 8 + (8 + k + 1))
                dve.wait_ge(S(nm + "out_chunk"), i * 8 + (8 + k - 3))
                tt(hid[:, k % 4, :], src[:, k % 2, :], ps[:, 4 + k % 2, :],
                   ALU.mult).then_inc(S(nm + "hid_ready"), 1)

            with dve.Fori(0, EXP2 // 2) as i:
                for k in range(2 * CHUNKS):
                    dve.wait_ge(S("f2_act"), i * 8 + (8 + k + 1))
                    weigh(2, act_out, i, k)
            dve.wait_ge(S("f2_out_chunk"), 8 + CHUNKS * EXP2)
            dve.tensor_copy(sums[:, 1, :], ps[:, 7, :]).then_inc(S("f2_sum_vec"), 1)
            for b in range(2):
                dve.wait_ge(S("f2_turned"), b + 1)
                t = T[:, 8 * b:8 * b + 8, :].rearrange("p (h i) c -> p i h c", h=2)
                step(tt(t, t, ps[:, b, :].rearrange("p (i h c) -> p i h c", i=4, h=2), ALU.add))
            layer_norm(2)
            l3_vector(dve, step, tt, ts, stt)
            layer_norm(3)
            gate(1)
            with dve.Fori(0, EXP3 // 2) as i:
                for k in range(0, 2 * CHUNKS, 2):
                    for kk in (k, k + 1):
                        dve.wait_ge(S("f3_act"), i * 8 + (kk + 1))
                        dve.wait_ge(S("f3_hid_ready"), i * 8 + (8 + kk - 1))
                        tt(glu[:, kk % 2, :], ps[:, 2 + kk % 2, :], act_out[:, kk % 2, :],
                           ALU.mult).then_inc(S("f3_glu"), 1)
                    for kk in (k, k + 1):
                        dve.wait_ge(S("f3_glu"), i * 8 + (8 + kk + 1))
                        weigh(3, glu, i, kk)
            dve.wait_ge(S("f3_out_chunk"), 8 + CHUNKS * EXP3)
            dve.tensor_copy(yfin[:, 512:1024], ps[:, 7, :]).then_inc(S("out_ready"), 1)

def kernel(**inputs):
    import concourse.bacc as bacc
    from concourse.bass_utils import run_bass_kernel_spmd

    a = {k: np.asarray(v) for k, v in inputs.items()}

    def twice(m):
        return np.concatenate([m, m], axis=0)

    def rows(v):
        return np.broadcast_to(v[None, :], (P, v.shape[0]))

    vec = {"bw": a["L0_conv_bw"], "gamma": a["L0_conv_gamma"], "beta": a["L0_conv_beta"]}
    vec.update({n: a["L1_conv_" + n] for n in VECS if n not in vec and n != "bpg_bt"})
    cols = [np.concatenate([a["L0_conv_bp"], a["L0_conv_bg"], a["L0_conv_bt"], np.zeros(IC, np.float32)])]
    cols += [np.concatenate([vec[n], vec[n]]) for n in VECS[1:]]

    def by_head(w, dup):
        t = w.reshape(C, HEADS, C).transpose(2, 1, 0)
        return np.concatenate([t, t], axis=2) if dup else t

    def twice_in(w):
        return np.concatenate([w, w], axis=1)

    def picks(experts):
        e, p = np.arange(experts)[:, None, None], np.arange(P)[None, :, None]
        return (p % C == e).astype(np.float32)

    def expert_rows(*parts):
        w = np.concatenate(parts, axis=2)
        return w.reshape(w.shape[0] * P, -1)

    w3, w1 = a["L1_conv_w3"], a["L1_conv_w1"]
    arrays = {
        "x": a["x"].reshape(G, J, C, N).transpose(0, 2, 1, 3).reshape(P, J * N),
        "w0": twice(np.concatenate([a["L0_conv_Wp"].T, a["L0_conv_Wg"].T, a["L0_conv_Wt"].T], axis=1)),
        "wwT": a["L0_conv_Ww"].T,
        "vec": np.stack(cols, axis=1),
        "w3T": twice(w3.transpose(1, 2, 3, 0).reshape(C, 9, C)),
        "w1T": twice(w1[:, :, 0, 0].T),
        "w3n": twice(w3.reshape(C, C * 9)),
        "w1n": twice(w1.reshape(C, C)),
        "wqT": by_head(a["L2_attn_Wq"], False),
        "wkT": by_head(a["L2_attn_Wk"], True),
        "wvT": by_head(a["L2_attn_Wv"], True),
        "wu": a["L2_attn_Wu"].reshape(HEADS, C, C).transpose(1, 0, 2),
        "bu": rows(a["L2_attn_bu"]),
        "q3": twice(a["L3_attn_W_Q"]),
        "q3T": np.concatenate([a["L3_attn_W_Q"].T] * 2, axis=1),
        "wv3": np.concatenate([a["L3_attn_W_V"]] * 2, axis=1),
        "wo3T": a["L3_attn_W_O"].T,
        "gw2": twice(a["L2_ffn_gate_w"]),
        "gb2": rows(a["L2_ffn_gate_b"]),
        "gw3": twice(a["L3_ffn_gate_w"]),
        "gb3": rows(a["L3_ffn_gate_b"]),
        "f2_in": expert_rows(twice_in(a["L2_ffn_W1"]), picks(EXP2)),
        "f2_out": expert_rows(a["L2_ffn_W2"], a["L2_ffn_b1"][:, :, None]),
        "b2": a["L2_ffn_b2"],
        "f3_in": expert_rows(twice_in(a["L3_ffn_w1"]), twice_in(a["L3_ffn_w2"]), picks(EXP3)),
        "f3_out": expert_rows(a["L3_ffn_w3"]),
        "consts": constants(),
    }
    arrays = {k: np.ascontiguousarray(v) for k, v in arrays.items()}
    nc = bacc.Bacc("TRN2", target_bir_lowering=False, num_devices=1)
    io = {k: nc.dram_tensor(f"in_{k}", v.shape, mybir.dt.from_np(v.dtype), kind="ExternalInput").ap()
          for k, v in arrays.items()}
    out = nc.dram_tensor("out_y", (P, J * N), F32, kind="ExternalOutput").ap()
    hybrid_kernel(nc, io, out)
    r = run_bass_kernel_spmd(nc, [{f"in_{k}": v for k, v in arrays.items()}], core_ids=[0])
    y = r.results[0]["out_y"]
    y = y.reshape(2, C, J // 2, U, G, P).transpose(4, 2, 0, 1, 3, 5)
    return y.reshape(B, C, IMG, IMG)
```

```python
from contextlib import ExitStack
import math

import numpy as np

import concourse.bass as bass
from concourse import mybir

F32 = mybir.dt.float32
F32R = mybir.dt.float32r
BF16 = mybir.dt.bfloat16
ALU = mybir.AluOpType
ACT = mybir.ActivationFunctionType
AX = mybir.AxisListType

P = 128
B, C, IMG = 8, 64, 16
N = IMG * IMG
G, J, U = 2, B // 2, N // P
TILES = B * U
TOK = B * N
IC = 32
POOLED = N // 4
HEADS = 8
EXP2, EXP3, HID = 8, 16, 128
CHUNK = 512
CHUNKS = TOK // CHUNK
CT = CHUNK // P
BLK = 32
NB = N // BLK
LEVELS = 3
THETA = 10000.0
PAD = IMG + 2
EPS_BN, EPS_LN, EPS_VAR, EPS_L2 = 1e-5, 1e-5, 1e-6, 1e-8
PAIRS = G * HEADS // 2
NEWTON = (J - 1) * PAIRS
HIDDEN_SCORE = -30000.0

VECS = ["bpg", "bt", "bw", "gamma", "beta", "b11", "b12", "b13", "b21", "b22", "b23",
        "g1", "be1", "m1", "v1", "g2", "be2", "m2", "v2", "a1", "a2"]
VI = {n: i for i, n in enumerate(VECS)}

CONSTS = [("ident", P), ("halfavg", P), ("cos", 256), ("sin", 256), ("lower", P), ("expand", U * P),
          ("basis", U * NB), ("inblock", U * P), ("own", U * NB), ("below", U * NB),
          ("count", U * 9), ("share", U * 9), ("mask", U * 9), ("scale", U), ("sameb", B), ("fold", C), ("newton", 2 * NEWTON)]
CO, _at = {}, 0
for _n, _w in CONSTS:
    CO[_n] = (_at, _w)
    _at += _w
NCONST = _at


def newton_scales():
    low = (10 * C * np.finfo(np.float32).eps) ** 2 / C
    scales = []
    for _ in range(NEWTON):
        scale = 2.0 / (1.0 + max(low, 1e-2)) if low < 0.9 else 1.0
        scales.append(scale)
        low = min(scale * v * (2.0 - scale * v) for v in (low, 1.0))
    assert low > 1 - 1e-7
    return np.array(scales)


def constants():
    out = np.zeros((P, NCONST), np.float32)

    def put(name, a):
        at, w = CO[name]
        a = np.asarray(a, np.float32)
        out[:a.shape[0], at:at + w] = a.reshape(a.shape[0], w)

    put("ident", np.eye(P))
    p = np.arange(P)
    put("halfavg", 0.5 * (p[:, None] % C == p[None, :] % C))
    half = C // 2
    inv_freq = 1.0 / THETA ** (np.arange(half, dtype=np.float32) / half)
    ang = np.arange(N, dtype=np.float32)[:, None] * inv_freq[None, :].astype(np.float32)

    def rope(t):
        t = t.astype(np.float32).reshape(U, P, 1, half).repeat(4, axis=2)
        return t.transpose(1, 0, 2, 3)
    put("cos", rope(np.cos(ang)))
    put("sin", rope(np.sin(ang)))
    put("lower", (p[:, None] // BLK == p[None, :] // BLK) & (p[:, None] < p[None, :]))
    tok = np.arange(N)
    blk = tok // BLK
    onehot = (blk[:, None] == np.arange(NB)[None, :]).astype(np.float32)
    put("expand", onehot.T)
    haar = []
    for level in range(LEVELS):
        size = N // 2 ** level
        for k in range(2 ** level):
            v = np.zeros(N)
            v[k * size:k * size + size // 2] = 1 / math.sqrt(size // 2)
            v[k * size + size // 2:(k + 1) * size] = -1 / math.sqrt(size // 2)
            haar.append(v)
    haar = np.stack(haar, 1)

    def by_tile(a):
        return np.asarray(a, np.float32).reshape(U, P, -1).transpose(1, 0, 2)
    put("basis", by_tile(haar @ haar[::BLK].T))
    put("inblock", by_tile(np.tile(onehot, (1, U * B))))
    put("own", by_tile(onehot))
    put("below", by_tile(np.arange(NB)[None, :] < blk[:, None]))
    count = np.zeros((N, 9), np.float32)
    count[:, :NB] = np.clip(tok[:, None] - BLK * np.arange(NB)[None, :], 0, BLK)
    count[:, NB] = 1
    put("count", by_tile(count))
    put("mask", by_tile(np.where(count > 0, 0.0, HIDDEN_SCORE)))
    put("share", by_tile(count / (tok[:, None] + 1.0)))
    put("sameb", p[:, None] // NB % B == np.arange(B)[None, :])
    put("fold", p[:, None] % C == np.arange(C)[None, :])
    f = newton_scales()
    put("newton", np.tile(np.stack([-f * f, 2 * f], axis=1).reshape(1, -1), (P, 1)))
    put("scale", by_tile(1.0 / np.sqrt(float(C)) / np.sqrt(tok + 1.0)))
    return out


def hybrid_kernel(nc, io, out):
    ctx = ExitStack()
    with ctx:
        def sb(name, shape, dt=F32):
            return ctx.enter_context(nc.sbuf_tensor(name, shape, dt))

        sems = {}

        def S(name):
            if name not in sems:
                sems[name] = ctx.enter_context(nc.semaphore(name))
            return sems[name]

        consts = sb("consts", [P, NCONST])
        vec = sb("vec", [P, len(VECS)])

        def con(name):
            at, w = CO[name]
            return consts[:, at:at + w]

        def v_(name):
            return vec[:, VI[name]:VI[name] + 1]

        ident = con("ident")
        x0 = sb("x0", [P, J * N])
        w0 = sb("w0", [P, 2 * P])
        wwT = sb("wwT", [P, P])
        theta_qk = sb("theta_qk", [P, TOK])
        theta = theta_qk[:, 0:J * N]
        QK = theta_qk[:, :].rearrange("p (a t h c) -> p a t h c", a=2, t=TILES, h=2)
        probT_rot = sb("probT_rot", [P, TOK])
        probT = probT_rot[:, 0:J * N]
        squares = probT_rot[:, :].rearrange("p (a t h c) -> p a t h c", a=2, t=TILES, h=2)
        pooled = sb("pooled", [P, J, POOLED])
        pg_vsum = sb("pg_vsum", [P, B, C])
        pg = pg_vsum[:].rearrange("p (j d) m -> p j d m", d=2)
        phi = sb("phi", [P, J, G, POOLED])
        gw = sb("gw", [P, J, G, C])
        f_both = sb("f_both", [P, 2, TILES, POOLED])
        f_sub, f_exp = f_both[:, 0], f_both[:, 1]
        R = f_both[:, :].rearrange("p a t (h c) -> p (a t h c)", h=2).rearrange(
            "p (t h a c) -> p t h a c", t=TILES, h=2, a=2)
        f_prob = sb("f_prob", [P, TILES, POOLED])
        f_col = sb("f_col", [P, 3, TILES])
        wy = sb("wy", [P, J * N])
        bn6 = sb("bn6", [P, 2, 6])
        col = sb("col", [P, 64])
        x1 = sb("x1", [P, J * N])
        sgn = sb("sgn", [P, J, PAD, PAD], BF16)
        sgn2 = sb("sgn2", [P, J * N], BF16)
        w3T = sb("w3T", [P, 9, C])
        w1T = sb("w1T", [P, C])
        w3n = sb("w3n", [P, C * 9])
        w1n = sb("w1n", [P, C])
        w3s = sb("w3s", [P, 9, P], BF16)
        w1s = sb("w1s", [P, P], BF16)
        va_vb = sb("va_vb", [P, 2 * J * N])
        va, vb = va_vb[:, 0:J * N], va_vb[:, J * N:2 * J * N]
        prob = va_vb[:].rearrange("p (k u n) -> p k u n", k=4, u=U)
        r1 = sb("r1", [P, J * N])
        x2 = sb("x2", [P, J * N])

        T = sb("T", [P, TILES, C])
        ln6 = sb("ln6", [P, TILES, 6])
        lnc = sb("lnc", [P, 8, TILES])
        xn = sb("xn", [P, TILES, C])
        XS = sb("XS", [P, TILES * P], F32R)

        wqT = sb("wqT", [C, HEADS, C])
        wkvT = sb("wkvT", [C, 2, HEADS, P])
        wkT, wvT = wkvT[:, 0], wkvT[:, 1]
        wu = sb("wu", [C, HEADS, C])
        bu = sb("bu", [P, C])
        AH = sb("AH", [P, HEADS, 2, C], F32R)
        AL = sb("AL", [P, HEADS, 2, C], F32R)
        GH = sb("GH", [P, HEADS * C], F32R)
        GL = sb("GL", [P, HEADS * C], F32R)
        xcur = sb("xcur", [P, G, U * P], F32R)
        keys_gates = sb("keys_gates", [P, TOK], F32R)
        KH, KL = (keys_gates[:, s * 4 * N:(s + 1) * 4 * N].rearrange("p (k h n) -> p k h n", k=2, h=2)
                  for s in range(2))
        vproj = sb("vproj", [P, G, U, HEADS * C])
        negmax = sb("negmax", [P, 4, U])
        rowsum = sb("rowsum", [P, 4, U])
        rowinv = sb("rowinv", [P, 4, U])
        scaled_eye = sb("scaled_eye", [P, 2, U, P])
        pT = sb("pT", [P, 4, U, N])
        outT = sb("outT", [P, N])

        nsA = sb("nsA", [C, C])
        nsAT = sb("nsAT", [C, C])
        nsX = sb("nsX", [C, 2, C])
        nsY = sb("nsY", [C, C])
        nsZ = sb("nsZ", [C, C])
        nscoef = sb("nscoef", [C, PAIRS, 2])
        nsc = sb("nsc", [C, 4])
        zeros = sb("zeros", [P, HID])
        ones64 = sb("ones64", [C, C])
        eyedup = sb("eyedup", [C, P])

        gw2 = sb("gw2", [P, EXP2])
        gb2 = sb("gb2", [P, EXP2])
        gw3 = sb("gw3", [P, EXP3])
        gb3 = sb("gb3", [P, EXP3])
        logit = sb("logit", [P, TILES, EXP3])
        top8 = sb("top8", [P, TILES, 8])
        gexp = w3n[:, TILES * EXP3:2 * TILES * EXP3].rearrange("p (t e) -> p t e", e=EXP3)
        gsel = w3n[:, 0:TILES * EXP3].rearrange("p (t e) -> p t e", e=EXP3)
        gates = sb("gates", [P, TILES, C])
        gcol = sb("gcol", [P, 2, TILES])
        b2two = sb("b2two", [P, C])

        in2, in3 = sb("in2", [P, 2, HID + 1]), sb("in3", [P, 2, 2 * HID + 1])
        out2, out3 = sb("out2", [P, 2, C + 1]), sb("out3", [P, 2, C])
        wp1 = sb("wp1", [P, 2, 2, HID], F32R)
        wp2 = sb("wp2", [P, 2, 2, HID], F32R)
        pick = sb("pick", [P, 2, HID], F32R)
        gatesT = keys_gates
        act_out = wy[:].rearrange("p (a n) -> p a n", a=2)
        glu = x0[:].rearrange("p (a n) -> p a n", a=2)
        hid = probT_rot[:].rearrange("p (a n) -> p a n", a=4)
        sums = x0[:].rearrange("p (a n) -> p a n", a=2)

        wv3 = sb("wv3", [C, P])
        wo3T = sb("wo3T", [C, C])
        wq3 = sb("wq3", [P, C])
        qkvw = sb("qkvw", [P, 2, 192], F32R)
        m_a, m_b, m_c, m_d = va, vb, r1, x1
        V3 = f_prob
        basis2 = sb("basis2", [P, TILES, 2, NB])
        q8 = sb("q8", [C, B, NB])
        k8 = sb("k8", [C, B, NB])
        F8 = sb("F8", [NB, B * NB])
        a9 = sb("a9", [P, U, B, 9])
        z9 = sb("z9", [P, U, B, 9])
        e9 = sb("e9", [P, U, B, 9])
        t9 = sb("t9", [P, U, B, 9])
        s9 = sb("s9", [P, 8, U, B])
        dcol = sb("dcol", [P, 2, TILES])
        n2 = sb("n2", [P, 3, TILES * 2])
        pown = sb("pown", [P, TILES])
        pdia = sb("pdia", [P, TILES])
        p8 = sb("p8", [P, U, B, NB])
        p8T = sb("p8T", [P, P])
        vsum = pg_vsum
        yfin = x2

        ps = ctx.enter_context(nc.psum_tensor("ps", [P, 8, 512], F32))

        def banks(a, b):
            return ps[:, a:b, :].rearrange("p a n -> p (a n)")

        def upto(eng, name, j, a_round, more):
            if isinstance(j, int) and j * a_round + more <= 0:
                return
            eng.wait_ge(S(name), j * a_round + more)

        def expert_rounds(eng, experts, pair):
            with eng.Fori(0, experts // 2 - 1) as i:
                for k in range(0, 2 * CHUNKS, 2):
                    pair(i, k, lambda chunk: True)
            for k in range(0, 2 * CHUNKS, 2):
                pair(experts // 2 - 1, k, lambda chunk: chunk < 2 * CHUNKS)

        def attention_steps(eng, step, in_loop=None):
            for k in range(-2, 2):
                step(0, k, lambda pair: pair >= 0)
            with eng.Fori(0, J - 1) as j:
                if in_loop:
                    in_loop(j)
                for k in range(2, 2 + PAIRS):
                    step(j, k, lambda pair: True)
            for k in range(2, 2 + PAIRS):
                step(J - 1, k, lambda pair: pair < PAIRS)

        def step_of(eng, name):
            done = [0]

            def step(ins):
                done[0] += 1
                ins.then_inc(S(name), 1)
                eng.wait_ge(S(name), done[0])
            return step

        block = ctx.enter_context(nc.Block())

        def split_high(act, stack, bank, p, signal):
            for odd in range(2):
                h = slice(C * odd, C * odd + C)
                act.activation(tiles_of(stack, p, odd)[h], ps[h, bank, 0:2 * P].rearrange("p (t n) -> p t n", n=P),
                               ACT.Copy).then_inc(S(signal), 1)

        def split_low(dve, stack, bank, p, high, so_far, signal):
            for odd in range(2):
                h, o = slice(C * odd, C * odd + C), slice(C * (1 - odd), C * (1 - odd) + C)
                dve.wait_ge(S(high), so_far + 2 * p + odd + 1)
                ins = dve.tensor_tensor(tiles_of(stack, p, odd)[o], ps[h, bank, 0:2 * P].rearrange("p (t n) -> p t n", n=P),
                                        tiles_of(stack, p, odd)[h].bitcast(F32), ALU.subtract)
            ins.then_inc(S(signal), 1)

        def tiles_of(stack, p, odd):
            return stack[:, p * CHUNK:(p + 1) * CHUNK].rearrange("p (t o n) -> p t o n", o=2, n=P)[:, :, odd, :]

        @block.sync
        def _(sp):
            def load(dst, src, name):
                sp.dma_start(dst, src).then_inc(S(name), 16)

            load(w0[:], io["w0"], "l0_loaded")
            load(x0[:], io["x"], "l0_loaded")
            load(vec[:], io["vec"], "vec_loaded")
            load(wwT[:], io["wwT"], "ww_loaded")
            load(w3T[:], io["w3T"], "l1_loaded")
            load(w1T[:], io["w1T"], "l1_loaded")
            load(w3n[:], io["w3n"], "l1_loaded")
            load(w1n[:], io["w1n"], "l1_loaded")
            load(nsA[:], io["q3"][0:C, :], "ns_loaded")
            load(nsAT[:], io["q3T"], "ns_loaded")
            load(consts[:], io["consts"], "consts_loaded")
            load(wqT[:], io["wqT"], "attn_loaded")
            load(wkT[:], io["wkT"], "attn_loaded")
            load(wvT[:], io["wvT"], "attn_loaded")
            load(wu[:], io["wu"], "attn_loaded")
            load(bu[:], io["bu"], "bu_loaded")
            load(wq3[:], io["q3"], "l3_loaded")
            load(wv3[:], io["wv3"], "l3_loaded")
            load(wo3T[:], io["wo3T"], "l3_loaded")
            load(gw2[:], io["gw2"], "gate_loaded")
            load(gb2[:], io["gb2"], "gate_loaded")
            load(gw3[:], io["gw3"], "gate_loaded")
            load(gb3[:], io["gb3"], "gate_loaded")
            sp.wait_ge(S("b2_zeroed"), 1)
            for half in range(2):
                load(b2two[C * half:C * half + EXP2, :], io["b2"], "b2_loaded")
            for which, experts, w_in, w_out, n in ((2, EXP2, in2, out2, 2), (3, EXP3, in3, out3, 3)):
                nm = f"f{which}_"
                sp.sem_inc(S(nm + "w_split"), 2 * n)
                sp.sem_inc(S(nm + "out_chunk"), 8)
                with sp.Fori(0, experts // 2) as i:
                    for e in range(2):
                        rows = bass.ds(i * (2 * P) + e * P, P)
                        sp.wait_ge(S(nm + "w_split"), i * (2 * n) + n * (e + 1))
                        sp.dma_start(w_in[:, e, :], io[nm + "in"][rows, :]).then_inc(S(nm + f"in{e}"), 16)
                        sp.wait_ge(S(nm + "out_chunk"), i * 8 + 4 * (e + 1))
                        sp.dma_start(w_out[:, e, :], io[nm + "out"][rows, :]).then_inc(S(nm + f"out{e}"), 16)
            for half in range(2):
                sp.wait_ge(S(("out_ready_act", "out_ready_vec")[half]), 1)
                s = slice(half * 512, (half + 1) * 512)
                sp.dma_start(out[:, s], yfin[:, s]).then_inc(S("stored"), 16)
            sp.wait_ge(S("stored"), 32)

        def ffn(gp, which):
            experts, w_in, parts = {2: (EXP2, in2, [wp1]), 3: (EXP3, in3, [wp1, wp2])}[which]
            nm = f"f{which}_"
            n = len(parts)
            with gp.Fori(0, experts // 2) as i:
                for e in range(2):
                    gp.wait_ge(S(nm + "spread"), i * 8 + 4 * (e + 1))
                    gp.wait_ge(S(nm + f"in{e}"), i * 16 + 16)
                    gp.tensor_tensor(pick[:, e, :], zeros[:],
                                     w_in[:, e, n * HID:n * HID + 1].broadcast_to([P, HID]),
                                     ALU.add).then_inc(S(nm + "w_split"), 1)
                    for k, part in enumerate(parts):
                        src = w_in[:, e, k * HID:(k + 1) * HID]
                        gp.tensor_tensor(part[:, e, 0, :], src, zeros[:], ALU.add).then_inc(S(nm + "w_high"), 1)
                        gp.wait_ge(S(nm + "w_high"), i * (2 * n) + (n * e + k + 1))
                        gp.tensor_tensor(part[:, e, 1, :], src, part[:, e, 0, :].bitcast(F32),
                                         ALU.subtract).then_inc(S(nm + "w_split"), 1)

        def ln_pool(gp, n):
            gp.wait_ge(S("ln_mean"), n + 1)
            gp.tensor_tensor(xn[:, 8:16], T[:, 8:16], lnc[:, 1, 8:16].unsqueeze(2).broadcast_to([P, 8, C]),
                             ALU.subtract).then_inc(S("ln_centred"), 1)

        def projection_bank(q):
            return (q // 2 + 4) % 8

        def by_round(a, half):
            return a[:, half * 512:(half + 1) * 512].rearrange("p (j r) -> p j r", j=J // 2)

        def queries_keys(a, half):
            return QK[:, a, 8 * half:8 * half + 8].rearrange("p (j r) h c -> p j (r h c)", j=J // 2)

        def rotary(name):
            return con(name).unsqueeze(1).broadcast_to([P, J // 2, 256])

        def l3_pool(gp):
            gp.wait_ge(S("consts_loaded"), 16)
            for half in range(2):
                gp.wait_ge(S("qk_evac"), 4 * (half + 1))
                gp.tensor_tensor(by_round(m_b, half), queries_keys(1, half), rotary("sin"),
                                 ALU.mult).then_inc(S("rope_pool"), 1)
                gp.tensor_tensor(by_round(m_c, half), queries_keys(0, half), rotary("sin"),
                                 ALU.mult).then_inc(S("rope_pool"), 1)
            gp.wait_ge(S("pdia_ready"), 1)
            gp.tensor_tensor(m_d[:].rearrange("p (t c) -> p t c", c=C), V3[:],
                             pdia[:].unsqueeze(2).broadcast_to([P, TILES, C]),
                             ALU.mult).then_inc(S("diag_done"), 1)

        @block.gpsimd
        def _(gp):
            gp.memset(phi[:], 0.0).then_inc(S("blocks_zeroed"), 1)
            gp.memset(gw[:], 0.0).then_inc(S("blocks_zeroed"), 1)
            gp.memset(sgn[:], 0.0).then_inc(S("pads_zeroed"), 1)
            gp.memset(w3s[:], 0.0).then_inc(S("pads_zeroed"), 1)
            gp.memset(w1s[:], 0.0).then_inc(S("pads_zeroed"), 1)
            gp.memset(zeros[:], 0.0).then_inc(S("zeros_ready"), 1)
            gp.wait_ge(S("zeros_ready"), 1)
            gp.memset(ones64[:], 1.0).then_inc(S("ones_ready"), 1)
            gp.memset(b2two[:], 0.0).then_inc(S("b2_zeroed"), 1)
            gp.memset(gates[:], 0.0).then_inc(S("gates_zeroed"), 1)
            gp.wait_ge(S("bu_loaded"), 16)
            ln_pool(gp, 0)
            gp.wait_ge(S("ln_normalised"), 4)
            for u in range(2):
                t8 = T[:, 8 * u:8 * u + 8, :]
                gp.tensor_tensor(t8, t8, bu[:].unsqueeze(1).broadcast_to([P, 8, C]),
                                 ALU.add).then_inc(S("t_biased"), 1)
            ln_pool(gp, 1)
            ffn(gp, 2)
            ln_pool(gp, 2)
            l3_pool(gp)
            ln_pool(gp, 3)
            ffn(gp, 3)

        def stream_half(b):
            return T[:, 8 * b:8 * b + 8, :].rearrange("p (h i) c -> p i h c", h=2)

        def turned_half(b):
            return ps[:, b, :].rearrange("p (i h c) -> p i h c", i=4, h=2)

        def ln_act(act, n, table_after=None):
            act.wait_ge(S("ln_var"), n + 1)
            act.activation(lnc[:, 6, :], lnc[:, 5, :], ACT.Sqrt).then_inc(S("ln_std"), 1)
            if table_after:
                act.preload_act_table(table_after)
            for p in range(4):
                act.wait_ge(S("ln_transposed"), 4 * n + p + 1)
                split_high(act, XS, p, p, "ln_high")

        def gate_act(act, n, first_chunks):
            experts = (EXP2, EXP3)[n]
            act.wait_ge(S("gate_shifted"), n + 1)
            act.activation(gexp[:, :, 0:experts], logit[:, :, 0:experts],
                           ACT.Exp).then_inc(S("gate_exp"), 1)
            act.preload_act_table((ACT.Gelu, ACT.Silu)[n])
            for k in range(2):
                first_chunks(0, k)
            for p in range(4):
                act.wait_ge(S("gates_transposed"), 4 * n + p + 1)
                split_high(act, gatesT, 4 + p % 2, p, "gates_high")

        def transposed_copy(eng, j, n):
            upto(eng, "p_turned", j, 2 * PAIRS, n + 1)
            upto(eng, "pv_done", j, PAIRS, PAIRS + n // 2 - 1)
            dst = pT[:, n % 4].rearrange("p u n -> p (u n)")
            src = ps[:, 3 + n % 2, :]
            if n % 2 == 0:
                eng.activation(dst, src, ACT.Copy).then_inc(S("pT_even"), 1)
            else:
                eng.tensor_copy(dst, src).then_inc(S("pT_odd"), 1)

        def attention_act(act):
            def key_high(j, k):
                upto(act, "k_projected", j, PAIRS, k + 1)
                upto(act, "scores_ready", j, 2 * PAIRS, 2 * k - 2)
                act.activation(KH[:, k % 2].rearrange("p h n -> p (h n)"), ps[:, 0, :],
                               ACT.Copy).then_inc(S("kh_ready"), 1)

            def exponentials(j, n):
                upto(act, "max_ready", j, 2 * PAIRS, n + 1)
                upto(act, "p_turned", j, 2 * PAIRS, n - 3)
                for u in range(U):
                    ins = act.activation(prob[:, n % 4, u, :], ps[:, 1 + n % 2, u * N:(u + 1) * N], ACT.Exp,
                                         bias=negmax[:, n % 4, u:u + 1], accum_out=rowsum[:, n % 4, u:u + 1])
                ins.then_inc(S("probs_ready"), 1)

            def value_copy(j, m, u):
                upto(act, "v_projected", j, G * U, U * m + u + 1)
                upto(act, "pv_done", j, PAIRS, PAIRS + 4 * m - 4)
                act.activation(vproj[:, m % 2, u, :], ps[:, 7, :], ACT.Copy).then_inc(S("v_ready"), 1)

            def out_copy(j, m):
                upto(act, "pv_done", j, PAIRS, PAIRS + 4 * m + 4)
                upto(act, "out_turned", j, G, G + m)
                act.activation(outT[:], ps[:, 5, 0:N], ACT.Copy).then_inc(S("outT_ready"), 1)

            def step(j, k, there):
                if there(k + 2):
                    key_high(j, k + 2)
                if there(k + 1):
                    exponentials(j, 2 * k + 2)
                if there(k):
                    transposed_copy(act, j, 2 * k)
                if k % 4 == 3 and there(k + 1):
                    value_copy(j, (k + 1) // 4, 0)
                if k % 4 == 0 and there(k):
                    value_copy(j, k // 4, 1)
                if there(k + 1):
                    exponentials(j, 2 * k + 3)
                if k % 4 == 0 and there(k - 1):
                    out_copy(j, k // 4 - 1)

            attention_steps(act, step)

        @block.scalar
        def _(act):
            act.sem_inc(S("f2_act"), 8)
            act.wait_ge(S("vec_loaded"), 16)
            for p in range(2):
                act.wait_ge(S("l0_projected"), p + 3)
                act.activation(theta[:, p * 512:(p + 1) * 512], ps[:, 2 + p, :], ACT.Identity,
                               bias=v_("bt")).then_inc(S("theta_ready"), 1)
            act.wait_ge(S("l1_loaded"), 64)
            act.wait_ge(S("pads_zeroed"), 3)
            for g in range(G):
                h = slice(C * g, C * g + C)
                act.activation(w3s[h, :, h], w3T[h], ACT.Sign).then_inc(S("wsign_ready"), 1)
                act.activation(w1s[h, h], w1T[h], ACT.Sign).then_inc(S("wsign_ready"), 1)
            for half in range(2):
                act.wait_ge(S("f_shifted"), half + 1)
                act.activation(f_exp[:, 8 * half:8 * half + 8], f_sub[:, 8 * half:8 * half + 8],
                               ACT.Exp).then_inc(S("f_exp_ready"), 1)
            act.wait_ge(S("folded"), 1)
            for d in range(2):
                act.activation(AH[:, :, d, :], ps[:, 7, :].rearrange("p (h c) -> p h c", c=C), ACT.Copy,
                               scale=1.0 / math.sqrt(C)).then_inc(S("fold_high"), 1)
            act.wait_ge(S("f_transposed"), 1)
            act.activation(probT[:, 0:512], ps[:, 0, :], ACT.Copy).then_inc(S("probT_act"), 1)
            for p in range(2):
                act.wait_ge(S("wy_ready"), p + 1)
                act.activation(wy[:, p * 512:(p + 1) * 512], ps[:, 4 + p, :], ACT.Identity,
                               bias=v_("bw")).then_inc(S("wy_evac"), 1)
            act.wait_ge(S("bn_var_ready"), 1)
            act.activation(col[:, 11:14], col[:, 8:11], ACT.Sqrt).then_inc(S("bn_std_ready"), 1)
            for p in range(2):
                act.wait_ge(S("x1_ready"), p + 1)
                act.activation(sgn[:, 2 * p:2 * p + 2, 1:1 + IMG, 1:1 + IMG],
                               x1[:, p * 512:(p + 1) * 512].rearrange("p (j h w) -> p j h w", j=2, h=IMG),
                               ACT.Sign, bias=v_("b11")).then_inc(S("sgn_ready"), 1)
            act.wait_ge(S("folded"), 2)
            act.activation(GH[:], ps[:, 3, :], ACT.Copy).then_inc(S("fold_high"), 1)

            def positive(p, so_far):
                s = slice(p * 512, (p + 1) * 512)
                act.wait_ge(S("prelu_in"), so_far + p + 1)
                act.activation(vb[:, s], va[:, s], ACT.Relu).then_inc(S("positive_ready"), 1)

            for p in range(2):
                positive(p, 0)
                act.wait_ge(S("r1_ready"), p + 1)
                act.activation(sgn2[:, p * 512:(p + 1) * 512], r1[:, p * 512:(p + 1) * 512],
                               ACT.Sign, bias=v_("b21")).then_inc(S("sgn2_ready"), 1)
                act.activation(va[:, p * 512:(p + 1) * 512], r1[:, p * 512:(p + 1) * 512],
                               ACT.Identity, bias=col[:, 37:38]).then_inc(S("r1_shifted"), 1)
            for p in range(2):
                positive(p, 2)
            act.wait_ge(S("x2_transposed"), 1)
            act.activation(T[:, 0:8, :].rearrange("p t c -> p (t c)"), ps[:, 4, :],
                           ACT.Copy).then_inc(S("T_act"), 1)
            ln_act(act, 0, ACT.Exp)
            attention_act(act)
            ln_act(act, 1, ACT.Exp)

            def gelu(i, k):
                e = (k // CHUNKS) % 2
                act.wait_ge(S("f2_h_ready"), i * 8 + (k + 1))
                act.wait_ge(S("f2_hid_ready"), i * 8 + (8 + k - 1))
                act.wait_ge(S(f"f2_out{e}"), i * 16 + 16 * (k // 8 + 1))
                act.activation(act_out[:, k % 2, :], ps[:, k % 2, :], ACT.Gelu,
                               bias=out2[:, e, C:C + 1]).then_inc(S("f2_act"), 1)

            def silu(i, k):
                act.wait_ge(S("f3_h_ready"), i * 8 + (k + 1))
                act.wait_ge(S("f3_glu"), i * 8 + (8 + k - 1))
                act.activation(act_out[:, k % 2, :], ps[:, k % 2, :],
                               ACT.Silu).then_inc(S("f3_act"), 1)

            def two_ahead(function):
                def pair(i, k, there):
                    for kk in (k + 2, k + 3):
                        if there(kk):
                            function(i, kk)
                return pair

            gate_act(act, 0, gelu)
            expert_rounds(act, EXP2, two_ahead(gelu))
            act.wait_ge(S("f2_out_chunk"), 8 + CHUNKS * EXP2 - 2)
            act.activation(sums[:, 0, :], ps[:, 6, :], ACT.Copy).then_inc(S("f2_sum_act"), 1)
            act.wait_ge(S("f2_turned"), 1)
            act.activation(stream_half(0), turned_half(0), ACT.Copy).then_inc(S("T_act"), 2)
            ln_act(act, 2)
            for q in range(0, TILES, 2):
                act.wait_ge(S("qkv_ready"), q // 2 + 1)
                z = ps[:, projection_bank(q), 0:384].rearrange("p (g c) -> p g c", g=2)
                act.activation(QK[:, :, q:q + 2].rearrange("p a t h c -> p t a (h c)"),
                               z[:, :, 0:P].rearrange("p g (a c) -> p g a c", a=2),
                               ACT.Copy).then_inc(S("qk_evac"), 1)
                act.activation(squares[:, :, q:q + 2].rearrange("p a t h c -> p t a (h c)"),
                               z[:, :, 0:P].rearrange("p g (a c) -> p g a c", a=2),
                               ACT.Square).then_inc(S("squared"), 1)
            act.wait_ge(S("n2_ready"), 2)
            act.activation(n2[:, 1, :], n2[:, 0, :], ACT.Sqrt).then_inc(S("norm_ready"), 1)
            act.wait_ge(S("qk8_ready"), 1)
            both = ps[:, 0, 0:B * NB].rearrange("p (b n) -> p b n", n=NB)
            act.activation(q8[:], both[0:C],
                           ACT.Copy).then_inc(S("qk8_evac"), 1)
            act.activation(k8[:], both[C:P],
                           ACT.Copy).then_inc(S("qk8_evac"), 1)
            act.wait_ge(S("F8_ready"), 1)
            act.activation(F8[:], ps[0:NB, 1, 0:64], ACT.Copy).then_inc(S("F8_evac"), 1)
            act.wait_ge(S("a_var_ready"), 1)
            act.activation(s9[:, 3], s9[:, 2], ACT.Sqrt).then_inc(S("a_std_ready"), 1)
            act.wait_ge(S("z_ready"), 1)
            act.activation(e9[:], z9[:], ACT.Exp).then_inc(S("e9_ready"), 1)
            act.wait_ge(S("p8T_ready"), 1)
            act.activation(p8T[:], ps[:, 4, 0:P], ACT.Copy).then_inc(S("p8T_evac"), 1)
            ln_act(act, 3, ACT.Exp)
            gate_act(act, 1, silu)
            expert_rounds(act, EXP3, two_ahead(silu))
            act.wait_ge(S("f3_out_chunk"), 8 + CHUNKS * EXP3 - 2)
            act.activation(yfin[:, 0:512], ps[:, 6, :], ACT.Copy).then_inc(S("out_ready_act"), 1)

        def keep_clock(pe, bank, products):
            for _ in range(products):
                pe.matmul(ps[:, bank, :], w3s[:, 0, :], sgn2[:, 0:512], start=True, stop=True)

        def ln_pe(pe, n):
            for p in range(4):
                pe.wait_ge(S("ln_normalised"), 4 * n + p + 1)
                for t in range(2):
                    q = CT * p + 2 * t
                    mm = pe.transpose(ps[:, p, t * P:(t + 1) * P],
                                      xn[:, q:q + 2].rearrange("p t c -> p (t c)"), ident)
                mm.then_inc(S("ln_transposed"), 1)

        def gate_pe(pe, n):
            experts, weight = ((EXP2, gw2), (EXP3, gw3))[n]
            pe.wait_ge(S("gate_loaded"), 64)
            for q in range(TILES):
                if q % 4 == 0:
                    pe.wait_ge(S("ln_low"), 4 * (2 * n + 1) + q // 4 + 1)
                for h in range(2):
                    tokens = slice(q * P + h * C, q * P + (h + 1) * C)
                    mm = pe.matmul(ps[h * C:(h + 1) * C, 4 + q // 8, (q % 8) * experts:(q % 8 + 1) * experts],
                                   XS[:, tokens].bitcast(F32), weight[:], start=True, stop=True)
                if q % 8 == 7:
                    mm.then_inc(S("gate_logits"), 1)

        def gates_pe(pe, n, between):
            pe.wait_ge(S("gates_ready"), n + 1)
            for p in range(4):
                if p == 2:
                    between()
                if p >= 2:
                    pe.wait_ge(S("gates_low"), 4 * n + p - 1)
                for t in range(2):
                    q = CT * p + 2 * t
                    mm = pe.transpose(ps[:, 4 + p % 2, t * P:(t + 1) * P],
                                      gates[:, q:q + 2].rearrange("p t c -> p (t c)"), ident)
                mm.then_inc(S("gates_transposed"), 1)

        def attention_pe(pe):
            def keys(j, k):
                upto(pe, "xcur_ready", j, G, k // 4 + 1)
                upto(pe, "kl_ready", j, PAIRS, k)
                g = (k // 4) % 2
                for h in range(2):
                    o = ps[:, 0, h * N:(h + 1) * N]
                    head = 2 * (k % 4) + h
                    pe.matmul(o, AH[:, head].rearrange("p d c -> p (d c)"), xcur[:, g, :], start=True, stop=False)
                    mm = pe.matmul(o, AL[:, head].rearrange("p d c -> p (d c)"), xcur[:, g, :],
                                   start=False, stop=True)
                mm.then_inc(S("k_projected"), 1)

            def value(j, m, u):
                g = m % 2
                if u == 0:
                    upto(pe, "stream_added", j, G, G + m - 1)
                upto(pe, "v_ready", j, G * U, U * m + u)
                x = xcur[:, g, u * P:(u + 1) * P]
                pe.matmul(ps[:, 7, :], x, GH[:], start=True, stop=False)
                pe.matmul(ps[:, 7, :], x, GL[:], start=False, stop=True).then_inc(S("v_projected"), 1)

            def scores(j, n):
                g, k = (n // 8) % 2, n // 2
                upto(pe, "kl_ready", j, PAIRS, k + 1)
                upto(pe, "probs_ready", j, 2 * PAIRS, n - 1)
                for u in range(U):
                    for part, K in enumerate((KH, KL)):
                        mm = pe.matmul(ps[:, 1 + n % 2, u * N:(u + 1) * N], xcur[:, g, u * P:(u + 1) * P],
                                       K[:, k % 2, n % 2, :], start=(part == 0), stop=(part == 1))
                mm.then_inc(S("scores_ready"), 1)

            def turn(j, n):
                upto(pe, "eye_scaled", j, 2 * PAIRS, n + 1)
                upto(pe, ("pT_even", "pT_odd")[n % 2], j, PAIRS, n // 2)
                for su in range(U):
                    for u in range(U):
                        mm = pe.matmul(ps[:, 3 + n % 2, su * N + u * P:su * N + (u + 1) * P],
                                       prob[:, n % 4, u, su * P:(su + 1) * P], scaled_eye[:, n % 2, u, :],
                                       start=True, stop=True)
                mm.then_inc(S("p_turned"), 1)

            def products(j, k):
                g = (k // 4) % 2
                upto(pe, "pT_even", j, PAIRS, k + 1)
                upto(pe, "pT_odd", j, PAIRS, k + 1)
                upto(pe, "v_ready", j, G * U, U * (k // 4 + 1))
                if k % 4 == 0:
                    upto(pe, "outT_ready", j, G, k // 4)
                for su in range(U):
                    for h in range(2):
                        head = 2 * (k % 4) + h
                        mm = pe.matmul(ps[h * C:(h + 1) * C, 5, 0:N], vproj[:, g, su, head * C:(head + 1) * C],
                                       pT[:, (2 * k + h) % 4, su, :], start=(k % 4 == 0 and su == 0),
                                       stop=(k % 4 == 3 and su == 1), skip_group_check=True)
                mm.then_inc(S("pv_done"), 1)

            def turn_out(j, m, there):
                upto(pe, "outT_ready", j, G, m + 1)
                upto(pe, "v_ready", j, G * U, U * (m + 2 if there(4 * m + 4) else m + 1))
                for u in range(U):
                    mm = pe.matmul(ps[:, 7, u * C:(u + 1) * C], outT[:, u * P:(u + 1) * P], con("fold"),
                                   start=True, stop=True)
                mm.then_inc(S("out_turned"), 1)

            def newton_a():
                pe.matmul(ps[0:C, 6, 0:C], nsAT[:], nsX[:, 1, :], start=True,
                          stop=True).then_inc(S("ns_ax"), 1)

            def newton_b():
                pe.matmul(ps[0:C, 6, 2 * C:3 * C], nsX[:, 0, :], nsY[:], start=True, stop=True)
                pe.matmul(ps[0:C, 6, C:2 * C], nsY[:], nsX[:, 0, :], start=True,
                          stop=True).then_inc(S("ns_xy"), 1)

            def step(j, k, there):
                in_loop = not isinstance(j, int)
                if there(k + 1):
                    scores(j, 2 * k + 2)
                if in_loop:
                    upto(pe, "nsx_ready", j, PAIRS, k)
                if there(k + 2):
                    keys(j, k + 2)
                if in_loop:
                    newton_a()
                if there(k):
                    turn(j, 2 * k)
                if there(k + 1):
                    scores(j, 2 * k + 3)
                if k % 4 == 3 and there(k + 1):
                    value(j, (k + 1) // 4, 0)
                if k % 4 == 0 and there(k):
                    value(j, k // 4, 1)
                if k % 4 == 1 and there(k - 2):
                    turn_out(j, k // 4 - 1, there)
                if in_loop:
                    upto(pe, "nsy_ready", j, PAIRS, k - 1)
                if there(k):
                    turn(j, 2 * k + 1)
                if in_loop:
                    newton_b()
                if there(k - 1):
                    products(j, k - 1)

            pe.wait_ge(S("fold_split"), 3)
            pe.wait_ge(S("nsx_ready"), 2)
            pe.sem_inc(S("pv_done"), PAIRS)
            pe.sem_inc(S("out_turned"), G)
            attention_steps(pe, step)

        def start_sums(pe):
            for q in range(TILES):
                c, t = q // CT, q % CT
                pe.matmul(ps[C * (c % 2):C * (c % 2) + C, 6 + c // 2, t * P:(t + 1) * P], T[:, q, :], ident,
                          start=(t == 0), stop=False, skip_group_check=True)

        def ffn_pe(pe, which):
            experts, parts, w_out = {2: (EXP2, [wp1], out2), 3: (EXP3, [wp1, wp2], out3)}[which]
            nm = f"f{which}_"
            n = len(parts) + 1
            left = {2: "f2_act", 3: "f3_glu"}[which]

            def hidden(i, k):
                e, c = (k // CHUNKS) % 2, k % CHUNKS
                if c == 0:
                    pe.wait_ge(S(nm + "w_split"), i * (2 * n) + (2 * n + n * (k // CHUNKS + 1)))
                pe.wait_ge(S(left), i * 8 + (8 + k - 1))
                chunk = slice(c * CHUNK, (c + 1) * CHUNK)
                for w, part in enumerate(parts):
                    for s in range(2):
                        mm = pe.matmul(ps[:, 2 * w + c % 2, :], part[:, e, s, :], XS[:, chunk],
                                       start=(s == 0), stop=(s == 1))
                mm.then_inc(S(nm + "h_ready"), 1)

            def spread(i, k):
                e, c = (k // CHUNKS) % 2, k % CHUNKS
                chunk = slice(c * CHUNK, (c + 1) * CHUNK)
                pe.wait_ge(S(nm + "hid_ready"), i * 8 + (8 + k - 1))
                pe.matmul(ps[:, 4 + c % 2, :], pick[:, e, :], gatesT[:, chunk],
                          start=True, stop=True).then_inc(S(nm + "spread"), 1)

            def output(i, k):
                e, c = k // CHUNKS, k % CHUNKS
                if c == 0:
                    pe.wait_ge(S(nm + f"out{e}"), i * 16 + 16)
                pe.wait_ge(S(nm + "hid_ready"), i * 8 + (8 + k + 1))
                half = slice(C * (c % 2), C * (c % 2) + C)
                pe.matmul(ps[half, 6 + c // 2, :], w_out[:, e, 0:C], hid[:, c, :], start=False,
                          stop=False, skip_group_check=True).then_inc(S(nm + "out_chunk"), 1)

            def pair(i, k, there):
                if which == 2 and isinstance(i, int) and k == 0:
                    pe.wait_ge(S("b2_loaded"), 32)
                    for c in range(CHUNKS):
                        pe.matmul(ps[C * (c % 2):C * (c % 2) + C, 6 + c // 2, :], b2two[:],
                                  gatesT[:, c * CHUNK:(c + 1) * CHUNK].bitcast(F32), start=False, stop=False,
                                  skip_group_check=True)
                for function, ahead in ((output, 0), (spread, 2), (hidden, 4)):
                    for kk in (k + ahead, k + ahead + 1):
                        if there(kk):
                            function(i, kk)

            for k in range(2):
                hidden(0, k)
            gates_pe(pe, which - 2, lambda: [hidden(0, k) for k in (2, 3)])
            for k in range(2):
                pe.wait_ge(S("gates_low"), 4 * (which - 2) + k + 3)
                spread(0, k)
            expert_rounds(pe, experts, pair)

        def l3_pe(pe):
            pe.wait_ge(S("qkvw_ready"), 6)
            for q in range(TILES):
                if q % CT == 0:
                    pe.wait_ge(S("ln_low"), 8 + q // CT + 1)
                for part in range(2):
                    mm = pe.matmul(ps[:, projection_bank(q), (q % 2) * 192:(q % 2 + 1) * 192], XS[:, q * P:(q + 1) * P],
                                   qkvw[:, part, :], start=(part == 0), stop=(part == 1))
                if q % 2 == 1:
                    mm.then_inc(S("qkv_ready"), 1)
            pass
            pe.wait_ge(S("v3_ready"), 8)
            for u in range(U):
                mm = pe.matmul(ps[:, 3, :], con("inblock")[:, u * P:(u + 1) * P],
                               V3[:].rearrange("p (j u g) c -> p j u (g c)", j=J, u=U)[:, :, u, :],
                               start=(u == 0), stop=(u == 1))
            mm.then_inc(S("vsum_ready"), 1)
            for p in range(2):
                pe.matmul(ps[:, 6 + p, :], con("lower"), V3[:, 8 * p:8 * p + 8, :].rearrange("p t c -> p (t c)"),
                          start=True, stop=True).then_inc(S("prefix_ready"), 1)
            pe.wait_ge(S("rotated"), 4)
            pe.wait_ge(S("basis_ready"), 2)
            for j in range(J):
                for g in range(G):
                    b = 2 * j + g
                    for u in range(U):
                        t = 4 * j + 2 * u + g
                        for h in range(2):
                            mm = pe.matmul(ps[h * C:(h + 1) * C, 0, b * NB:(b + 1) * NB],
                                           R[:, t, h].rearrange("p a c -> p (a c)"), basis2[:, t, h],
                                           start=(u == 0), stop=(u == 1))
            mm.then_inc(S("qk8_ready"), 1)
            pe.wait_ge(S("qk8_evac"), 2)
            for b in range(B):
                mm = pe.matmul(ps[0:NB, 1, b * NB:(b + 1) * NB], q8[:, b, :], k8[:, b, :],
                               start=True, stop=True)
            mm.then_inc(S("F8_ready"), 1)
            pe.wait_ge(S("F8_evac"), 1)
            for u in range(U):
                mm = pe.matmul(ps[:, 2, u * 64:(u + 1) * 64], con("expand")[0:NB, u * P:(u + 1) * P],
                               F8[:], start=True, stop=True)
            mm.then_inc(S("far_ready"), 1)
            pass
            pe.wait_ge(S("p8_ready"), 1)
            pe.transpose(ps[:, 4, 0:P], p8[:].rearrange("p u b n -> p (u b n)"), ident).then_inc(S("p8T_ready"), 1)
            pe.wait_ge(S("p8T_evac"), 1)
            pe.wait_ge(S("vsum_evac"), 1)
            for u in range(U):
                h = slice(C * u, C * u + C)
                mm = pe.matmul(ps[:, u, :], p8T[h, :], vsum[h].rearrange("p b c -> p (b c)"), start=True, stop=True)
            mm.then_inc(S("yfar_ready"), 1)
            pass

        @block.tensor
        def _(pe):
            pe.wait_ge(S("l0_loaded"), 32)
            pe.sem_inc(S("f2_spread"), 8)
            pe.sem_inc(S("f3_spread"), 8)
            for w in range(2):
                for p in range(2):
                    pe.matmul(ps[:, 2 * w + p, :], w0[:, w * P:(w + 1) * P], x0[:, p * 512:(p + 1) * 512],
                              start=True, stop=True).then_inc(S("l0_projected"), 1)
            pe.wait_ge(S("phi_ready"), 2)
            for j in range(J):
                pe.wait_ge(S("theta_ready"), j // 2 + 1)
                for u in range(U):
                    at = (j % 2) * N + u * P
                    mm = pe.matmul(ps[:, 5 + j // 2, at:at + P], theta[:, j * N + u * P:j * N + (u + 1) * P],
                                   phi[:, j].rearrange("p g m -> p (g m)"), start=True, stop=True)
                if j % 2 == 1:
                    mm.then_inc(S("f_ready"), 1)
            pe.wait_ge(S("pg_ready"), 1)
            pe.wait_ge(S("ww_loaded"), 16)
            for j in range(J):
                mm = pe.matmul(ps[:, 4, j * P:(j + 1) * P], pg[:, j].rearrange("p d m -> p (d m)"), wwT[:],
                               start=True, stop=True)
            mm.then_inc(S("gw_done"), 1)
            pe.wait_ge(S("attn_loaded"), 64)
            for h in range(HEADS):
                mm = pe.matmul(ps[:, 7, h * C:(h + 1) * C], wkT[:, h, :], wqT[:, h, :],
                               start=True, stop=True)
            mm.then_inc(S("folded"), 1)
            pe.wait_ge(S("consts_loaded"), 16)
            for p in range(2):
                pe.wait_ge(S("f_prob_ready"), p + 1)
                for t in range(CT):
                    q = 8 * p + 2 * t
                    mm = pe.transpose(ps[:, p, t * P:(t + 1) * P],
                                      f_prob[:, q:q + 2, :].rearrange("p g m -> p (g m)"), ident)
                mm.then_inc(S("f_transposed"), 1)
            pe.wait_ge(S("gw_evac"), 2)
            for j in range(J):
                if j % 2 == 0:
                    pe.wait_ge(S(("probT_act", "probT_vec")[j // 2]), 1)
                mm = pe.matmul(ps[:, 4 + j // 2, (j % 2) * N:(j % 2 + 1) * N], gw[:, j].rearrange("p g c -> p (g c)"),
                               probT[:, j * N:(j + 1) * N], start=True, stop=True)
                if j % 2 == 1:
                    mm.then_inc(S("wy_ready"), 1)
            pe.wait_ge(S("bn_mean_half"), 1)
            pe.matmul(ps[:, 6, 0:1], con("halfavg"), col[:, 0:1], start=True,
                      stop=True).then_inc(S("bn_mu_done"), 1)
            pe.wait_ge(S("bn_var_half"), 1)
            pe.matmul(ps[:, 6, 1:2], con("halfavg"), col[:, 4:5], start=True,
                      stop=True).then_inc(S("bn_var_done"), 1)
            for h in range(HEADS):
                mm = pe.matmul(ps[:, 3, h * C:(h + 1) * C], wvT[:, h, :], wu[:, h, :],
                               start=True, stop=True)
            mm.then_inc(S("folded"), 1)
            pe.wait_ge(S("wsign_ready"), 4)
            for p in range(2):
                pe.wait_ge(S("sgn_ready"), p + 1)
                for k in range(9):
                    mm = pe.matmul(ps[:, p, :], w3s[:, k, :],
                                   sgn[:, 2 * p:2 * p + 2, k // 3:k // 3 + IMG, k % 3:k % 3 + IMG],
                                   start=(k == 0), stop=(k == 8))
                mm.then_inc(S("conv3_ready"), 1)
            pe.wait_ge(S("fold_split"), 3)
            for p in range(2):
                pe.wait_ge(S("sgn2_ready"), p + 1)
                pe.matmul(ps[:, 2 + p, :], w1s[:], sgn2[:, p * 512:(p + 1) * 512], start=True,
                          stop=True).then_inc(S("conv1_ready"), 1)
            pe.wait_ge(S("l3_loaded"), 48)
            pe.matmul(ps[:, 7, 0:C], wv3[:], wo3T[:], start=True, stop=True).then_inc(S("vo_done"), 1)
            pe.wait_ge(S("ones_ready"), 1)
            pe.wait_ge(S("ns_sq_ready"), 1)
            pe.matmul(ps[0:C, 7, C:C + 1], ones64[:], nsc[:, 0:1], start=True,
                      stop=True).then_inc(S("ns_norm_done"), 1)
            for p in range(2):
                pe.wait_ge(S("x2_ready"), p + 1)
                for t in range(4 * p, 4 * p + 4):
                    mm = pe.transpose(ps[:, 4 + p, (t % 4) * P:(t % 4 + 1) * P],
                                      x2[:, t * P:(t + 1) * P], ident)
                mm.then_inc(S("x2_transposed"), 1)
            ln_pe(pe, 0)
            attention_pe(pe)
            pe.wait_ge(S("nsx_ready"), NEWTON + 2)
            pe.matmul(ps[:, 6, 0:C], eyedup[:], nsX[:, 0, :], start=True, stop=True).then_inc(S("pinv_done"), 1)
            pe.wait_ge(S("stream_added"), G + G * J)
            pe.wait_ge(S("qkvw_ready"), 6)
            start_sums(pe)
            ln_pe(pe, 1)
            gate_pe(pe, 0)
            ffn_pe(pe, 2)
            for b, done in enumerate(("f2_sum_act", "f2_sum_vec")):
                pe.wait_ge(S(done), 1)
                for t in range(CT):
                    mm = pe.transpose(ps[:, b, t * P:(t + 1) * P], sums[:, b, t * P:(t + 1) * P], ident)
                mm.then_inc(S("f2_turned"), 1)
            keep_clock(pe, 3, 20)
            ln_pe(pe, 2)
            l3_pe(pe)
            pe.wait_ge(S("haar_added"), U)
            start_sums(pe)
            ln_pe(pe, 3)
            gate_pe(pe, 1)
            ffn_pe(pe, 3)

        def l3_vector(dve, step, tt, ts, stt):
            def cosines(half):
                tt(by_round(m_a, half), queries_keys(0, half), rotary("cos"), ALU.mult)
                step(tt(by_round(m_d, half), queries_keys(1, half), rotary("cos"), ALU.mult))

            def norms(half):
                dve.wait_ge(S("squared"), 4 * half + 4)
                dve.tensor_reduce(n2[:, 0, TILES * half:TILES * (half + 1)],
                                  squares[:, :, 8 * half:8 * half + 8].rearrange("p a t h c -> p (t h) a c"), AX.XY,
                                  ALU.add).then_inc(S("n2_ready"), 1)

            for q in range(0, TILES, 2):
                dve.wait_ge(S("squared"), q // 2 + 1)
                z = ps[:, projection_bank(q), 0:384].rearrange("p (g c) -> p g c", g=2)
                dve.tensor_copy(V3[:, q:q + 2, :], z[:, :, P:192]).then_inc(S("v3_ready"), 1)
                if q == 8:
                    cosines(0)
                if q == 10:
                    norms(0)
            cosines(1)

            def rotate(half):
                q = slice(8 * half, 8 * half + 8)
                for a, (one, other, op) in enumerate(((m_a, m_b, ALU.subtract), (m_c, m_d, ALU.add))):
                    dve.wait_ge(S("rope_pool"), 2 * half + a + 1)
                    tt(R[:, q, :, a, :].rearrange("p t h c -> p (t h) c"),
                       one[:, half * 512:(half + 1) * 512].rearrange("p (r c) -> p r c", c=C // 2),
                       other[:, half * 512:(half + 1) * 512].rearrange("p (r c) -> p r c", c=C // 2),
                       op).then_inc(S("rotated"), 1)
            norms(1)
            rotate(0)
            rotate(1)
            dve.wait_ge(S("norm_ready"), 1)
            step(ts(n2[:, 2, :], n2[:, 1, :], EPS_L2, None, ALU.add))
            step(dve.reciprocal(n2[:, 0, :], n2[:, 2, :]))
            inv = n2[:, 0, :].rearrange("p (j u g h) -> p j u (g h)", j=J, u=U, g=G)
            for u in range(U):
                dst = basis2[:].rearrange("p (j u g) h n -> p j u (g h) n", j=J, u=U)[:, :, u]
                tt(dst, con("basis")[:, u * NB:(u + 1) * NB].unsqueeze(1).unsqueeze(1).broadcast_to([P, J, 2 * G, NB]),
                   inv[:, :, u].unsqueeze(3).broadcast_to([P, J, 2 * G, NB]), ALU.mult).then_inc(S("basis_ready"), 1)
            dve.wait_ge(S("vsum_ready"), 1)
            tt(vsum[:], ps[:, 3, :].rearrange("p (b c) -> p b c", c=C),
               con("sameb").unsqueeze(2).broadcast_to([P, B, C]), ALU.mult).then_inc(S("vsum_evac"), 1)
            dve.wait_ge(S("rotated"), 4)
            step(tt(m_a[:].rearrange("p (t c) -> p t c", c=C), R[:, :, 0].rearrange("p t a c -> p t (a c)"),
                    R[:, :, 1].rearrange("p t a c -> p t (a c)"), ALU.mult))
            of_head = n2[:, 0, :].rearrange("p (t h) -> p t h", h=2)
            tt(dcol[:, 1, :], of_head[:, :, 0], of_head[:, :, 1], ALU.mult)
            step(dve.tensor_reduce(dcol[:, 0, :], m_a[:].rearrange("p (t c) -> p t c", c=C), AX.X, ALU.add))
            step(tt(dcol[:, 0, :], dcol[:, 0, :], dcol[:, 1, :], ALU.mult))

            def table(name):
                return con(name).rearrange("p (u n) -> p u n", u=U).unsqueeze(2).broadcast_to([P, U, B, 9])
            def of_u(a, u):
                return a.rearrange("p (j u g) -> p j u g", j=J, u=U)[:, :, u, :]
            for u in range(U):
                step(ts(a9[:, u, :, NB].rearrange("p (j g) -> p j g", g=G), of_u(dcol[:, 0, :], u),
                        con("scale")[:, u:u + 1], None, ALU.mult))
            dve.wait_ge(S("far_ready"), 1)
            for u in range(U):
                step(ts(a9[:, u, :, 0:NB], ps[:, 2, u * 64:(u + 1) * 64].rearrange("p (b n) -> p b n", n=NB),
                        con("scale")[:, u:u + 1], None, ALU.mult))

            def over(c):
                return c.unsqueeze(3).broadcast_to([P, U, B, 9])
            step(tt(t9[:], a9[:], table("share"), ALU.mult))
            step(dve.tensor_reduce(s9[:, 1], t9[:], AX.X, ALU.add))
            step(tt(z9[:], a9[:], over(s9[:, 1]), ALU.subtract))
            step(tt(t9[:], z9[:], z9[:], ALU.mult))
            step(tt(t9[:], t9[:], table("share"), ALU.mult))
            step(dve.tensor_reduce(s9[:, 0], t9[:], AX.X, ALU.add))
            ts(s9[:, 2], s9[:, 0], EPS_VAR, None, ALU.max).then_inc(S("a_var_ready"), 1)
            dve.wait_ge(S("a_std_ready"), 1)
            step(dve.reciprocal(s9[:, 4], s9[:, 3]))
            step(tt(z9[:], z9[:], over(s9[:, 4]), ALU.mult))
            step(tt(z9[:], z9[:], table("mask"), ALU.add))
            step(dve.tensor_reduce(s9[:, 5], z9[:], AX.X, ALU.max))
            tt(z9[:], z9[:], over(s9[:, 5]), ALU.subtract).then_inc(S("z_ready"), 1)
            dve.wait_ge(S("e9_ready"), 1)
            step(tt(t9[:], e9[:], table("count"), ALU.mult))
            step(dve.tensor_reduce(s9[:, 6], t9[:], AX.X, ALU.add))
            step(dve.reciprocal(s9[:, 7], s9[:, 6]))
            step(tt(e9[:], e9[:], over(s9[:, 7]), ALU.mult))

            def blocks(name):
                return con(name).rearrange("p (u n) -> p u n", u=U).unsqueeze(2).broadcast_to([P, U, B, NB])
            tt(p8[:], e9[:, :, :, 0:NB], blocks("below"), ALU.mult).then_inc(S("p8_ready"), 1)
            for u in range(U):
                ins = dve.tensor_copy(of_u(pdia[:], u), e9[:, u, :, NB].rearrange("p (j g) -> p j g", g=G))
                step(ins)
            dve.nop().then_inc(S("pdia_ready"), 1)
            step(tt(t9[:, :, :, 0:NB], e9[:, :, :, 0:NB], blocks("own"), ALU.mult))
            for u in range(U):
                step(dve.tensor_reduce(of_u(pown[:], u), t9[:, u, :, 0:NB].rearrange("p (j g) n -> p j g n", g=G),
                                       AX.X, ALU.add))
            dve.wait_ge(S("prefix_ready"), 2)
            t = T[:].rearrange("p t c -> p (t c)")
            ma = m_a[:].rearrange("p (t c) -> p t c", c=C)
            step(tt(ma, ps[:, 6:8, :].rearrange("p a (t c) -> p (a t) c", c=C),
                    pown[:].unsqueeze(2).broadcast_to([P, TILES, C]), ALU.mult))
            step(tt(t, t, m_a[:], ALU.add))
            dve.wait_ge(S("diag_done"), 1)
            step(tt(t, t, m_d[:], ALU.add))
            dve.wait_ge(S("yfar_ready"), 1)
            tu = T[:].rearrange("p (j u g) c -> p j u g c", j=J, u=U)
            for u in range(U):
                tt(tu[:, :, u], tu[:, :, u], ps[:, u, :].rearrange("p (j g c) -> p j g c", j=J, g=G),
                   ALU.add).then_inc(S("haar_added"), 1)
            dve.wait_ge(S("haar_added"), U)

        @block.vector
        def _(dve):
            step = step_of(dve, "dve_step")
            tt, ts, stt = dve.tensor_tensor, dve.tensor_scalar, dve.scalar_tensor_tensor

            def wide(c, n=C, t=TILES):
                return c.unsqueeze(2).broadcast_to([P, t, n])

            for name in ("f2_hid_ready", "f3_glu", "f3_hid_ready"):
                dve.sem_inc(S(name), 8)

            for p in range(2):
                dve.wait_ge(S("l0_projected"), p + 1)
                ins = dve.tensor_reduce(pooled[:, 2 * p:2 * p + 2, :].rearrange("p b n -> p (b n)")
                                        .rearrange("p (r w) -> p r w", w=IMG // 2),
                                        ps[:, p, :].rearrange("p (r a w b) -> p r w a b", a=2, b=2, w=IMG // 2),
                                        AX.XY, ALU.max)
            step(ins)
            dve.wait_ge(S("vec_loaded"), 16)
            dve.wait_ge(S("blocks_zeroed"), 2)
            for g in range(G):
                h = slice(C * g, C * g + IC)
                ts(phi[h, :, g, :], pooled[h], v_("bpg")[h], None, ALU.add).then_inc(S("phi_ready"), 1)
            ts(pg[:], pooled[:].unsqueeze(2).broadcast_to([P, J, 2, POOLED]), v_("bpg"), None,
               ALU.add).then_inc(S("pg_ready"), 1)
            dve.wait_ge(S("l1_loaded"), 64)
            ones = [("w3n", w3n, 9 * C, 20), ("w1n", w1n, C, 21)]
            for _, w, n, c in ones:
                step(dve.tensor_reduce(col[:, c:c + 1], w[:], AX.X, ALU.add, apply_absolute_value=True))
            step(ts(col[:, 22:23], col[:, 20:21], 1.0 / (9 * C), None, ALU.mult))
            step(ts(col[:, 23:24], col[:, 21:22], 1.0 / C, None, ALU.mult))
            step(ts(col[:, 9:10], v_("v1"), EPS_BN, None, ALU.add))
            step(ts(col[:, 10:11], v_("v2"), EPS_BN, None, ALU.add))
            dve.wait_ge(S("ns_loaded"), 32)
            step(dve.tensor_tensor_reduce(nsY[:], nsA[:], nsA[:], 1.0, 0.0, ALU.mult, ALU.add, nsc[:, 0:1]))
            dve.nop().then_inc(S("ns_sq_ready"), 1)
            f = ps[:, 5:7, :].rearrange("p a (t c) -> p (a t) c", c=POOLED)
            halves = [slice(8 * half, 8 * half + 8) for half in range(2)]
            for half, q in enumerate(halves):
                dve.wait_ge(S("f_ready"), half + 1)
                ins = dve.tensor_reduce(f_col[:, 0, q], f[:, q], AX.X, ALU.max)
            step(ins)
            for q in halves:
                tt(f_sub[:, q], f[:, q], wide(f_col[:, 0, q], t=8), ALU.subtract).then_inc(S("f_shifted"), 1)
            dve.wait_ge(S("gw_done"), 1)
            for g in range(G):
                h = slice(C * g, C * g + C)
                dve.tensor_copy(gw[h, :, g, :], ps[h, 4, :].rearrange("p (j g c) -> p j g c", g=G, c=C)[:, :, g, :]
                                ).then_inc(S("gw_evac"), 1)
            for half, q in enumerate(halves):
                dve.wait_ge(S("f_exp_ready"), half + 1)
                ins = dve.tensor_reduce(f_col[:, 1, q], f_exp[:, q], AX.X, ALU.add)
            step(ins)
            step(dve.reciprocal(f_col[:, 2, :], f_col[:, 1, :]))
            for q in halves:
                tt(f_prob[:, q], f_exp[:, q], wide(f_col[:, 2, q], t=8), ALU.mult).then_inc(S("f_prob_ready"), 1)
            dve.wait_ge(S("f_transposed"), 2)
            dve.tensor_copy(probT[:, 512:1024], ps[:, 1, :]).then_inc(S("probT_vec"), 1)
            dve.wait_ge(S("fold_high"), 2)
            for d in range(2):
                stt(AL[:, :, d, :], ps[:, 7, :].rearrange("p (h c) -> p h c", c=C), 1.0 / math.sqrt(C),
                    AH[:, :, d, :].bitcast(F32), ALU.mult, ALU.subtract).then_inc(S("fold_split"), 1)
            dve.wait_ge(S("wy_evac"), 2)
            for p in range(2):
                step(dve.bn_stats(bn6[:, p, :], wy[:, p * 512:(p + 1) * 512]))
            dve.bn_aggr(col[:, 0:2], bn6[:].rearrange("p a s -> p (a s)")).then_inc(S("bn_mean_half"), 1)
            dve.wait_ge(S("bn_mean_half"), 1)
            dve.wait_ge(S("bn_mu_done"), 1)
            step(dve.tensor_copy(col[:, 2:3], ps[:, 6, 0:1]))
            step(tt(col[:, 3:4], col[:, 0:1], col[:, 2:3], ALU.subtract))
            stt(col[:, 4:5], col[:, 3:4], col[:, 3:4], col[:, 1:2], ALU.mult, ALU.add).then_inc(S("bn_var_half"), 1)
            dve.wait_ge(S("bn_var_done"), 1)
            ts(col[:, 8:9], ps[:, 6, 1:2], EPS_BN, None, ALU.add).then_inc(S("bn_var_ready"), 1)
            dve.wait_ge(S("bn_std_ready"), 1)
            step(dve.reciprocal(col[:, 24:27], col[:, 11:14]))
            step(tt(col[:, 28:29], col[:, 24:25], v_("gamma"), ALU.mult))
            step(tt(col[:, 30:31], col[:, 28:29], col[:, 2:3], ALU.mult))
            step(tt(col[:, 29:30], v_("beta"), col[:, 30:31], ALU.subtract))
            dve.wait_ge(S("l0_loaded"), 32)
            for p in range(2):
                s = slice(p * 512, (p + 1) * 512)
                step(ts(va[:, s], wy[:, s], col[:, 28:29], col[:, 29:30], ALU.mult, ALU.add))
                tt(x1[:, s], va[:, s], x0[:, s], ALU.add).then_inc(S("x1_ready"), 1)
            for k, (g_, be, m_, b_) in enumerate((("g1", "be1", "m1", "b12"), ("g2", "be2", "m2", "b22"))):
                inv = col[:, 32 + k:33 + k]
                step(tt(inv, v_(g_), col[:, 25 + k:26 + k], ALU.mult))
                step(tt(col[:, 34 + k:35 + k], inv, col[:, 22 + k:23 + k], ALU.mult))
                step(tt(col[:, 38:39], inv, v_(m_), ALU.mult))
                step(tt(col[:, 39:40], v_(be), col[:, 38:39], ALU.subtract))
                step(tt(col[:, 36 + k:37 + k], col[:, 39:40], v_(b_), ALU.add))

            dve.wait_ge(S("fold_high"), 3)
            tt(GL[:], ps[:, 3, :], GH[:].bitcast(F32), ALU.subtract).then_inc(S("fold_split"), 1)

            def half_of(a, p):
                return a[:, p * 512:(p + 1) * 512]

            def norm_and_prelu(p, bank, ready, k, dst, a, after, done):
                v = half_of(va, p)
                dve.wait_ge(S(ready), p + 1)
                stt(v, ps[:, bank + p, :], col[:, 34 + k:35 + k], v, ALU.mult, ALU.add).then_inc(S("prelu_in"), 1)
                dve.wait_ge(S("prelu_in"), 2 * k + p + 1)
                step(ts(half_of(dst, p), v, 0.0, v_(a), ALU.min, ALU.mult))
                dve.wait_ge(S("positive_ready"), 2 * k + p + 1)
                stt(half_of(dst, p), half_of(dst, p), v_(after), half_of(vb, p), ALU.add,
                    ALU.add).then_inc(S(done), 1)

            for p in range(2):
                ins = ts(half_of(va, p), half_of(x1, p), col[:, 36:37], None, ALU.add)
            step(ins)
            for p in range(2):
                norm_and_prelu(p, 0, "conv3_ready", 0, r1, "a1", "b13", "r1_ready")
            for p in range(2):
                dve.wait_ge(S("r1_shifted"), p + 1)
                norm_and_prelu(p, 2, "conv1_ready", 1, x2, "a2", "b23", "x2_ready")
            dve.wait_ge(S("consts_loaded"), 16)
            for d in range(2):
                ins = dve.tensor_copy(eyedup[:, d * C:(d + 1) * C], ident[0:C, 0:C])
            step(ins)
            dve.wait_ge(S("ns_norm_done"), 1)
            step(dve.reciprocal(nsc[:, 1:2], ps[0:C, 7, C:C + 1]))
            ts(nsX[:, 1, :], nsAT[:], nsc[:, 1:2], None, ALU.mult).then_inc(S("nsx_ready"), 1)
            ts(nsX[:, 0, :], nsA[:], nsc[:, 1:2], None, ALU.mult).then_inc(S("nsx_ready"), 1)

            def query_or_key(part, h):
                return qkvw[:, part, 0:P].rearrange("p (a h c) -> p a h c", a=2, h=2)[:, :, h, :]

            def split_projections():
                dve.wait_ge(S("vo_done"), 1)
                dve.wait_ge(S("l3_loaded"), 48)
                for high, low, raw in ((query_or_key(0, 0), query_or_key(1, 0), wq3[:].rearrange("p (a c) -> p a c", a=2)),
                                       (qkvw[:, 0, P:192], qkvw[:, 1, P:192], ps[:, 7, 0:C])):
                    step(dve.tensor_copy(high, raw))
                    tt(low, raw, high.bitcast(F32), ALU.subtract).then_inc(S("qkvw_ready"), 2)
            split_projections()
            dve.wait_ge(S("x2_transposed"), 2)
            step(dve.tensor_copy(T[:, 8:16, :].rearrange("p t c -> p (t c)"), ps[:, 5, :]))
            dve.wait_ge(S("T_act"), 1)

            def layer_norm(n, after_first=None):
                for q in range(TILES):
                    ins = dve.bn_stats(ln6[:, q, :], T[:, q, :])
                step(ins)
                me, mo = ln6[:, :, 1], ln6[:, :, 4]
                tt(lnc[:, 0, :], me, mo, ALU.add)
                tt(lnc[:, 2, :], ln6[:, :, 2], ln6[:, :, 5], ALU.add)
                step(tt(lnc[:, 1, :], me, mo, ALU.subtract))
                step(tt(lnc[:, 3, :], lnc[:, 1, :], lnc[:, 1, :], ALU.mult))
                ts(lnc[:, 1, :], lnc[:, 0, :], 0.5, None, ALU.mult).then_inc(S("ln_mean"), 1)
                step(stt(lnc[:, 4, :], lnc[:, 3, :], C / 4.0, lnc[:, 2, :], ALU.mult, ALU.add))
                ts(lnc[:, 5, :], lnc[:, 4, :], 1.0 / C, EPS_LN, ALU.mult, ALU.add).then_inc(S("ln_var"), 1)
                step(tt(xn[:, 0:8], T[:, 0:8], wide(lnc[:, 1, 0:8], t=8), ALU.subtract))
                dve.wait_ge(S("ln_std"), n + 1)
                step(dve.reciprocal(lnc[:, 7, :], lnc[:, 6, :]))
                for p in range(4):
                    q = slice(CT * p, CT * p + CT)
                    if p == 2:
                        dve.wait_ge(S("ln_centred"), n + 1)
                    tt(xn[:, q], xn[:, q], wide(lnc[:, 7, q], t=CT), ALU.mult).then_inc(S("ln_normalised"), 1)
                for p in range(4):
                    split_low(dve, XS, p, p, "ln_high", 8 * n, "ln_low")
                    if p == 0 and after_first:
                        after_first()

            def gate(n, before_low=None):
                experts, gb = ((EXP2, gb2), (EXP3, gb3))[n]
                dve.wait_ge(S("gate_loaded"), 64)
                lg, ge, gs = logit[:, :, 0:experts], gexp[:, :, 0:experts], gsel[:, :, 0:experts]
                for half in range(2):
                    dve.wait_ge(S("gate_logits"), 2 * n + half + 1)
                    raw = ps[:, 4 + half, 0:8 * experts].rearrange("p (t e) -> p t e", e=experts)
                    step(tt(lg[:, 8 * half:8 * half + 8, :], raw, gb[:].unsqueeze(1).broadcast_to([P, 8, experts]),
                            ALU.add))
                    for q in range(8 * half, 8 * half + 8):
                        ins = dve.max(top8[:, q, :], lg[:, q, :])
                step(ins)
                step(tt(gs, lg, wide(top8[:, :, 1], experts), ALU.is_ge))
                tt(lg, lg, wide(top8[:, :, 0], experts), ALU.subtract).then_inc(S("gate_shifted"), 1)
                dve.wait_ge(S("gate_exp"), n + 1)
                step(tt(gs, ge, gs, ALU.mult))
                step(dve.tensor_reduce(gcol[:, 0, :], (ge, gs)[n], AX.X, ALU.add))
                step(dve.reciprocal(gcol[:, 1, :], gcol[:, 0, :]))
                dve.wait_ge(S("gates_zeroed"), 1)
                tt(gates[:, :, 0:experts], gs, wide(gcol[:, 1, :], experts),
                   ALU.mult).then_inc(S("gates_ready"), 1)
                if before_low:
                    before_low()
                for p in range(4):
                    split_low(dve, gatesT, 4 + p % 2, p, "gates_high", 8 * n, "gates_low")

            def tokens(j, m):
                upto(dve, "scores_ready", j, 2 * PAIRS, 8 * m - 8)
                dve.wait_ge(S("ln_low"), 1 if isinstance(j, int) else 4)
                src = XS[:].bitcast(F32).rearrange("p (j u g n) -> p j u g n", j=J, u=U, g=G)
                at = j + m // 2
                at = slice(at, at + 1) if isinstance(at, int) else bass.ds(at, 1)
                dve.tensor_copy(xcur[:, m % 2, :].rearrange("p (u n) -> p u n", u=U).unsqueeze(1),
                                src[:, at, :, m % 2, :]).then_inc(S("xcur_ready"), 1)

            layer_norm(0, after_first=lambda: tokens(0, 0))
            def key_low(j, k):
                upto(dve, "kh_ready", j, PAIRS, k + 1)
                tt(KL[:, k % 2].rearrange("p h n -> p (h n)"), ps[:, 0, :],
                   KH[:, k % 2].rearrange("p h n -> p (h n)").bitcast(F32),
                   ALU.subtract).then_inc(S("kl_ready"), 1)

            def maxima(j, n):
                upto(dve, "scores_ready", j, 2 * PAIRS, n + 1)
                upto(dve, "probs_ready", j, 2 * PAIRS, n - 3)
                dve.tensor_reduce(negmax[:, n % 4, :],
                                  ps[:, 1 + n % 2, :].rearrange("p (u n) -> p u n", u=U), AX.X, ALU.max,
                                  negate=True).then_inc(S("max_ready"), 1)

            def scale_eye(j, n):
                upto(dve, "probs_ready", j, 2 * PAIRS, n + 1)
                dve.reciprocal(rowinv[:, n % 4, :], rowsum[:, n % 4, :]).then_inc(S("rowinv_ready"), 1)
                upto(dve, "rowinv_ready", j, 2 * PAIRS, n + 1)
                upto(dve, "p_turned", j, 2 * PAIRS, n - 1)
                tt(scaled_eye[:, n % 2], ident.unsqueeze(1).broadcast_to([P, U, P]),
                   rowinv[:, n % 4, :].unsqueeze(2).broadcast_to([P, U, P]), ALU.mult).then_inc(S("eye_scaled"), 1)

            def add_out(j, m):
                dve.wait_ge(S("t_biased"), 2)
                upto(dve, "out_turned", j, G, G + m + 1)
                at = slice(j, j + 1) if isinstance(j, int) else bass.ds(j, 1)
                t = T[:].rearrange("p (j u g) c -> p j u g c", j=J, u=U)[:, at, :, m % 2, :]
                tt(t, t, ps[:, 7, 0:U * C].rearrange("p (u c) -> p u c", u=U).unsqueeze(1),
                   ALU.add).then_inc(S("stream_added"), 1)

            def newton_factors(j):
                dve.tensor_copy(nscoef[:].rearrange("p s a -> p (s a)").unsqueeze(1),
                                con("newton")[0:C].rearrange("p (j n) -> p j n", j=J - 1)[:, bass.ds(j, 1), :]
                                ).then_inc(S("ns_factors"), 1)
                dve.wait_ge(S("ns_factors"), j + 1)

            def newton_y(j, s):
                ts(nsZ[:], ident[0:C, 0:C], nscoef[:, s, 1:2], None, ALU.mult).then_inc(S("nsz_ready"), 1)
                upto(dve, "nsz_ready", j, PAIRS, s + 1)
                upto(dve, "ns_ax", j, PAIRS, s + 1)
                stt(nsY[:], ps[0:C, 6, 0:C], nscoef[:, s, 0:1], nsZ[:], ALU.mult, ALU.add).then_inc(S("nsy_ready"), 1)

            def newton_x(j, s):
                upto(dve, "ns_xy", j, PAIRS, s + 1)
                dve.tensor_copy(nsX[:].rearrange("p a c -> p (a c)"),
                                ps[0:C, 6, C:3 * C]).then_inc(S("nsx_ready"), 1)

            def attention_step(j, k, there):
                in_loop = not isinstance(j, int)
                if k % 4 == 1 and there(k + 3):
                    tokens(j, (k + 3) // 4)
                if there(k + 1):
                    maxima(j, 2 * k + 2)
                if in_loop:
                    newton_y(j, k - 2)
                if there(k + 2):
                    key_low(j, k + 2)
                if there(k + 1):
                    scale_eye(j, 2 * k + 2)
                    maxima(j, 2 * k + 3)
                if k % 4 == 1 and there(k - 2):
                    add_out(j, k // 4 - 1)
                if in_loop:
                    newton_x(j, k - 2)
                if there(k):
                    transposed_copy(dve, j, 2 * k + 1)
                if there(k + 1):
                    scale_eye(j, 2 * k + 3)

            dve.sem_inc(S("stream_added"), G)
            attention_steps(dve, attention_step, in_loop=newton_factors)
            dve.wait_ge(S("pinv_done"), 1)
            raw = ps[:, 6, 0:C].rearrange("p (a c) -> p a c", a=2)
            step(dve.tensor_copy(query_or_key(0, 1), raw))
            tt(query_or_key(1, 1), raw, query_or_key(0, 1).bitcast(F32), ALU.subtract).then_inc(S("qkvw_ready"), 2)

            dve.wait_ge(S("stream_added"), G + G * J)
            layer_norm(1)
            gate(0)

            def weigh(which, src, i, k):
                nm = f"f{which}_"
                dve.wait_ge(S(nm + "spread"), i * 8 + (8 + k + 1))
                dve.wait_ge(S(nm + "out_chunk"), i * 8 + (8 + k - 3))
                tt(hid[:, k % 4, :], src[:, k % 2, :], ps[:, 4 + k % 2, :],
                   ALU.mult).then_inc(S(nm + "hid_ready"), 1)

            def second(i, k, there):
                for kk in (k, k + 1):
                    dve.wait_ge(S("f2_act"), i * 8 + (8 + kk + 1))
                    weigh(2, act_out, i, kk)

            expert_rounds(dve, EXP2, second)
            dve.wait_ge(S("f2_out_chunk"), 8 + CHUNKS * EXP2)
            dve.tensor_copy(sums[:, 1, :], ps[:, 7, :]).then_inc(S("f2_sum_vec"), 1)
            dve.wait_ge(S("f2_turned"), 2)
            step(dve.tensor_copy(stream_half(1), turned_half(1)))
            dve.wait_ge(S("T_act"), 2)
            layer_norm(2)
            l3_vector(dve, step, tt, ts, stt)
            layer_norm(3)

            def product(i, k):
                dve.wait_ge(S("f3_act"), i * 8 + (k + 1))
                dve.wait_ge(S("f3_hid_ready"), i * 8 + (8 + k - 1))
                tt(glu[:, k % 2, :], ps[:, 2 + k % 2, :], act_out[:, k % 2, :], ALU.mult).then_inc(S("f3_glu"), 1)

            def third(i, k, there):
                for kk in (k, k + 1):
                    dve.wait_ge(S("f3_glu"), i * 8 + (8 + kk + 1))
                    weigh(3, glu, i, kk)
                for kk in (k + 2, k + 3):
                    if there(kk):
                        product(i, kk)

            gate(1, before_low=lambda: [product(0, k) for k in range(2)])
            expert_rounds(dve, EXP3, third)
            dve.wait_ge(S("f3_out_chunk"), 8 + CHUNKS * EXP3)
            dve.tensor_copy(yfin[:, 512:1024], ps[:, 7, :]).then_inc(S("out_ready_vec"), 1)

def kernel(**inputs):
    import concourse.bacc as bacc
    from concourse.bass_utils import run_bass_kernel_spmd

    a = {k: np.asarray(v) for k, v in inputs.items()}

    def twice(m):
        return np.concatenate([m, m], axis=0)

    def rows(v):
        return np.broadcast_to(v[None, :], (P, v.shape[0]))

    vec = {"bw": a["L0_conv_bw"], "gamma": a["L0_conv_gamma"], "beta": a["L0_conv_beta"]}
    vec.update({n: a["L1_conv_" + n] for n in VECS if n not in vec and n not in ("bpg", "bt")})
    nothing = np.zeros(IC, np.float32)
    vec["bpg"] = np.concatenate([a["L0_conv_bp"], a["L0_conv_bg"]])
    vec["bt"] = np.concatenate([a["L0_conv_bt"], nothing])
    cols = [np.concatenate([vec[n], vec[n]]) for n in VECS]

    def blocks(m):
        z = np.zeros_like(m)
        return np.block([[m, z], [z, m]])

    no_weight = np.zeros((C, IC), np.float32)

    def by_head(w, dup):
        t = w.reshape(C, HEADS, C).transpose(2, 1, 0)
        return np.concatenate([t, t], axis=2) if dup else t

    def twice_in(w):
        return np.concatenate([w, w], axis=1)

    def picks(experts):
        e, p = np.arange(experts)[:, None, None], np.arange(P)[None, :, None]
        return (p % C == e).astype(np.float32)

    def expert_rows(*parts):
        w = np.concatenate(parts, axis=2)
        return w.reshape(w.shape[0] * P, -1)

    w3, w1 = a["L1_conv_w3"], a["L1_conv_w1"]
    arrays = {
        "x": a["x"].reshape(G, J, C, N).transpose(0, 2, 1, 3).reshape(P, J * N),
        "w0": np.concatenate([blocks(np.concatenate([a["L0_conv_Wp"].T, a["L0_conv_Wg"].T], axis=1)),
                              blocks(np.concatenate([a["L0_conv_Wt"].T, no_weight], axis=1))], axis=1),
        "wwT": blocks(np.concatenate([no_weight.T, a["L0_conv_Ww"].T], axis=0)),
        "vec": np.stack(cols, axis=1),
        "w3T": twice(w3.transpose(1, 2, 3, 0).reshape(C, 9, C)),
        "w1T": twice(w1[:, :, 0, 0].T),
        "w3n": twice(w3.reshape(C, C * 9)),
        "w1n": twice(w1.reshape(C, C)),
        "wqT": by_head(a["L2_attn_Wq"], False),
        "wkT": by_head(a["L2_attn_Wk"], True),
        "wvT": by_head(a["L2_attn_Wv"], True),
        "wu": a["L2_attn_Wu"].reshape(HEADS, C, C).transpose(1, 0, 2),
        "bu": rows(a["L2_attn_bu"]),
        "q3": twice(a["L3_attn_W_Q"]),
        "q3T": a["L3_attn_W_Q"].T,
        "wv3": np.concatenate([a["L3_attn_W_V"]] * 2, axis=1),
        "wo3T": a["L3_attn_W_O"].T,
        "gw2": twice(a["L2_ffn_gate_w"]),
        "gb2": rows(a["L2_ffn_gate_b"]),
        "gw3": twice(a["L3_ffn_gate_w"]),
        "gb3": rows(a["L3_ffn_gate_b"]),
        "f2_in": expert_rows(twice_in(a["L2_ffn_W1"]), picks(EXP2)),
        "f2_out": expert_rows(a["L2_ffn_W2"], a["L2_ffn_b1"][:, :, None]),
        "b2": a["L2_ffn_b2"],
        "f3_in": expert_rows(twice_in(a["L3_ffn_w1"]), twice_in(a["L3_ffn_w2"]), picks(EXP3)),
        "f3_out": expert_rows(a["L3_ffn_w3"]),
        "consts": constants(),
    }
    arrays = {k: np.ascontiguousarray(v) for k, v in arrays.items()}
    nc = bacc.Bacc("TRN2", target_bir_lowering=False, num_devices=1)
    io = {k: nc.dram_tensor(f"in_{k}", v.shape, mybir.dt.from_np(v.dtype), kind="ExternalInput").ap()
          for k, v in arrays.items()}
    out = nc.dram_tensor("out_y", (P, J * N), F32, kind="ExternalOutput").ap()
    hybrid_kernel(nc, io, out)
    r = run_bass_kernel_spmd(nc, [{f"in_{k}": v for k, v in arrays.items()}], core_ids=[0])
    y = r.results[0]["out_y"]
    y = y.reshape(2, C, J // 2, U, G, P).transpose(4, 2, 0, 1, 3, 5)
    return y.reshape(B, C, IMG, IMG)
```
